# Optimizing a Trainium2 kernel written in Bass

```python
import numpy as np
import jax
import jax.numpy as jnp

def _softmax(x, axis=-1):
    return jax.nn.softmax(x, axis=axis)

def _gelu(x):
    return jax.nn.gelu(x, approximate=True)

def _silu(x):
    return jax.nn.silu(x)

def _sigmoid(x):
    return jax.nn.sigmoid(x)

def _layernorm(x, axis=-1, eps=1e-05):
    m = jnp.mean(x, axis=axis, keepdims=True)
    v = jnp.var(x, axis=axis, keepdims=True)
    return (x - m) / jnp.sqrt(v + eps)

def _scatter_add(tgt, idx, src, axis=0):
    return tgt.at[idx].add(src)

def _segment_sum(src, seg, n):
    return jax.ops.segment_sum(src, seg, n)
kernel_name = 'mk_seq_postln_d1_jaxref_r4_67778f'

def setup_inputs(seed: int=0):
    np.random.seed(seed)
    _w = jnp.asarray

    def _L0_attn_setup():
        import math
        import jax, jax.numpy as jnp
        import numpy as np
        B, T, D, H = (4, 512, 256, 16)
        HD = D // H

        def apply_rope(x, base=10000.0):
            _, t, _, dh = x.shape
            half = dh // 2
            inv_freq = 1.0 / base ** (jnp.arange(half, dtype=jnp.float32) / float(half))
            pos = jnp.arange(t, dtype=jnp.float32)
            angles = pos[:, None] * inv_freq[None, :]
            sin = jnp.sin(angles)[None, :, None, :]
            cos = jnp.cos(angles)[None, :, None, :]
            x1 = x[..., :half]
            x2 = x[..., half:2 * half]
            rot1 = x1 * cos - x2 * sin
            rot2 = x1 * sin + x2 * cos
            return jnp.concatenate([rot1, rot2, x[..., 2 * half:]], axis=-1)
        key = jax.random.key(seed)
        k1, k2, k3 = jax.random.split(key, 3)
        x = jax.random.normal(k1, (B, T, D), dtype=jnp.float32)
        Wqkv = jax.random.normal(k2, (D, 3 * D), dtype=jnp.float32) / math.sqrt(D)
        Wo = jax.random.normal(k3, (D, D), dtype=jnp.float32) / math.sqrt(D)
        bo = jnp.zeros((D,), dtype=jnp.float32)
        return {'x': x, 'Wqkv': Wqkv, 'Wo': Wo, 'bo': bo}
    _L0_attn_in = _L0_attn_setup()

    def _L0_ffn_setup():
        import jax, jax.numpy as jnp
        import numpy as np
        B, N, D, H, E = (4, 256, 256, 16, 8)
        DK = D // H
        HID = 4 * D
        EPS = 1e-05

        def _layernorm(x, w, b):
            m = jnp.mean(x, axis=-1, keepdims=True)
            v = jnp.mean(jnp.square(x - m), axis=-1, keepdims=True)
            return (x - m) * jax.lax.rsqrt(v + EPS) * w + b

        def _msa(x, w_qkv, w_proj):
            b, n, d = x.shape
            qkv = (x @ w_qkv).reshape(b, n, 3, H, DK)
            q = qkv[:, :, 0].transpose(0, 2, 1, 3)
            k = qkv[:, :, 1].transpose(0, 2, 1, 3)
            v = qkv[:, :, 2].transpose(0, 2, 1, 3)
            attn = jnp.einsum('bhnd,bhmd->bhnm', q, k) * (1.0 / np.sqrt(DK))
            attn = jax.nn.softmax(attn, axis=-1)
            y = jnp.einsum('bhnm,bhmd->bhnd', attn, v)
            y = y.transpose(0, 2, 1, 3).reshape(b, n, d)
            return y @ w_proj

        def _moe_mlp(x, gate_w, gate_b, w1, w2):
            b, n, d = x.shape
            xf = x.reshape(b * n, d)
            logits = xf @ gate_w + gate_b
            one_hot = jax.nn.one_hot(jnp.argmax(logits, axis=-1), E, dtype=xf.dtype)
            h = jax.nn.gelu(jnp.einsum('td,edh->teh', xf, w1), approximate=True)
            y = jnp.einsum('teh,ehd->ted', h, w2)
            out = jnp.einsum('te,ted->td', one_hot, y)
            return out.reshape(b, n, d)
        key = jax.random.key(seed)
        ks = jax.random.split(key, 8)
        s = 0.02
        return {'x': jax.random.normal(ks[0], (B, N, D), jnp.float32), 'ln1_w': jnp.ones((D,), jnp.float32), 'ln1_b': jnp.zeros((D,), jnp.float32), 'w_qkv': jax.random.normal(ks[1], (D, 3 * D), jnp.float32) * s, 'w_proj': jax.random.normal(ks[2], (D, D), jnp.float32) * s, 'ln2_w': jnp.ones((D,), jnp.float32), 'ln2_b': jnp.zeros((D,), jnp.float32), 'gate_w': jax.random.normal(ks[3], (D, E), jnp.float32) * s, 'gate_b': jnp.zeros((E,), jnp.float32), 'w1': jax.random.normal(ks[4], (E, D, HID), jnp.float32) * s, 'w2': jax.random.normal(ks[5], (E, HID, D), jnp.float32) * s}
    _L0_ffn_in = _L0_ffn_setup()
    _d = {'L0_attn_x': _L0_attn_in['x'], 'L0_attn_Wqkv': _L0_attn_in['Wqkv'], 'L0_attn_Wo': _L0_attn_in['Wo'], 'L0_attn_bo': _L0_attn_in['bo'], 'L0_ffn_ln1_w': _L0_ffn_in['ln1_w'], 'L0_ffn_ln1_b': _L0_ffn_in['ln1_b'], 'L0_ffn_w_qkv': _L0_ffn_in['w_qkv'], 'L0_ffn_w_proj': _L0_ffn_in['w_proj'], 'L0_ffn_ln2_w': _L0_ffn_in['ln2_w'], 'L0_ffn_ln2_b': _L0_ffn_in['ln2_b'], 'L0_ffn_gate_w': _L0_ffn_in['gate_w'], 'L0_ffn_gate_b': _L0_ffn_in['gate_b'], 'L0_ffn_w1': _L0_ffn_in['w1'], 'L0_ffn_w2': _L0_ffn_in['w2']}
    _x0 = _d['L0_attn_x']
    _d['L0_attn_x'] = jax.random.normal(jax.random.fold_in(jax.random.key(seed), 1), (8, 512, 256), dtype=_x0.dtype)
    del _x0
    return _d

def reference(L0_attn_x, L0_attn_Wqkv, L0_attn_Wo, L0_attn_bo, L0_ffn_ln1_w, L0_ffn_ln1_b, L0_ffn_w_qkv, L0_ffn_w_proj, L0_ffn_ln2_w, L0_ffn_ln2_b, L0_ffn_gate_w, L0_ffn_gate_b, L0_ffn_w1, L0_ffn_w2):

    def _L0_attn_ref(x, Wqkv, Wo, bo):
        import math
        import jax, jax.numpy as jnp
        import numpy as np
        B, T, D, H = (4, 512, 256, 16)
        HD = D // H

        def apply_rope(x, base=10000.0):
            _, t, _, dh = x.shape
            half = dh // 2
            inv_freq = 1.0 / base ** (jnp.arange(half, dtype=jnp.float32) / float(half))
            pos = jnp.arange(t, dtype=jnp.float32)
            angles = pos[:, None] * inv_freq[None, :]
            sin = jnp.sin(angles)[None, :, None, :]
            cos = jnp.cos(angles)[None, :, None, :]
            x1 = x[..., :half]
            x2 = x[..., half:2 * half]
            rot1 = x1 * cos - x2 * sin
            rot2 = x1 * sin + x2 * cos
            return jnp.concatenate([rot1, rot2, x[..., 2 * half:]], axis=-1)
        b, t, d = x.shape
        qkv = x @ Wqkv
        q, k, v = jnp.split(qkv, 3, axis=-1)
        q = q.reshape(b, t, H, HD)
        k = k.reshape(b, t, H, HD)
        v = v.reshape(b, t, H, HD)
        q = apply_rope(q)
        k = apply_rope(k)
        q = q / jnp.sqrt(jnp.sum(q * q, axis=-1, keepdims=True) + 1e-06)
        k = k / jnp.sqrt(jnp.sum(k * k, axis=-1, keepdims=True) + 1e-06)
        attn = jnp.einsum('bthd,bshd->bhts', q, k) / math.sqrt(HD)
        attn = jax.nn.softmax(attn, axis=-1)
        out = jnp.einsum('bhts,bshd->bthd', attn, v).reshape(b, t, d)
        return out @ Wo + bo

    def _L0_ffn_ref(x, ln1_w, ln1_b, w_qkv, w_proj, ln2_w, ln2_b, gate_w, gate_b, w1, w2):
        import jax, jax.numpy as jnp
        import numpy as np
        B, N, D, H, E = (4, 256, 256, 16, 8)
        DK = D // H
        HID = 4 * D
        EPS = 1e-05

        def _layernorm(x, w, b):
            m = jnp.mean(x, axis=-1, keepdims=True)
            v = jnp.mean(jnp.square(x - m), axis=-1, keepdims=True)
            return (x - m) * jax.lax.rsqrt(v + EPS) * w + b

        def _msa(x, w_qkv, w_proj):
            b, n, d = x.shape
            qkv = (x @ w_qkv).reshape(b, n, 3, H, DK)
            q = qkv[:, :, 0].transpose(0, 2, 1, 3)
            k = qkv[:, :, 1].transpose(0, 2, 1, 3)
            v = qkv[:, :, 2].transpose(0, 2, 1, 3)
            attn = jnp.einsum('bhnd,bhmd->bhnm', q, k) * (1.0 / np.sqrt(DK))
            attn = jax.nn.softmax(attn, axis=-1)
            y = jnp.einsum('bhnm,bhmd->bhnd', attn, v)
            y = y.transpose(0, 2, 1, 3).reshape(b, n, d)
            return y @ w_proj

        def _moe_mlp(x, gate_w, gate_b, w1, w2):
            b, n, d = x.shape
            xf = x.reshape(b * n, d)
            logits = xf @ gate_w + gate_b
            one_hot = jax.nn.one_hot(jnp.argmax(logits, axis=-1), E, dtype=xf.dtype)
            h = jax.nn.gelu(jnp.einsum('td,edh->teh', xf, w1), approximate=True)
            y = jnp.einsum('teh,ehd->ted', h, w2)
            out = jnp.einsum('te,ted->td', one_hot, y)
            return out.reshape(b, n, d)
        x = x + _msa(_layernorm(x, ln1_w, ln1_b), w_qkv, w_proj)
        x = x + _moe_mlp(_layernorm(x, ln2_w, ln2_b), gate_w, gate_b, w1, w2)
        return x
    x = L0_attn_x
    x = _layernorm(x + _L0_attn_ref(x, L0_attn_Wqkv, L0_attn_Wo, L0_attn_bo), axis=-1)
    x = _layernorm(x + _L0_ffn_ref(x, L0_ffn_ln1_w, L0_ffn_ln1_b, L0_ffn_w_qkv, L0_ffn_w_proj, L0_ffn_ln2_w, L0_ffn_ln2_b, L0_ffn_gate_w, L0_ffn_gate_b, L0_ffn_w1, L0_ffn_w2), axis=-1)
    return x

_drawn_inputs = setup_inputs


def setup_inputs(seed=0):
    import zlib

    import numpy as np

    out = dict(_drawn_inputs(seed))
    spreads = {'L0_attn_bo': (0.0, 0.1),
     'L0_ffn_ln1_w': (1.0, 0.6),
     'L0_ffn_ln1_b': (0.0, 0.8),
     'L0_ffn_ln2_w': (1.0, 0.6),
     'L0_ffn_ln2_b': (0.0, 1.469),
     'L0_ffn_gate_b': (0.0, 0.403)}
    factors = {'L0_ffn_w_qkv': 4.889, 'L0_ffn_w_proj': 5.285}
    for name, (base, spread) in spreads.items():
        noise = np.random.default_rng([zlib.crc32(name.encode()), seed]).standard_normal(out[name].shape)
        drawn = base * np.exp(spread * noise) if base else spread * noise
        out[name] = jnp.asarray(drawn.astype(out[name].dtype))
    for name, factor in factors.items():
        out[name] = (out[name] * factor).astype(out[name].dtype)
    return out
```

```python
from contextlib import ExitStack

import numpy as np

import concourse.bass as bass
from concourse import mybir

FP32 = mybir.dt.float32
BF16 = mybir.dt.bfloat16
I32 = mybir.dt.int32
U32 = mybir.dt.uint32
ALU = mybir.AluOpType
ACT = mybir.ActivationFunctionType
AX = mybir.AxisListType

BATCH, T, D, H = 8, 512, 256, 16
HD = D // H
P = 128
TT = T // P
KD = D // P
HALF = HD // 2
E = 8
HEADS_AT_ONCE = 4
GROUPS = H // HEADS_AT_ONCE
QUADS = GROUPS * TT
CHUNKS = QUADS * HEADS_AT_ONCE
VW = 32
Q_SLOTS = (0, 1, 2, 0, 1, 0)
K_SLOTS = (0, 0, 0, 1, 1, 2)
STACK = HD * len(Q_SLOTS)
NEG = 3
STACK_DMAS = 2 * len(Q_SLOTS)
F = 4 * D
KF = F // P
TILES = BATCH * T // P + E - 1
LOG_P = P.bit_length() - 1
ONE_HOT_STEP = 6
EPS = 1e-5
SCALE = 1.0 / HD ** 0.5


class Ring:

    def __init__(self, name, banks, order, sem):
        self.banks, self.order = banks, order
        assert len(order) % len(banks) == 0
        self.filled = sem(f"{name}_filled")
        self.drained = [sem(f"{name}_drained{i}") for i in range(len(banks))]

    def _k(self, use):
        return self.order.index(use)

    def bank(self, use):
        return self.banks[self._k(use) % len(self.banks)]

    def drain_sem(self, use):
        return self.drained[self._k(use) % len(self.banks)]

    def free(self, b, use):
        k, n = self._k(use), len(self.banks)
        return self.drain_sem(use), b * (len(self.order) // n) + k // n

    def full(self, b, use):
        return self.filled, b * len(self.order) + self._k(use) + 1

    def empty(self, b, use):
        s, v = self.free(b, use)
        return s, v + 1


def all_empty(eng, ring, b, uses):
    for use in uses[-len(ring.banks):]:
        eng.wait_ge(*ring.empty(b, use))


def wait(eng, sem, value):
    if not (isinstance(value, int) and value <= 0):
        eng.wait_ge(sem, value)


class Layer:

    def __init__(self, name, number, sem, psum):
        self.number, self.second = number, number == 1
        self.rows = STACK + (NEG if self.second else 0)
        self.p_tasks, self.o_tasks = {}, {}
        if not self.second:
            p_steps = ((1, 2, "T0"), (2, 0, "T1"), (2, 2, "qA"), (3, 2, "qB"), (4, 2, "kA"),
                       (5, 2, "sq"), (5, 2, "kB"), (6, 2, "nq"), (7, 0, "uq"), (7, 2, "hq"),
                       (7, 2, "sk"), (8, 2, "nk"), (8, 2, "lq"), (9, 0, "uk"), (9, 2, "hk"),
                       (10, 0, "lk"), (10, 2, "V0"), (12, 2, "V1"))
            o_at = lambda t: (("TO", 4 + 6 * t), ("TP", 6 + 6 * t), ("WO", 8 + 6 * t),
                              ("N1", 10 + 6 * t), ("N2", 12 + 6 * t))
            p_banks, o_banks, st_banks, pv_banks, mx_banks = [4], [5], [0, 1, 2, 3], [6, 7], []
        else:
            p_steps = ((1, 0, "T0"), (1, 2, "T1"), (2, 2, "qA"), (3, 2, "qB"), (4, 0, "mq"),
                       (4, 2, "kA"), (5, 2, "kB"), (6, 0, "mk"), (7, 2, "V0"), (9, 2, "V1"))
            o_at = lambda t: (("TO", 3 + 5 * t), ("TP", 5 + 5 * t), ("WO", 7 + 5 * t),
                              ("N2", 9 + 5 * t), ("HT", 11 + 5 * t), ("GT", 14 + 5 * t))
            p_banks, o_banks, st_banks, pv_banks, mx_banks = [5], [6], [0, 1, 7], [2], [3, 4]
        for q, j, step in p_steps:
            self.p_tasks.setdefault((q, j), []).append(step)
        for t in range(TT):
            for step, at in o_at(t):
                self.o_tasks.setdefault(SLOTS[at], []).append(f"{step}{t}")
        in_psum = lambda tasks: [x for slot in SLOTS for x in tasks.get(slot, [])
                                 if x[0] not in "Nmsuhl"]
        banks = lambda ids: [psum[i] for i in ids]
        self.p_ring = Ring(f"{name}_proj", banks(p_banks), in_psum(self.p_tasks), sem)
        self.o_ring = Ring(f"{name}_out", banks(o_banks), in_psum(self.o_tasks), sem)
        self.st_banks, self.pv_banks = banks(st_banks), banks(pv_banks)
        s = lambda n: sem(f"{name}_{n}")
        if self.second:
            order = []
            for g in range(GROUPS):
                order += [("MX", g, c) for c in range(HEADS_AT_ONCE * TT)] + [("NG", g)]
            self.mx_ring = Ring(f"{name}_max", banks(mx_banks), order, sem)
            self.neg_step = s("neg_step")
            self.neg_ready = s("neg_ready")
            self.neg_in = s("neg_in")
        self.x_in = s("x_in")
        self.res_in = s("res_in")
        self.res_ready = s("res_ready")
        self.sq_done = s("sq_done")
        self.rot_done = s("rot_done")
        self.rs_ready = s("rs_ready")
        self.high_done = s("high_done")
        self.mid_done = s("mid_done")
        self.p_step = s("p_step")
        self.parts_ready = s("parts_ready")
        self.stack_in = [s("q_in"), s("k_in")]
        self.scores = s("scores")
        self.exps = s("exps")
        self.pv_done = s("pv_done")
        self.oT_ready = s("oT_ready")
        self.sum_ready = s("sum_ready")
        self.o_step = s("o_step")
        self.mv_ready = s("mv_ready")
        self.rstd_step = s("rstd_step")
        self.rstd_ready = s("rstd_ready")
        self.hn_ready = s("hn_ready")
        self.hw_step = s("hw_step")
        self.h_ready = s("h_ready")
        self.x_out = [s("x_out0"), s("x_out1")]
        self.h_out = [s("h_out0"), s("h_out1")]


SLOTS = [(q, j) for q in range(QUADS) for j in (0, 2)]
SPLIT_STEPS = 7
MAX_LEAD = 6
ACT_LAG, DVE_LAG = (1, 0), (1, 0)
PV_AFTER = 1
O_STEPS = (4, 2)


def program(nc, x, w_qkv1, w_o1, b_o, ln1_w, ln1_b, w_qkv2, w_o2, ln2_w, ln2_b, gate_w, gate_b,
            w1, w2, cos_t, sin_t, head_sum, ident, route_consts, out):
    ctx = ExitStack()
    with ctx:
        def sb(name, shape, dt=FP32):
            return ctx.enter_context(nc.sbuf_tensor(name, shape, dt))

        def sem(name):
            return ctx.enter_context(nc.semaphore(name))

        def dram(name, shape, dt=FP32):
            return nc.dram_tensor(name, shape, dt).ap()

        x1_dram = dram("x1_dram", [BATCH, T, D])
        h1_dram = dram("h1_dram", [BATCH, T, D])
        sum_dram = dram("sum_dram", [BATCH, T, D])
        h2_dram = dram("h2_dram", [BATCH, T, D])

        psum = [ctx.enter_context(nc.psum_tensor(f"bank{i}", [P, T], FP32)) for i in range(8)]
        ident_sb = sb("ident_sb", [P, P])
        ident_bf = sb("ident_bf", [P, P], BF16)
        head_sum_sb = sb("head_sum_sb", [P, P])
        cos_sb = sb("cos_sb", [P, T])
        sin_sb = sb("sin_sb", [P, T])
        wqkv_sb = sb("wqkv_sb", [P, 2, KD, 3 * D])
        wo_sb = sb("wo_sb", [P, 2, KD, D])
        rows_sb = sb("rows_sb", [P, 5, D])
        gate_w_sb = sb("gate_w_sb", [P, KD, E])
        gate_b_sb = sb("gate_b_sb", [P, E])
        eps_sb = sb("eps_sb", [P, 2])
        logits = sb("logits", [P, BATCH * TT, E])

        def carve(space, pieces):
            at, got = 0, []
            for dims, shape, dt in pieces:
                n = int(np.prod(list(shape.values()))) * (1 if dt == FP32 else 2) // (
                    1 if dt == FP32 else 4)
                piece = space[:, at:at + n]
                if dt != FP32:
                    piece = piece.bitcast(dt)
                got.append(piece.rearrange(f"p ({dims}) -> p {dims}", **shape))
                at += n
            assert at <= space.shape[1], (at, space.shape)
            return got

        NTOK = BATCH * TT

        w1_space = sb("w1_space", [P, E * KD * F])
        w2_space = sb("w2_space", [P, E * KF * D])
        work_space = sb("work_space", [P, 8192])
        q_stack, k_stack = carve(w1_space, [("s h t", dict(s=2, h=H, t=T), BF16)] * 2)
        v_aug, probs, oT, trig, rest = carve(w2_space, [
            ("s t h e", dict(s=2, t=TT, h=H, e=VW), FP32),
            ("s j t", dict(s=2, j=HEADS_AT_ONCE, t=T), FP32),
            ("s g t", dict(s=2, g=GROUPS, t=T), FP32),
            ("n t", dict(n=4, t=T), FP32),
            ("a c t", dict(a=2, c=2, t=T), FP32)])
        x_sb, res_sb, xT, sq, rs, parts = carve(work_space, [
            ("t d", dict(t=TT, d=D), FP32), ("t d", dict(t=TT, d=D), FP32),
            ("k t", dict(k=KD, t=T), FP32), ("c t", dict(c=2, t=T), FP32),
            ("a t", dict(a=1, t=T), FP32),
            ("a n c t", dict(a=2, n=3, c=2, t=T), BF16)])
        rs = rs[:, 0, :]
        (w1_sb,) = carve(w1_space, [("e k f", dict(e=E, k=KD, f=F), FP32)])
        (w2_sb,) = carve(w2_space, [("e k d", dict(e=E, k=KF, d=D), FP32)])
        xs_sb, xsT, hid, hidT, ys_sb, stage, slot3, cum = carve(work_space, [
            ("s d", dict(s=2, d=D), FP32), ("s k t", dict(s=2, k=KD, t=P), FP32),
            ("s f", dict(s=2, f=F), FP32), ("s k t", dict(s=2, k=KF, t=P), FP32),
            ("s d", dict(s=2, d=D), FP32), ("s t d", dict(s=2, t=TT, d=D), FP32),
            ("t e", dict(t=NTOK, e=E), FP32), ("e t", dict(e=E, t=NTOK), FP32)])
        sum_ring = hid.rearrange("p s (t d) -> p s t d", t=TT)
        out_ring = hidT.rearrange("p s k t -> p s (k t)").rearrange("p s (t d) -> p s t d", t=TT)

        route_c = sb("route_c", [P, P + E + TILES])
        ones_sb = sb("ones_sb", [P, P])
        top = sb("top", [P, NTOK])
        one_hot = sb("one_hot", [P, NTOK, E])
        counts_i = sb("counts_i", [P, E], I32)
        n_tiles = sb("n_tiles", [P, E])
        tile_end = sb("tile_end", [P, E])
        row_base = sb("row_base", [P, E])
        slot_f = sb("slot_f", [P, NTOK])
        slot_u = sb("slot_u", [P, NTOK], U32)
        past = sb("past", [1, TILES, E])
        tile_e_f = sb("tile_e_f", [1, TILES])
        tile_expert = sb("tile_expert", [1, TILES], I32)
        xs_dram = dram("xs_dram", [TILES * P, D])
        ys_dram = dram("ys_dram", [TILES * P, D])
        mv4 = sb("mv4", [P, 2, TT, 2])
        stats4 = sb("stats4", [P, TT, 6])
        rstd4 = sb("rstd4", [P, 2, TT])

        zeros_set = sem("zeros_set")
        zeros_sb = sb("zeros_sb", [P, 1, D])
        weights_in = [sem("w1_in"), sem("w2_in")]
        route_step = sem("route_step")
        route_sums = sem("route_sums")
        slots_ready = sem("slots_ready")
        zeros_in = sem("zeros_in")
        stage_in = [sem("stage_in0"), sem("stage_in1")]
        dispatched = [sem("dispatched0"), sem("dispatched1")]
        xs_in = [sem("xs_in0"), sem("xs_in1")]
        xs_T = sem("xs_T")
        xsT_ready = sem("xsT_ready")
        up_done = sem("up_done")
        gelu_done = sem("gelu_done")
        hid_T = sem("hid_T")
        hidT_ready = sem("hidT_ready")
        down_done = sem("down_done")
        ys_ready = sem("ys_ready")
        ys_out = [sem("ys_out0"), sem("ys_out1")]
        sum_in = [sem("sum_in0"), sem("sum_in1")]
        gathered = [sem("gathered0"), sem("gathered1")]
        sum_done = sem("sum_done")
        last_stats = sem("last_stats")
        last_mv = sem("last_mv")
        last_ln = sem("last_ln")
        last_rstd = sem("last_rstd")
        out_ready = sem("out_ready")
        out_done = [sem("out_done0"), sem("out_done1")]
        recip = sb("recip", [P, H])
        on = sb("on", [P, 2, D])
        onT = sb("onT", [P, 2, KD, P])
        y = sb("y", [P, 2, D])
        xo = sb("xo", [P, 2, D])
        hn = sb("hn", [P, 2, D])
        stats = sb("stats", [P, 6])
        wait_cell = sb("wait_cell", [P, 1])
        mv = sb("mv", [P, 2, 2, 2])
        rstd = sb("rstd", [P, 2, 2])
        negm = sb("negm", [P, TT, HEADS_AT_ONCE])
        neg_rest = sb("neg_rest", [P, TT, HEADS_AT_ONCE])
        neg_parts = sb("neg_parts", [P, TT, NEG, HEADS_AT_ONCE], BF16)
        neg_T = sb("neg_T", [NEG * HEADS_AT_ONCE, T], BF16)

        consts_in = sem("consts_in")
        consts_set = sem("consts_set")
        pool_set = sem("pool_set")
        layers = [Layer("a", 0, sem, psum), Layer("b", 1, sem, psum)]
        N_CONST_DMAS, N_CONST_OPS = 19, 4
        PARTS_OF = (("qA", "qB"), ("kA", "kB"))

        def tiles(ap, b):
            return ap[bass.ds(b, 1), :, :].rearrange("a (t p) d -> p (a t) d", p=P)

        def tile_of(ap, b, t):
            return ap[bass.ds(b, 1), t * P:(t + 1) * P, :].rearrange("a p d -> (a p) d")

        def pipeline(eng, L, body):
            body(L, 0, 0, None, None)
            body(L, 1, 1, 0, None)
            with eng.Fori(1, BATCH // 2) as pair:
                body(L, 0, 2 * pair, 2 * pair - 1, 2 * pair - 2)
                body(L, 1, 2 * pair + 1, 2 * pair, 2 * pair - 1)
            body(L, 0, None, BATCH - 1, BATCH - 2)
            body(L, 1, None, None, BATCH - 1)

        def outer_tasks(L, slot, bP, bO, par, task):
            if bO is not None:
                for name in L.o_tasks.get(slot, []):
                    task(L, name, bO, par)
            if bP is not None:
                for name in L.p_tasks.get(slot, []):
                    task(L, name, bP, par)

        def max_tiles(q, par, bP, bA):
            at = q - (QUADS - MAX_LEAD)
            b, at, s = (bP, at, par) if at >= 0 else (bA, at + QUADS, 1 - par)
            return [] if b is None else [
                (b, at // TT, HEADS_AT_ONCE * (at % TT) + j, s) for j in range(HEADS_AT_ONCE)]

        def neg_group(q, par, bP, bA):
            at = q - (QUADS - MAX_LEAD)
            b, at, s = (bP, at, par) if at > 0 else (bA, at + QUADS, 1 - par)
            return [] if b is None or at % TT else [(b, at // TT - 1, s)]

        def half_of(name):
            return "qk".index(name[0]), "AB".index(name[1])

        def v_out(eng, ops, L, name, b, s):
            j, p = int(name[1]), L.p_ring
            eng.wait_ge(*p.full(b, name))
            if not isinstance(b, int) or b >= 2:
                eng.wait_ge(L.pv_done, QUADS * (b - 2) + QUADS)
            dst = v_aug[:, s, 2 * j:2 * j + 2, :, 0:HD]
            src = p.bank(name)[:, :].rearrange("p (t h e) -> p t h e", t=2, h=H)
            if ops is nc.scalar:
                last = nc.scalar.activation(dst, src, ACT.Copy)
            else:
                last = nc.vector.tensor_copy(dst, src)
            last.then_inc(p.drain_sem(name), 1)

        block = ctx.enter_context(nc.Block())

        @block.tensor
        def _(pe):
            pe.wait_ge(consts_in, 16 * N_CONST_DMAS)
            pe.wait_ge(consts_set, N_CONST_OPS)
            pe.wait_ge(pool_set, 3)

            def score(L, b, s, c):
                q, j = c // HEADS_AT_ONCE, c % HEADS_AT_ONCE
                g, kt = q // TT, q % TT
                h, n = HEADS_AT_ONCE * g + j, len(L.st_banks)
                if c == 0:
                    for arrived in L.stack_in:
                        pe.wait_ge(arrived, 16 * STACK_DMAS * b + 16 * STACK_DMAS)
                if L.second and j == 0 and kt == 0:
                    pe.wait_ge(L.neg_in, 16 * GROUPS * b + 16 * (g + 1))
                wait(pe, L.exps, CHUNKS * b + (c + 1 - n if CHUNKS % n == 0 or c else 0))
                nc.tensor.matmul(L.st_banks[c % n][:, :],
                                 k_stack[0:L.rows, s, h, kt * P:(kt + 1) * P],
                                 q_stack[0:L.rows, s, h, :], start=True, stop=True
                                 ).then_inc(L.scores, 1)

            def pv(L, b, s, q):
                g, kt, n = q // TT, q % TT, len(L.pv_banks)
                pe.wait_ge(L.exps, CHUNKS * b + HEADS_AT_ONCE * (q + 1))
                if q == 0:
                    all_empty(pe, L.p_ring, b, ("V0", "V1"))
                if kt == 0:
                    wait(pe, L.oT_ready, GROUPS * b + (g + 1 - n))
                for j in range(HEADS_AT_ONCE):
                    last = nc.tensor.matmul(L.pv_banks[g % n][VW * j:VW * (j + 1), :],
                                            v_aug[:, s, kt, HEADS_AT_ONCE * g + j, :],
                                            probs[:, q % 2, j, :],
                                            start=(kt == 0), stop=(kt == TT - 1))
                last.then_inc(L.pv_done, 1)

            def max_score(L, b, g, c, s):
                use, h, qt = ("MX", g, c), HEADS_AT_ONCE * g + c // TT, c % TT
                if g == 0 and c == 0:
                    for arrived in L.stack_in:
                        pe.wait_ge(arrived, 16 * STACK_DMAS * b + 16 * STACK_DMAS)
                wait(pe, *L.mx_ring.free(b, use))
                nc.tensor.matmul(L.mx_ring.bank(use)[:, :],
                                 q_stack[0:STACK, s, h, qt * P:(qt + 1) * P],
                                 k_stack[0:STACK, s, h, :], start=True, stop=True
                                 ).then_inc(L.mx_ring.filled, 1)

            def neg_rows(L, b, g):
                pe.wait_ge(L.neg_ready, GROUPS * b + (g + 1))
                wait(pe, *L.mx_ring.free(b, ("NG", g)))
                rows = L.mx_ring.bank(("NG", g))[0:NEG * HEADS_AT_ONCE, 0:T // 2].bitcast(BF16)
                for qt in range(TT):
                    last = nc.tensor.transpose(rows[:, qt * P:(qt + 1) * P],
                                               neg_parts[:, qt, :, :].rearrange("p a h -> p (a h)"),
                                               ident_bf[:, :])
                last.then_inc(L.mx_ring.filled, 1)

            def task(L, name, b, s):
                kind, t = name[:2], name[-1]
                if kind[0] in "Nmsuhl":
                    return
                ring = L.p_ring if name in L.p_ring.order else L.o_ring
                bank = ring.bank(name)
                if not (name == "qA" and len(ring.banks) > 1):
                    wait(pe, *ring.free(b, name))
                if name in ("T0", "T1"):
                    pe.wait_ge(L.x_in, 16 * b + 16)
                    for j in range(TT):
                        last = nc.tensor.transpose(bank[:, j * P:(j + 1) * P],
                                                   x_sb[:, j, int(t) * P:(int(t) + 1) * P],
                                                   ident_sb[:, :])
                elif name in ("qA", "qB", "kA", "kB"):
                    if name == "qA" and len(ring.banks) > 1:
                        all_empty(pe, ring, b, ("T0", "T1"))
                    c = ("qA", "qB", "kA", "kB").index(name)
                    for k in range(KD):
                        last = nc.tensor.matmul(bank[:, :],
                                                wqkv_sb[:, L.number, k, c * P:(c + 1) * P],
                                                xT[:, k, :], start=(k == 0), stop=(k == KD - 1))
                elif name in ("nq", "nk"):
                    pe.wait_ge(L.sq_done, 2 * b + (1 if name == "nq" else 2))
                    for k in range(2):
                        last = nc.tensor.matmul(bank[:, :], head_sum_sb[:, :], sq[:, k, :],
                                                start=(k == 0), stop=(k == 1))
                elif kind[0] == "V":
                    for j in range(2):
                        tt = 2 * int(t) + j
                        for k in range(KD):
                            last = nc.tensor.matmul(bank[:, j * D:(j + 1) * D],
                                                    xT[:, k, tt * P:(tt + 1) * P],
                                                    wqkv_sb[:, L.number, k, 2 * D:3 * D],
                                                    start=(k == 0), stop=(k == KD - 1))
                elif kind == "TO":
                    t = int(t)
                    if t == 0:
                        pe.wait_ge(L.oT_ready, GROUPS * b + GROUPS)
                    for g in range(GROUPS):
                        last = nc.tensor.transpose(bank[:, g * P:(g + 1) * P],
                                                   oT[:, s, g, t * P:(t + 1) * P], ident_sb[:, :])
                elif kind == "TP":
                    t = int(t)
                    pe.wait_ge(*ring.empty(b, f"TO{t}"))
                    for k in range(KD):
                        last = nc.tensor.transpose(bank[:, k * P:(k + 1) * P],
                                                   on[:, t % 2, k * P:(k + 1) * P], ident_sb[:, :])
                elif kind == "WO":
                    t = int(t)
                    pe.wait_ge(*ring.empty(b, f"TP{t}"))
                    for k in range(KD):
                        last = nc.tensor.matmul(bank[:, 0:D], onT[:, t % 2, k, :],
                                                wo_sb[:, L.number, k, :],
                                                start=(k == 0), stop=(k == KD - 1))
                elif kind == "HT":
                    t = int(t)
                    pe.wait_ge(L.h_ready, TT * b + (t + 1))
                    for k in range(KD):
                        last = nc.tensor.transpose(bank[:, k * P:(k + 1) * P],
                                                   hn[:, t % 2, k * P:(k + 1) * P], ident_sb[:, :])
                elif kind == "GT":
                    t = int(t)
                    pe.wait_ge(*ring.empty(b, f"HT{t}"))
                    for k in range(KD):
                        last = nc.tensor.matmul(bank[:, 0:E], onT[:, t % 2, k, :],
                                                gate_w_sb[:, k, :],
                                                start=(k == 0), stop=(k == KD - 1))
                last.then_inc(ring.filled, 1)

            def body(L, par, bP, bA, bO):
                for q in range(QUADS):
                    mx = max_tiles(q, par, bP, bA) if L.second else []
                    groups = neg_group(q, par, bP, bA) if L.second else []
                    late = []
                    for j in range(HEADS_AT_ONCE):
                        if bA is not None:
                            score(L, bA, 1 - par, HEADS_AT_ONCE * q + j)
                        late += mx[j:j + 1]
                        if j == PV_AFTER:
                            if q == 0 and bO is not None:
                                pv(L, bO, par, QUADS - 1)
                            if q and bA is not None:
                                pv(L, bA, 1 - par, q - 1)
                            for b, g, s in groups:
                                neg_rows(L, b, g)
                            groups = []
                        if not groups:
                            for tile in late:
                                max_score(L, *tile)
                            late = []
                        outer_tasks(L, (q, j), bP, bO, par, task)

            for L in layers:
                pipeline(pe, L, body)

            pe.wait_ge(route_step, ONE_HOT_STEP)
            flat = one_hot[:, :, :].rearrange("p t e -> p (t e)")
            nc.tensor.matmul(psum[0][:, 0:NTOK * E], route_c[:, 0:P], flat, start=True, stop=True
                             ).then_inc(route_sums, 1)
            nc.tensor.matmul(psum[1][:, 0:NTOK * E], ones_sb[:, :], flat, start=True, stop=True
                             ).then_inc(route_sums, 1)
            pe.wait_ge(slots_ready, 2)
            for arrived in weights_in:
                pe.wait_ge(arrived, 16 * E)

            def expert_of(j):
                return pe.value_load(tile_expert[0:1, bass.ds(j, 1)], min_val=0, max_val=E - 1)

            def transpose_in(j, s):
                pe.wait_ge(xs_in[s], 8 * (j - s) + 16)
                wait(pe, xsT_ready, j)
                for k in range(KD):
                    last = nc.tensor.transpose(psum[4][:, k * P:(k + 1) * P],
                                               xs_sb[:, s, k * P:(k + 1) * P], ident_sb[:, :])
                last.then_inc(xs_T, 1)

            def up(j, s):
                e = expert_of(j)
                pe.wait_ge(xsT_ready, j + 1)
                for n in range(2):
                    wait(pe, gelu_done, 2 * j + (n - 1))
                    for k in range(KD):
                        last = nc.tensor.matmul(
                            psum[n][:, :], xsT[:, s, k, :],
                            w1_sb[:, bass.ds(e, 1), k, n * T:(n + 1) * T].rearrange(
                                "p a f -> p (a f)"),
                            start=(k == 0), stop=(k == KD - 1))
                    last.then_inc(up_done, 1)

            def transpose_hidden(j, s):
                for n in range(2):
                    pe.wait_ge(gelu_done, 2 * j + (n + 1))
                    wait(pe, hidT_ready, 2 * j + (n - 1))
                    for k in range(KF // 2):
                        at = n * T + k * P
                        last = nc.tensor.transpose(psum[2 + n][:, k * P:(k + 1) * P],
                                                   hid[:, s, at:at + P], ident_sb[:, :])
                    last.then_inc(hid_T, 1)

            def down(j, s):
                e = expert_of(j)
                pe.wait_ge(hidT_ready, 2 * j + 2)
                wait(pe, ys_ready, j)
                for k in range(KF):
                    last = nc.tensor.matmul(
                        psum[5][:, 0:D], hidT[:, s, k, :],
                        w2_sb[:, bass.ds(e, 1), k, :].rearrange("p a d -> p (a d)"),
                        start=(k == 0), stop=(k == KF - 1))
                last.then_inc(down_done, 1)

            def expert_body(j, s, ends=False):
                transpose_hidden(j - 1, 1 - s)
                up(j, s)
                if not ends:
                    transpose_in(j + 1, 1 - s)
                down(j - 1, 1 - s)

            transpose_in(0, 0)
            up(0, 0)
            transpose_in(1, 1)
            expert_body(1, 1)
            expert_body(2, 0)
            with pe.Fori(1, TILES // 2 - 1) as pair:
                expert_body(2 * pair + 1, 1)
                expert_body(2 * pair + 2, 0)
            expert_body(TILES - 2, 1)
            expert_body(TILES - 1, 0, ends=True)
            transpose_hidden(TILES - 1, 0)
            down(TILES - 1, 0)

        @block.scalar
        def _(act):
            nc.scalar.preload_act_table_set("natural_log_exp_and_others")
            act.wait_ge(consts_set, N_CONST_OPS)

            def exp(L, b, c):
                q, j = c // HEADS_AT_ONCE, c % HEADS_AT_ONCE
                act.wait_ge(L.scores, CHUNKS * b + (c + 1))
                if j == 0:
                    wait(act, L.pv_done, QUADS * b + (q - 1))
                nc.scalar.activation(probs[:, q % 2, j, :], L.st_banks[c % len(L.st_banks)][:, :],
                                     ACT.Exp, scale=SCALE).then_inc(L.exps, 1)

            def group_out(L, b, s, g):
                act.wait_ge(L.pv_done, QUADS * b + TT * (g + 1))
                nc.scalar.activation(oT[:, s, g, :], L.pv_banks[g % len(L.pv_banks)][:, :], ACT.Copy
                                     ).then_inc(L.oT_ready, 1)

            def neg_rows(L, b, g):
                act.wait_ge(*L.mx_ring.full(b, ("NG", g)))
                wait(act, L.neg_in, 16 * GROUPS * b + 16 * g)
                nc.scalar.activation(neg_T[:, :],
                                     L.mx_ring.bank(("NG", g))[0:NEG * HEADS_AT_ONCE, 0:T // 2]
                                     .bitcast(BF16), ACT.Copy
                                     ).then_inc(L.mx_ring.drain_sem(("NG", g)), 1)

            def task(L, name, b, s):
                kind, t = name[:2], name[-1]
                p, o = L.p_ring, L.o_ring
                if name in ("T0", "T1") and L.second:
                    act.wait_ge(*p.full(b, name))
                    nc.scalar.activation(xT[:, int(t), :], p.bank(name)[:, :], ACT.Copy
                                         ).then_inc(p.drain_sem(name), 1)
                elif name in ("qA", "qB", "kA", "kB") and L.second:
                    qk, half = half_of(name)
                    act.wait_ge(*p.full(b, name))
                    wait(act, L.stack_in[qk], 16 * STACK_DMAS * b)
                    nc.scalar.activation(parts[:, qk, 0, half, :], p.bank(name)[:, :], ACT.Copy
                                         ).then_inc(L.high_done, 1)
                elif name in ("sq", "sk"):
                    qk = "qk".index(name[1])
                    act.wait_ge(L.rot_done, 2 * b + (qk + 1))
                    if qk:
                        act.wait_ge(*p.full(b, "nq"))
                    elif not isinstance(b, int) or b >= 1:
                        act.wait_ge(*p.full(b - 1, "nk"))
                    nc.scalar.activation(sq[:, :, :], rest[:, qk, :, :], ACT.Square
                                         ).then_inc(L.sq_done, 1)
                elif name in ("nq", "nk"):
                    n = "qk".index(name[1])
                    act.wait_ge(*p.full(b, name))
                    wait(act, L.p_step, 2 * SPLIT_STEPS * b + (SPLIT_STEPS * (n - 1) + 2))
                    nc.scalar.activation(rs[:, :], p.bank(name)[:, :], ACT.Ln,
                                         bias=eps_sb[:, 1:2]).then_inc(p.drain_sem(name), 1)
                    act.wait_ge(*p.empty(b, name))
                    nc.scalar.activation(rs[:, :], rs[:, :], ACT.Exp, scale=-0.5
                                         ).then_inc(L.rs_ready, 1)
                elif name in ("mq", "mk"):
                    qk = "qk".index(name[1])
                    all_empty(act, p, b, PARTS_OF[qk])
                    nc.scalar.activation(parts[:, qk, 1, :, :], rest[:, qk, :, :], ACT.Copy
                                         ).then_inc(L.mid_done, 1)
                elif kind[0] == "V" and L.second:
                    v_out(act, nc.scalar, L, name, b, s)
                elif kind in ("TP", "HT"):
                    act.wait_ge(*o.full(b, name))
                    nc.scalar.activation(onT[:, int(t) % 2, :, :].rearrange("p k c -> p (k c)"),
                                         o.bank(name)[:, 0:D], ACT.Copy
                                         ).then_inc(o.drain_sem(name), 1)
                elif kind[0] == "N":
                    t = int(t)
                    n = TT * b + (t + 1) if L.second else 2 * TT * b + (2 * t + int(kind[1]))
                    which = int(kind[1]) - 1
                    r = rstd[:, t % 2, which:which + 1]
                    act.wait_ge(L.mv_ready, n)
                    nc.scalar.activation(r, mv[:, t % 2, which, 1:2], ACT.Ln, bias=eps_sb[:, 0:1]
                                         ).then_inc(L.rstd_step, 1)
                    act.wait_ge(L.rstd_step, n)
                    nc.scalar.activation(r, r, ACT.Exp, scale=-0.5).then_inc(L.rstd_ready, 1)

            def body(L, par, bP, bA, bO):
                if bP is not None:
                    if not isinstance(bP, int) or bP >= 1:
                        act.wait_ge(*L.p_ring.full(bP - 1, "T1"))
                    act.dma_start(x_sb[:, :, :], tiles(h1_dram if L.second else x, bP)
                                 ).then_inc(L.x_in, 16)
                if bO is not None:
                    if not isinstance(bO, int) or bO >= 1:
                        if L.second:
                            act.wait_ge(L.x_out[0], 16 * bO)
                        else:
                            act.wait_ge(*L.o_ring.empty(bO - 1, f"WO{TT - 1}"))
                    act.dma_start(res_sb[:, :, :], tiles(x1_dram if L.second else x, bO)
                                 ).then_inc(L.res_in, 16)
                for q in range(QUADS):
                    for j in range(HEADS_AT_ONCE):
                        if bA is not None:
                            exp(L, bA, HEADS_AT_ONCE * q + j)
                        if j == 1 and L.second:
                            for b, g, s in neg_group(q, par, bP, bA):
                                neg_rows(L, b, g)
                        if j == 2 and q == 0 and bO is not None:
                            group_out(L, bO, par, GROUPS - 1)
                        if j == 2 and q and q % TT == 0 and bA is not None:
                            group_out(L, bA, 1 - par, q // TT - 1)
                        outer_tasks(L, (q, j - ACT_LAG[L.number]), bP, bO, par, task)

            for L in layers:
                pipeline(act, L, body)

            def gelu(j, s):
                for n in range(2):
                    act.wait_ge(up_done, 2 * j + (n + 1))
                    if n == 0:
                        wait(act, hid_T, 2 * j - 2)
                    nc.scalar.activation(hid[:, s, n * T:(n + 1) * T], psum[n][:, :],
                                         ACT.Gelu_apprx_tanh).then_inc(gelu_done, 1)

            gelu(0, 0)
            gelu(1, 1)
            gelu(2, 0)
            with act.Fori(1, TILES // 2) as pair:
                gelu(2 * pair + 1, 1)
                gelu(2 * pair + 2, 0)

            def last_norm(b, s):
                act.wait_ge(last_mv, b + 1)
                nc.scalar.activation(rstd4[:, s, :], mv4[:, s, :, 1], ACT.Ln, bias=eps_sb[:, 0:1]
                                     ).then_inc(last_ln, 1)
                act.wait_ge(last_ln, b + 1)
                nc.scalar.activation(rstd4[:, s, :], rstd4[:, s, :], ACT.Exp, scale=-0.5
                                     ).then_inc(last_rstd, 1)

            with act.Fori(0, BATCH // 2) as pair:
                last_norm(2 * pair, 0)
                last_norm(2 * pair + 1, 1)

        @block.vector
        def _(dve):
            ve = nc.vector
            dve.wait_ge(consts_in, 16 * N_CONST_DMAS)
            ve.tensor_copy(ident_bf[:, :], ident_sb[:, :]).then_inc(consts_set, 1)
            ve.memset(eps_sb[:, 0:1], EPS).then_inc(consts_set, 1)
            ve.memset(eps_sb[:, 1:2], 1e-6).then_inc(consts_set, 1)
            ve.memset(ones_sb[:, :], 1.0).then_inc(consts_set, 1)

            def max_tile(L, b, g, c, s):
                use = ("MX", g, c)
                dve.wait_ge(*L.mx_ring.full(b, use))
                ve.tensor_reduce(negm[:, c % TT, c // TT:c // TT + 1], L.mx_ring.bank(use)[:, :],
                                 axis=AX.X, op=ALU.max, negate=True
                                 ).then_inc(L.mx_ring.drain_sem(use), 1)

            def neg_split(L, b, g):
                last_tile = HEADS_AT_ONCE * TT - 1
                dve.wait_ge(*L.mx_ring.empty(b, ("MX", g, last_tile - 1)))
                dve.wait_ge(*L.mx_ring.empty(b, ("MX", g, last_tile)))
                if g:
                    dve.wait_ge(*L.mx_ring.full(b, ("NG", g - 1)))
                elif not isinstance(b, int) or b >= 1:
                    dve.wait_ge(*L.mx_ring.full(b - 1, ("NG", GROUPS - 1)))
                n = 3 * GROUPS * b
                ve.tensor_copy(neg_parts[:, :, 0, :], negm[:, :, :]).then_inc(L.neg_step, 1)
                dve.wait_ge(L.neg_step, n + (3 * g + 1))
                ve.tensor_tensor(neg_rest[:, :, :], negm[:, :, :], neg_parts[:, :, 0, :],
                                 ALU.subtract).then_inc(L.neg_step, 1)
                dve.wait_ge(L.neg_step, n + (3 * g + 2))
                ve.tensor_copy(neg_parts[:, :, 1, :], neg_rest[:, :, :]).then_inc(L.neg_step, 1)
                dve.wait_ge(L.neg_step, n + (3 * g + 3))
                ve.tensor_tensor(neg_parts[:, :, 2, :], neg_rest[:, :, :], neg_parts[:, :, 1, :],
                                 ALU.subtract).then_inc(L.neg_ready, 1)

            def norm_and_split(L, name, b):
                qk = "qk".index(name[1])
                n = 2 * SPLIT_STEPS * b + SPLIT_STEPS * qk
                if name[0] == "u":
                    dve.wait_ge(L.rs_ready, 2 * b + (qk + 1))
                    for half in range(2):
                        ve.tensor_tensor(rest[:, qk, half, :], rest[:, qk, half, :], rs[:, :],
                                         ALU.mult).then_inc(L.p_step, 1)
                elif name[0] == "h":
                    wait(dve, L.stack_in[qk], 16 * STACK_DMAS * b)
                    for half in range(2):
                        dve.wait_ge(L.p_step, n + (1 + half))
                        ve.tensor_copy(parts[:, qk, 0, half, :], rest[:, qk, half, :]
                                       ).then_inc(L.p_step, 1)
                    for half in range(2):
                        dve.wait_ge(L.p_step, n + (3 + half))
                        ve.tensor_tensor(rest[:, qk, half, :], rest[:, qk, half, :],
                                         parts[:, qk, 0, half, :], ALU.subtract
                                         ).then_inc(L.p_step, 1)
                else:
                    for half in range(2):
                        dve.wait_ge(L.p_step, n + (5 + half))
                        ve.tensor_copy(parts[:, qk, 1, half, :], rest[:, qk, half, :]
                                       ).then_inc(L.mid_done if half else L.p_step, 1)

            def moments(L, n, src, dst):
                ve.bn_stats(stats[:, :], src).then_inc(L.o_step, 1)
                dve.wait_ge(L.o_step, n + 1)
                ve.memset(wait_cell[:, :], 0.0)
                ve.bn_aggr(dst, stats[:, :]).then_inc(L.mv_ready, 1)

            def task(L, name, b, s):
                kind, t = name[:2], name[-1]
                p, o = L.p_ring, L.o_ring
                per_tile = O_STEPS[L.number]
                if name in ("T0", "T1") and not L.second:
                    dve.wait_ge(*p.full(b, name))
                    ve.tensor_copy(xT[:, int(t), :], p.bank(name)[:, :]
                                   ).then_inc(p.drain_sem(name), 1)
                elif name in ("qA", "qB", "kA", "kB"):
                    qk, half = half_of(name)
                    if not L.second:
                        dve.wait_ge(*p.full(b, name))
                        wait(dve, L.rot_done, 2 * b + qk)
                        first, then = (sin_sb, cos_sb) if half else (cos_sb, sin_sb)
                        ve.tensor_tensor(trig[:, 2 * half, :], p.bank(name)[:, :], first[:, :],
                                         ALU.mult)
                        ve.tensor_tensor(trig[:, 2 * half + 1, :], p.bank(name)[:, :], then[:, :],
                                         ALU.mult).then_inc(p.drain_sem(name), 1)
                    else:
                        dve.wait_ge(L.high_done, 4 * b + (2 * qk + half + 1))
                        wait(dve, L.parts_ready, 2 * b + (qk - 1))
                        ve.tensor_tensor(rest[:, qk, half, :], p.bank(name)[:, :],
                                         parts[:, qk, 0, half, :], ALU.subtract
                                         ).then_inc(p.drain_sem(name), 1)
                elif kind[0] in "uhl":
                    norm_and_split(L, name, b)
                elif kind[0] == "V" and not L.second:
                    v_out(dve, nc.vector, L, name, b, s)
                elif kind == "TO":
                    t = int(t)
                    heads = o.bank(name)[:, :].rearrange("p (h e) -> p h e", h=H)
                    dve.wait_ge(*o.full(b, name))
                    ve.reciprocal(recip[:, :], heads[:, :, HD]).then_inc(L.o_step, 1)
                    dve.wait_ge(L.o_step, per_tile * TT * b + (per_tile * t + 1))
                    ve.tensor_tensor(on[:, t % 2, :].rearrange("p (h e) -> p h e", h=H),
                                     heads[:, :, 0:HD],
                                     recip[:, :].unsqueeze(2).to_broadcast([P, H, HD]), ALU.mult
                                     ).then_inc(o.drain_sem(name), 1)
                elif kind == "WO":
                    t = int(t)
                    n = per_tile * TT * b + (per_tile * t + 1)
                    dst = xo if L.second else y
                    dve.wait_ge(*o.full(b, name))
                    if t == 0:
                        if L.second:
                            dve.wait_ge(L.res_in, 16 * b + 16)
                        else:
                            dve.wait_ge(L.res_ready, b + 1)
                    if L.second:
                        dve.wait_ge(L.sum_ready, TT * b + (t + 1))
                    ve.tensor_tensor(dst[:, t % 2, :], o.bank(name)[:, 0:D], res_sb[:, t, :],
                                     ALU.add).then_inc(o.drain_sem(name), 1)
                    dve.wait_ge(*o.empty(b, name))
                    moments(L, n, dst[:, t % 2, :], mv[:, t % 2, 1 if L.second else 0, :])
                elif kind == "N1":
                    t = int(t)
                    n = per_tile * TT * b + (per_tile * t + 2)
                    dve.wait_ge(L.rstd_ready, 2 * TT * b + (2 * t + 1))
                    wait(dve, L.x_out[t % 2], 8 * TT * b + 16 * (t // 2))
                    ve.tensor_scalar(xo[:, t % 2, :], y[:, t % 2, :], mv[:, t % 2, 0, 0:1],
                                     rstd[:, t % 2, 0:1], ALU.subtract, ALU.mult
                                     ).then_inc(L.o_step, 1)
                    dve.wait_ge(L.o_step, n + 1)
                    moments(L, n + 1, xo[:, t % 2, :], mv[:, t % 2, 1, :])
                elif kind == "N2":
                    t = int(t)
                    if L.second:
                        dve.wait_ge(L.rstd_ready, TT * b + (t + 1))
                    else:
                        dve.wait_ge(L.rstd_ready, 2 * TT * b + (2 * t + 2))
                    wait(dve, L.h_out[t % 2], 8 * TT * b + 16 * (t // 2))
                    ve.tensor_scalar(hn[:, t % 2, :], xo[:, t % 2, :], mv[:, t % 2, 1, 0:1],
                                     rstd[:, t % 2, 1:2], ALU.subtract, ALU.mult
                                     ).then_inc(L.hn_ready, 1)
                elif kind == "GT":
                    t = int(t)
                    dve.wait_ge(*o.full(b, name))
                    ve.tensor_tensor(logits[:, bass.ds(TT * b + t, 1), :].rearrange("p a e -> p (a e)"),
                                     o.bank(name)[:, 0:E], gate_b_sb[:, :], ALU.add
                                     ).then_inc(o.drain_sem(name), 1)

            def body(L, par, bP, bA, bO):
                for q in range(QUADS):
                    mx = max_tiles(q, par, bP, bA) if L.second else []
                    if L.second:
                        for b, g, s in neg_group(q, par, bP, bA):
                            neg_split(L, b, g)
                    for j in range(HEADS_AT_ONCE):
                        if mx:
                            max_tile(L, *mx[j])
                        outer_tasks(L, (q, j - DVE_LAG[L.number]), bP, bO, par, task)

            for L in layers:
                pipeline(dve, L, body)

            steps = [0]

            def then(op):
                op.then_inc(route_step, 1)
                steps[0] += 1
                dve.wait_ge(route_step, steps[0])

            numbers = route_c[:, P:P + E].unsqueeze(1).to_broadcast([P, NTOK, E])
            over_e = lambda ap: ap.unsqueeze(2).to_broadcast([P, NTOK, E])
            for t in range(TT - 2, TT):
                dve.wait_ge(*layers[1].o_ring.empty(BATCH - 1, f"GT{t}"))
            then(ve.tensor_reduce(top[:, :], logits[:, :, :], axis=AX.X, op=ALU.max))
            then(ve.tensor_tensor(one_hot[:, :, :], logits[:, :, :], over_e(top[:, :]), ALU.is_equal))
            then(ve.tensor_scalar(one_hot[:, :, :], one_hot[:, :, :], -float(E), float(E), ALU.mult,
                                  ALU.add))
            then(ve.tensor_tensor(one_hot[:, :, :], one_hot[:, :, :], numbers, ALU.add))
            then(ve.tensor_reduce(top[:, :], one_hot[:, :, :], axis=AX.X, op=ALU.min))
            then(ve.tensor_tensor(one_hot[:, :, :], numbers, over_e(top[:, :]), ALU.is_equal))
            assert steps[0] == ONE_HOT_STEP
            before = psum[0][:, 0:NTOK * E].rearrange("p (t e) -> p t e", e=E)
            totals = psum[1][:, 0:NTOK * E].rearrange("p (t e) -> p e t", e=E)
            dve.wait_ge(route_sums, 2)
            for e in range(E - 1):
                ve.tensor_tensor_scan(cum[:, e, :], ones_sb[:, 0:NTOK], totals[:, e, :], 0.0,
                                      ALU.mult, ALU.add)
            then(ve.tensor_tensor_scan(cum[:, E - 1, :], ones_sb[:, 0:NTOK], totals[:, E - 1, :], 0.0,
                                       ALU.mult, ALU.add))
            then(ve.tensor_scalar(counts_i[:, :], cum[:, :, NTOK - 1], float(P - 1), None, ALU.add))
            then(ve.tensor_scalar(counts_i[:, :], counts_i[:, :], LOG_P, None,
                                  ALU.logical_shift_right))
            then(ve.tensor_copy(n_tiles[:, :], counts_i[:, :]))
            then(ve.tensor_tensor_scan(tile_end[:, :], ones_sb[:, 0:E], n_tiles[:, :], 0.0,
                                       ALU.mult, ALU.add))
            then(ve.tensor_tensor(row_base[:, :], tile_end[:, :], n_tiles[:, :], ALU.subtract))
            then(ve.tensor_scalar(row_base[:, :], row_base[:, :], float(P), None, ALU.mult))
            then(ve.tensor_tensor(cum[:, :, :], cum[:, :, :], totals, ALU.subtract))
            then(ve.tensor_tensor(slot3[:, :, :], before,
                                  cum[:, :, :].rearrange("p e t -> p t e"), ALU.add))
            then(ve.tensor_tensor(slot3[:, :, :], slot3[:, :, :],
                                  row_base[:, :].unsqueeze(1).to_broadcast([P, NTOK, E]), ALU.add))
            then(ve.tensor_tensor(slot3[:, :, :], slot3[:, :, :], one_hot[:, :, :], ALU.mult))
            then(ve.tensor_reduce(slot_f[:, :], slot3[:, :, :], axis=AX.X, op=ALU.add))
            ve.tensor_copy(slot_u[:, :], slot_f[:, :]).then_inc(slots_ready, 1)
            then(ve.tensor_tensor(past[:, :, :],
                                  tile_end[0:1, :].unsqueeze(1).to_broadcast([1, TILES, E]),
                                  route_c[0:1, P + E:].unsqueeze(2).to_broadcast([1, TILES, E]),
                                  ALU.is_le))
            then(ve.tensor_reduce(tile_e_f[:, :], past[:, :, :], axis=AX.X, op=ALU.add))
            ve.tensor_scalar(tile_expert[:, :], tile_e_f[:, :], float(E - 1), None, ALU.min
                             ).then_inc(slots_ready, 1)

            def tile_in(j, s):
                dve.wait_ge(xs_T, j + 1)
                ve.tensor_copy(xsT[:, s, :, :].rearrange("p k t -> p (k t)"), psum[4][:, 0:D]
                               ).then_inc(xsT_ready, 1)

            def hidden(j, s):
                for n in range(2):
                    dve.wait_ge(hid_T, 2 * j + (n + 1))
                    if n == 0:
                        wait(dve, down_done, j - 1)
                    half = hidT[:, s, n * KF // 2:(n + 1) * KF // 2, :]
                    ve.tensor_copy(half.rearrange("p k t -> p (k t)"), psum[2 + n][:, :]
                                   ).then_inc(hidT_ready, 1)

            def tile_out(j, s):
                dve.wait_ge(down_done, j + 1)
                wait(dve, ys_out[s], 8 * (j - s))
                ve.tensor_copy(ys_sb[:, s, :], psum[5][:, 0:D]).then_inc(ys_ready, 1)

            def expert_body(j, s, ends=False):
                hidden(j - 1, 1 - s)
                if not ends:
                    tile_in(j + 1, 1 - s)
                tile_out(j - 1, 1 - s)

            tile_in(0, 0)
            tile_in(1, 1)
            expert_body(1, 1)
            expert_body(2, 0)
            with dve.Fori(1, TILES // 2 - 1) as pair:
                expert_body(2 * pair + 1, 1)
                expert_body(2 * pair + 2, 0)
            expert_body(TILES - 2, 1)
            expert_body(TILES - 1, 0, ends=True)
            hidden(TILES - 1, 0)
            tile_out(TILES - 1, 0)

            def finish(b, s):
                dve.wait_ge(sum_in[s], 8 * (b - s) + 16)
                dve.wait_ge(gathered[s], 8 * TT * (b - s) + 16 * TT)
                ve.tensor_tensor(sum_ring[:, s, :, :], sum_ring[:, s, :, :], stage[:, s, :, :], ALU.add
                                 ).then_inc(sum_done, 1)
                dve.wait_ge(sum_done, b + 1)
                for t in range(TT):
                    last = ve.bn_stats(stats4[:, t, :], sum_ring[:, s, t, :])
                last.then_inc(last_stats, 1)
                dve.wait_ge(last_stats, b + 1)
                ve.memset(wait_cell[:, :], 0.0)
                for t in range(TT):
                    last = ve.bn_aggr(mv4[:, s, t, :], stats4[:, t, :])
                last.then_inc(last_mv, 1)

            def scale_out(b, s):
                dve.wait_ge(last_rstd, b + 1)
                wait(dve, out_done[s], 8 * (b - s))
                for t in range(TT):
                    last = ve.tensor_scalar(out_ring[:, s, t, :], sum_ring[:, s, t, :],
                                            mv4[:, s, t, 0:1], rstd4[:, s, t:t + 1],
                                            ALU.subtract, ALU.mult)
                last.then_inc(out_ready, 1)

            finish(0, 0)
            finish(1, 1)
            scale_out(0, 0)
            with dve.Fori(1, BATCH // 2) as pair:
                finish(2 * pair, 0)
                scale_out(2 * pair - 1, 1)
                finish(2 * pair + 1, 1)
                scale_out(2 * pair, 0)
            scale_out(BATCH - 1, 1)

        @block.gpsimd
        def _(pool):
            pool.memset(xo[:, :, :], 0.0).then_inc(layers[-1].sum_ready, 2)
            pool.memset(zeros_sb[:, :, :], 0.0).then_inc(zeros_set, 1)
            pool.wait_ge(zeros_set, 1)
            pool.memset(v_aug[:, :, :, :, HD:VW], 0.0).then_inc(pool_set, 1)
            pool.wait_ge(pool_set, 1)
            pool.memset(v_aug[:, :, :, :, HD:HD + 1], 1.0).then_inc(pool_set, 1)
            pool.wait_ge(pool_set, 2)
            pool.memset(k_stack[STACK:STACK + NEG, :, :, :], 1.0).then_inc(pool_set, 1)
            pool.wait_ge(pool_set, 3)
            pool.wait_ge(consts_in, 16 * N_CONST_DMAS)

            def task(L, name, b, s):
                kind, t = name[:2], name[-1]
                p = L.p_ring
                if name in ("qB", "kB") and not L.second:
                    qk = "qk".index(name[0])
                    all_empty(pool, p, b, PARTS_OF[qk])
                    wait(pool, L.parts_ready, 2 * b + (qk - 1))
                    pool.tensor_tensor(rest[:, qk, 0, :], trig[:, 0, :], trig[:, 2, :],
                                       ALU.subtract)
                    pool.tensor_tensor(rest[:, qk, 1, :], trig[:, 1, :], trig[:, 3, :], ALU.add
                                       ).then_inc(L.rot_done, 1)
                elif kind[0] in "ml":
                    qk = "qk".index(name[1])
                    pool.wait_ge(L.mid_done, 2 * b + (qk + 1))
                    pool.tensor_tensor(parts[:, qk, 2, :, :], rest[:, qk, :, :],
                                       parts[:, qk, 1, :, :], ALU.subtract
                                       ).then_inc(L.parts_ready, 1)
                elif name == "TO0" and not L.second:
                    pool.wait_ge(L.res_in, 16 * b + 16)
                    pool.tensor_tensor(res_sb[:, :, :], res_sb[:, :, :],
                                       rows_sb[:, 0:1, :].to_broadcast([P, TT, D]), ALU.add
                                       ).then_inc(L.res_ready, 1)
                elif kind == "WO" and L.second:
                    t = int(t)
                    pool.wait_ge(*L.o_ring.empty(b, name))
                    pool.tensor_tensor(res_sb[:, t, :], res_sb[:, t, :], xo[:, t % 2, :], ALU.add
                                       ).then_inc(L.sum_ready, 1)
                elif kind == "N2":
                    t = int(t)
                    r = 3 if L.second else 1
                    pool.wait_ge(L.hn_ready, TT * b + (t + 1))
                    pool.tensor_tensor(hn[:, t % 2, :], hn[:, t % 2, :], rows_sb[:, r, :], ALU.mult
                                       ).then_inc(L.hw_step, 1)
                    pool.wait_ge(L.hw_step, TT * b + (t + 1))
                    pool.tensor_tensor(hn[:, t % 2, :], hn[:, t % 2, :], rows_sb[:, r + 1, :],
                                       ALU.add).then_inc(L.h_ready, 1)

            def body(L, par, bP, bA, bO):
                for slot in SLOTS:
                    outer_tasks(L, slot, bP, bO, par, task)

            for L in layers:
                pipeline(pool, L, body)

            pool.wait_ge(slots_ready, 1)
            pool.wait_ge(zeros_in, 16 * (TILES // 3))
            for b in range(BATCH):
                s = b % 2
                pool.wait_ge(stage_in[s], 8 * (b - s) + 16)
                for t in range(TT):
                    pool.indirect_dma_start(
                        xs_dram, bass.IndirectOffsetOnAxis(slot_u[:, TT * b + t:TT * b + t + 1], 0),
                        stage[:, s, t, :], None).then_inc(dispatched[s], 16)
            for s in range(2):
                pool.wait_ge(ys_out[s], 16 * ((TILES + 1 - s) // 2))
            for b in range(BATCH):
                s = b % 2
                if b >= 2:
                    pool.wait_ge(sum_done, b - 1)
                for t in range(TT):
                    pool.indirect_dma_start(
                        stage[:, s, t, :], None, ys_dram,
                        bass.IndirectOffsetOnAxis(slot_u[:, TT * b + t:TT * b + t + 1], 0)
                        ).then_inc(gathered[s], 16)

        @block.sync
        def _(sp):
            n = 0
            for dst, src in (
                    (ident_sb[:, :], ident), (head_sum_sb[:, :], head_sum),
                    (cos_sb[:, :], cos_t), (sin_sb[:, :], sin_t),
                    (wqkv_sb[:, 0, 0, :], w_qkv1[0:P, :]), (wqkv_sb[:, 0, 1, :], w_qkv1[P:D, :]),
                    (wqkv_sb[:, 1, 0, :], w_qkv2[0:P, :]), (wqkv_sb[:, 1, 1, :], w_qkv2[P:D, :]),
                    (wo_sb[:, 0, :, :], w_o1.rearrange("(k p) n -> p k n", p=P)),
                    (wo_sb[:, 1, :, :], w_o2.rearrange("(k p) n -> p k n", p=P)),
                    (rows_sb[:, 0, :], b_o.partition_broadcast(P)),
                    (rows_sb[:, 1, :], ln1_w.partition_broadcast(P)),
                    (rows_sb[:, 2, :], ln1_b.partition_broadcast(P)),
                    (rows_sb[:, 3, :], ln2_w.partition_broadcast(P)),
                    (rows_sb[:, 4, :], ln2_b.partition_broadcast(P)),
                    (gate_w_sb[:, 0, :], gate_w[0:P, :]), (gate_w_sb[:, 1, :], gate_w[P:D, :]),
                    (gate_b_sb[:, :], gate_b.partition_broadcast(P)),
                    (route_c[:, :], route_consts)):
                sp.dma_start(dst, src).then_inc(consts_in, 16)
                n += 1
            assert n == N_CONST_DMAS
            sp.wait_ge(zeros_set, 1)
            for n in range(TILES // 3):
                sp.dma_start(xs_dram[3 * P * n:3 * P * (n + 1), :].rearrange(
                    "(a p) d -> p a d", p=P), zeros_sb[:, :, :].to_broadcast([P, 3, D])
                    ).then_inc(zeros_in, 16)

            def task(L, name, b, s):
                kind, t = name[:2], name[-1]
                if kind[0] in "ml":
                    qk = "qk".index(name[1])
                    stack, slots = ((q_stack, Q_SLOTS), (k_stack, K_SLOTS))[qk]
                    sp.wait_ge(L.parts_ready, 2 * b + (qk + 1))
                    if not isinstance(b, int) or b >= 2:
                        sp.wait_ge(L.scores, CHUNKS * b - CHUNKS)
                    for slot, part in enumerate(slots):
                        for half in range(2):
                            at = HD * slot + HALF * half
                            sp.dma_start(stack[at:at + HALF, s, :, :], parts[:, qk, part, half, :]
                                         ).then_inc(L.stack_in[qk], 16)
                elif kind == "N1":
                    t = int(t)
                    sp.wait_ge(L.mv_ready, 2 * TT * b + (2 * t + 2))
                    sp.dma_start(tile_of(x1_dram, b, t), xo[:, t % 2, :]
                                 ).then_inc(L.x_out[t % 2], 16)
                elif name == f"HT{TT - 1}":
                    sp.wait_ge(L.sum_ready, TT * b + (TT + 2))
                    sp.dma_start(tiles(sum_dram, b), res_sb[:, :, :]).then_inc(L.x_out[0], 16)
                elif kind == "N2":
                    t = int(t)
                    sp.wait_ge(L.h_ready, TT * b + (t + 1))
                    sp.dma_start(tile_of(h2_dram if L.second else h1_dram, b, t), hn[:, t % 2, :]
                                 ).then_inc(L.h_out[t % 2], 16)

            def neg_rows(L, b, g, s):
                sp.wait_ge(*L.mx_ring.empty(b, ("NG", g)))
                sp.dma_start(q_stack[STACK:STACK + NEG, s, HEADS_AT_ONCE * g:HEADS_AT_ONCE * (g + 1), :],
                             neg_T[:, :]).then_inc(L.neg_in, 16)

            def body(L, par, bP, bA, bO):
                for q in range(QUADS):
                    if L.second:
                        for b, g, s in neg_group(q, par, bP, bA):
                            neg_rows(L, b, g, s)
                    for j in (0, 2):
                        outer_tasks(L, (q, j), bP, bO, par, task)

            for L in layers:
                pipeline(sp, L, body)
                if L.second:
                    sp.wait_ge(L.x_out[0], 16 * BATCH)
                else:
                    for stored in L.x_out:
                        sp.wait_ge(stored, 8 * TT * BATCH)
                for stored in L.h_out:
                    sp.wait_ge(stored, 8 * TT * BATCH)
            B = layers[1]

            sp.wait_ge(B.scores, CHUNKS * BATCH)
            for e in range(E):
                sp.dma_start(w1_sb[:, e, :, :], w1[e].rearrange("(k p) f -> p k f", p=P)
                             ).then_inc(weights_in[0], 16)
            sp.wait_ge(slots_ready, 2)
            for b in range(BATCH):
                s = b % 2
                if b >= 2:
                    sp.wait_ge(dispatched[s], 8 * TT * (b - s))
                sp.dma_start(stage[:, s, :, :], tiles(h2_dram, b)).then_inc(stage_in[s], 16)
            for e in range(E):
                sp.dma_start(w2_sb[:, e, :, :], w2[e].rearrange("(k p) d -> p k d", p=P)
                             ).then_inc(weights_in[1], 16)
            for s in range(2):
                sp.wait_ge(dispatched[s], 8 * TT * BATCH)

            def load_tile(j, s):
                wait(sp, xs_T, j - 1)
                sp.dma_start(xs_sb[:, s, :],
                             xs_dram[bass.ds(P * j, P), :]).then_inc(xs_in[s], 16)

            def store_tile(j, s):
                sp.wait_ge(ys_ready, j + 1)
                sp.dma_start(ys_dram[bass.ds(P * j, P), :], ys_sb[:, s, :]).then_inc(ys_out[s], 16)

            load_tile(0, 0)
            load_tile(1, 1)
            with sp.Fori(1, TILES // 2) as pair:
                load_tile(2 * pair, 0)
                store_tile(2 * pair - 2, 0)
                load_tile(2 * pair + 1, 1)
                store_tile(2 * pair - 1, 1)
            load_tile(TILES - 1, 0)
            store_tile(TILES - 3, 0)
            store_tile(TILES - 2, 1)
            store_tile(TILES - 1, 0)

            def load_stream(b, s):
                wait(sp, out_ready, b - 1)
                sp.dma_start(sum_ring[:, s, :, :], tiles(sum_dram, b)).then_inc(sum_in[s], 16)

            def store_out(b, s):
                sp.wait_ge(out_ready, b + 1)
                sp.dma_start(tiles(out, b), out_ring[:, s, :, :]).then_inc(out_done[s], 16)

            sp.wait_ge(down_done, TILES)
            load_stream(0, 0)
            load_stream(1, 1)
            with sp.Fori(1, BATCH // 2) as pair:
                store_out(2 * pair - 2, 0)
                load_stream(2 * pair, 0)
                store_out(2 * pair - 1, 1)
                load_stream(2 * pair + 1, 1)
            store_out(BATCH - 2, 0)
            store_out(BATCH - 1, 1)
            for s in range(2):
                sp.wait_ge(out_done[s], 8 * BATCH)


def lay_out(**inputs):
    a = {k.removeprefix("L0_"): np.asarray(v) for k, v in inputs.items()}
    def columns(w):
        qk = w[:, :2 * D].reshape(D, 2, H, 2, HALF).transpose(0, 1, 3, 4, 2).reshape(D, 2 * D)
        return np.ascontiguousarray(np.concatenate([qk, w[:, 2 * D:]], axis=1))
    inv_freq = (1.0 / np.float32(10000.0) ** (np.arange(HALF, dtype=np.float32) / np.float32(HALF)))
    angles = (np.arange(T, dtype=np.float32)[None, :] * inv_freq.astype(np.float32)[:, None])
    table = lambda f: np.repeat(f(angles).astype(np.float32), H, axis=0)
    of_head = np.arange(P) % H
    return {
        "x": a["attn_x"], "w_qkv1": columns(a["attn_Wqkv"]), "w_o1": a["attn_Wo"],
        "b_o": a["attn_bo"], "ln1_w": a["ffn_ln1_w"], "ln1_b": a["ffn_ln1_b"],
        "w_qkv2": columns(a["ffn_w_qkv"]), "w_o2": a["ffn_w_proj"], "ln2_w": a["ffn_ln2_w"],
        "ln2_b": a["ffn_ln2_b"], "gate_w": a["ffn_gate_w"], "gate_b": a["ffn_gate_b"],
        "w1": a["ffn_w1"], "w2": a["ffn_w2"], "cos_t": table(np.cos), "sin_t": table(np.sin),
        "head_sum": (of_head[:, None] == of_head[None, :]).astype(np.float32),
        "ident": np.eye(P, dtype=np.float32),
        "route_consts": np.concatenate([
            np.triu(np.ones((P, P)), 1), np.tile(np.arange(E), (P, 1)),
            np.tile(np.arange(TILES), (P, 1))], axis=1).astype(np.float32),
    }


def kernel(**inputs):
    import concourse.bacc as bacc
    from concourse.bass_utils import run_bass_kernel_spmd

    nc = bacc.Bacc("TRN2", target_bir_lowering=False, num_devices=1)
    arrays, args = {}, {}
    for name, a in lay_out(**inputs).items():
        a = np.ascontiguousarray(a)
        arrays[f"in_{name}_dram"] = a
        args[name] = nc.dram_tensor(f"in_{name}_dram", a.shape, mybir.dt.from_np(a.dtype),
                                    kind="ExternalInput").ap()
    args["out"] = nc.dram_tensor("out_0_dram", (BATCH, T, D), FP32, kind="ExternalOutput").ap()
    program(nc, **args)
    return run_bass_kernel_spmd(nc, [arrays], core_ids=[0]).results[0]["out_0_dram"]
```

```python
from contextlib import ExitStack

import numpy as np

import concourse.bass as bass
from concourse import mybir

FP32 = mybir.dt.float32
BF16 = mybir.dt.bfloat16
I32 = mybir.dt.int32
U32 = mybir.dt.uint32
ALU = mybir.AluOpType
ACT = mybir.ActivationFunctionType
AX = mybir.AxisListType

BATCH, T, D, H = 8, 512, 256, 16
HD = D // H
P = 128
TT = T // P
KD = D // P
HALF = HD // 2
E = 8
HEADS_AT_ONCE = 4
GROUPS = H // HEADS_AT_ONCE
QUADS = GROUPS * TT
CHUNKS = QUADS * HEADS_AT_ONCE
VW = 32
Q_SLOTS = (0, 1, 2, 0, 1, 0)
K_SLOTS = (0, 0, 0, 1, 1, 2)
STACK = HD * len(Q_SLOTS)
NEG = 3
STACK_DMAS = 2 * len(Q_SLOTS)
F = 4 * D
KF = F // P
TILES = BATCH * T // P + E - 1
LOG_P = P.bit_length() - 1
ONE_HOT_STEP = 6
EPS = 1e-5
SCALE = 1.0 / HD ** 0.5


class Ring:

    def __init__(self, name, banks, order, sem, first, before):
        self.banks, self.order, self.first = banks, order, first
        assert len(order) % len(banks) == 0
        self.base = before.base + len(before.order) * (first - before.first) if before else 0
        self.filled = sem(f"{name}_filled")
        self.drained = [sem(f"{name}_drained{i}") for i in range(len(banks))]

    def _k(self, use):
        return self.order.index(use)

    def bank(self, use):
        return self.banks[self._k(use) % len(self.banks)]

    def drain_sem(self, use):
        return self.drained[self._k(use) % len(self.banks)]

    def free(self, b, use):
        k, n = self._k(use), len(self.banks)
        return self.drain_sem(use), (b - self.first) * (len(self.order) // n) + (
            self.base // n + k // n)

    def full(self, b, use):
        return self.filled, (b - self.first) * len(self.order) + (self.base + self._k(use) + 1)

    def empty(self, b, use):
        s, v = self.free(b, use)
        return s, v + 1


def all_empty(eng, ring, b, uses):
    for use in uses[-len(ring.banks):]:
        eng.wait_ge(*ring.empty(b, use))


def wait(eng, sem, value):
    if not (isinstance(value, int) and value <= 0):
        eng.wait_ge(sem, value)


class Layer:

    def __init__(self, number, sem, psum, before=None):
        self.number, self.second = number, number == 1
        self.first = number * BATCH
        self.rows = STACK + (NEG if self.second else 0)
        self.p_tasks, self.o_tasks = {}, {}
        if not self.second:
            p_steps = ((1, 2, "T0"), (2, 0, "T1"), (2, 2, "qA"), (3, 2, "qB"), (4, 2, "kA"),
                       (5, 2, "sq"), (5, 2, "kB"), (6, 2, "nq"), (7, 0, "uq"), (7, 2, "hq"),
                       (7, 2, "sk"), (8, 2, "nk"), (8, 2, "lq"), (9, 0, "uk"), (9, 2, "hk"),
                       (10, 0, "lk"), (10, 2, "V0"), (12, 2, "V1"))
            o_at = lambda t: (("TO", 4 + 6 * t), ("TP", 6 + 6 * t), ("WO", 8 + 6 * t),
                              ("N1", 10 + 6 * t), ("N2", 12 + 6 * t))
            p_bank, o_bank, st_banks, pv_bank, mx_banks = 4, 5, [0, 1, 2], 6, []
        else:
            p_steps = ((1, 0, "T0"), (1, 2, "T1"), (2, 2, "qA"), (3, 2, "qB"), (4, 0, "mq"),
                       (4, 2, "kA"), (5, 2, "kB"), (6, 0, "mk"), (7, 2, "V0"), (9, 2, "V1"))
            o_at = lambda t: (("TO", 3 + 5 * t), ("TP", 5 + 5 * t), ("WO", 7 + 5 * t),
                              ("N2", 9 + 5 * t), ("HT", 11 + 5 * t), ("GT", 14 + 5 * t))
            p_bank, o_bank, st_banks, pv_bank, mx_banks = 4, 5, [0, 1, 2], 6, [3, 7]
        for q, j, step in p_steps:
            self.p_tasks.setdefault((q, j), []).append(step)
        for t in range(TT):
            for step, at in o_at(t):
                self.o_tasks.setdefault(SLOTS[at], []).append(f"{step}{t}")
        if self.second:
            self.o_tasks.setdefault(SLOTS[-1], []).append("RT")
        in_psum = lambda tasks: [x for slot in SLOTS for x in tasks.get(slot, [])
                                 if x[0] not in "Nmsuhl"]
        banks = lambda ids: [psum[i] for i in ids]
        ring = lambda n, ids, order, last: Ring(n, banks(ids), order, sem, self.first, last)
        self.p_ring = ring("proj", [p_bank], in_psum(self.p_tasks), before and before.p_ring)
        self.o_ring = ring("out", [o_bank], in_psum(self.o_tasks), before and before.o_ring)
        self.st_banks, self.pv_banks = banks(st_banks), banks([pv_bank])
        s = sem
        if self.second:
            order = []
            for g in range(GROUPS):
                order += [("MX", g, c) for c in range(HEADS_AT_ONCE * TT)] + [("NG", g)]
            self.mx_ring = ring("max", mx_banks, order, None)
            self.neg_step = s("neg_step")
            self.neg_ready = s("neg_ready")
            self.neg_in = s("neg_in")
        self.x_in = s("x_in")
        self.res_in = s("res_in")
        self.res_ready = s("res_ready")
        self.sq_done = s("sq_done")
        self.rot_done = s("rot_done")
        self.rs_ready = s("rs_ready")
        self.high_done = s("high_done")
        self.mid_done = s("mid_done")
        self.p_step = s("p_step")
        self.parts_ready = s("parts_ready")
        self.stack_in = [s("q_in"), s("k_in")]
        self.scores = s("scores")
        self.exps = s("exps")
        self.pv_done = s("pv_done")
        self.oT_ready = s("oT_ready")
        self.sum_ready = s("sum_ready")
        self.o_step = s("o_step")
        self.mv_ready = s("mv_ready")
        self.rstd_step = s("rstd_step")
        self.rstd_ready = s("rstd_ready")
        self.hn_ready = s("hn_ready")
        self.hw_step = s("hw_step")
        self.h_ready = s("h_ready")
        self.x_out = [s("x_out0"), s("x_out1")]
        self.h_out = [s("h_out0"), s("h_out1")]


SLOTS = [(q, j) for q in range(QUADS) for j in (0, 2)]
ROOM = BATCH * T + P
ROW = 2 * D + 1
ROUTE_STEPS = 10
SPLIT_STEPS = 7
MAX_LEAD = 6
ACT_LAG, DVE_LAG = (1, 0), (1, 0)
PV_AFTER = 1
O_STEPS = (4, 2)


def program(nc, x, w_qkv1, w_o1, b_o, ln1_w, ln1_b, w_qkv2, w_o2, ln2_w, ln2_b, gate_w, gate_b,
            w1, w2, cos_t, sin_t, head_sum, ident, route_consts, out):
    ctx = ExitStack()
    with ctx:
        def sb(name, shape, dt=FP32):
            return ctx.enter_context(nc.sbuf_tensor(name, shape, dt))

        sems = {}

        def sem(name):
            if name not in sems:
                sems[name] = ctx.enter_context(nc.semaphore(name))
            return sems[name]

        def dram(name, shape, dt=FP32):
            return nc.dram_tensor(name, shape, dt).ap()

        x1_dram = dram("x1_dram", [BATCH, T, D])
        h1_dram = dram("h1_dram", [BATCH, T, D])
        rows_dram = dram("rows_dram", [(E + 1) * ROOM, ROW])
        out_rows = dram("out_rows", [BATCH * T + P, D])

        psum = [ctx.enter_context(nc.psum_tensor(f"bank{i}", [P, T], FP32)) for i in range(8)]
        ident_sb = sb("ident_sb", [P, P])
        ident_bf = sb("ident_bf", [P, P], BF16)
        head_sum_sb = sb("head_sum_sb", [P, P])
        cos_sb = sb("cos_sb", [P, T])
        sin_sb = sb("sin_sb", [P, T])
        wqkv_sb = sb("wqkv_sb", [P, 2, KD, 3 * D])
        wo_sb = sb("wo_sb", [P, 2, KD, D])
        rows_sb = sb("rows_sb", [P, 5, D])
        gate_w_sb = sb("gate_w_sb", [P, KD, E])
        gate_b_sb = sb("gate_b_sb", [P, E])
        eps_sb = sb("eps_sb", [P, 2])
        logits = sb("logits", [P, TT, E])

        def carve(space, pieces):
            at, got = 0, []
            for dims, shape, dt in pieces:
                n = int(np.prod(list(shape.values()))) * (1 if dt == FP32 else 2) // (
                    1 if dt == FP32 else 4)
                piece = space[:, at:at + n]
                if dt != FP32:
                    piece = piece.bitcast(dt)
                got.append(piece.rearrange(f"p ({dims}) -> p {dims}", **shape))
                at += n
            assert at <= space.shape[1], (at, space.shape)
            return got

        w1_space = sb("w1_space", [P, E * KD * F])
        w2_space = sb("w2_space", [P, E * KF * D])
        work_space = sb("work_space", [P, 7680])
        q_stack, k_stack = carve(w1_space, [("s h t", dict(s=2, h=H, t=T), BF16)] * 2)
        v_aug, probs, oT, trig, rest = carve(w2_space, [
            ("s t h e", dict(s=2, t=TT, h=H, e=VW), FP32),
            ("s j t", dict(s=2, j=HEADS_AT_ONCE, t=T), FP32),
            ("s g t", dict(s=2, g=GROUPS, t=T), FP32),
            ("n t", dict(n=4, t=T), FP32),
            ("a c t", dict(a=2, c=2, t=T), FP32)])
        x_sb, res_sb, xT, sq, rs, parts = carve(work_space, [
            ("t d", dict(t=TT, d=D), FP32), ("t d", dict(t=TT, d=D), FP32),
            ("k t", dict(k=KD, t=T), FP32), ("c t", dict(c=2, t=T), FP32),
            ("a t", dict(a=1, t=T), FP32),
            ("a n c t", dict(a=2, n=3, c=2, t=T), BF16)])
        rs = rs[:, 0, :]
        (w1_sb,) = carve(w1_space, [("e k f", dict(e=E, k=KD, f=F), FP32)])
        (w2_sb,) = carve(w2_space, [("e k d", dict(e=E, k=KF, d=D), FP32)])
        xs_sb, xsT, hid, hidT, rest_sb, z_sb, o_sb = carve(work_space, [
            ("s d", dict(s=2, d=D), FP32), ("s k t", dict(s=2, k=KD, t=P), FP32),
            ("s f", dict(s=2, f=F), FP32), ("s k t", dict(s=2, k=KF, t=P), FP32),
            ("s d", dict(s=2, d=ROW - D), FP32), ("s d", dict(s=2, d=D), FP32),
            ("s d", dict(s=2, d=D), FP32)])
        pad_row = work_space[:, 0:ROW]

        route_c = sb("route_c", [P, P + E + (E + 1) + TILES + TT + 1])
        at = np.cumsum([P, E, E + 1, TILES, TT, 1])
        rank_c, room_c, tile_c, tok_c, pad_c = (
            route_c[:, lo:hi] for lo, hi in zip(at[:-1].tolist(), at[1:].tolist()))
        ones_sb = sb("ones_sb", [P, P])
        top = sb("top", [P, TT])
        one_hot = sb("one_hot", [P, TT, E])
        slot3 = sb("slot3", [P, TT, E])
        next_row = sb("next_row", [P, E + 1])
        token = sb("token", [P, TT])
        slot_f = sb("slot_f", [P, TT])
        slot_u = sb("slot_u", [P, TT], U32)
        pad_u = sb("pad_u", [P, E + 1], U32)
        counts_i = sb("counts_i", [1, E], I32)
        n_tiles = sb("n_tiles", [1, E])
        tile_end = sb("tile_end", [1, E])
        past = sb("past", [1, TILES, E])
        tile_e_f = sb("tile_e_f", [1, TILES])
        tile_at = sb("tile_at", [1, TILES])
        tile_used = sb("tile_used", [1, TILES])
        tile_expert = sb("tile_expert", [1, TILES], I32)
        tile_row = sb("tile_row", [1, TILES], I32)
        row_sb = sb("row_sb", [P, TT, ROW])
        hn = row_sb[:, :, 0:D]

        weights_in = [sem("w1_in"), sem("w2_in")]
        route_step = sem("route_step")
        one_hot_ready = sem("one_hot_ready")
        slots_ready = sem("slots_ready")
        dispatched = sem("dispatched")
        pad_set = sem("pad_set")
        tiles_ready = sem("tiles_ready")
        padded = sem("padded")
        xs_in = [sem("xs_in0"), sem("xs_in1")]
        rest_in = [sem("rest_in0"), sem("rest_in1")]
        xs_T = sem("xs_T")
        xsT_ready = sem("xsT_ready")
        up_done = sem("up_done")
        gelu_done = sem("gelu_done")
        hid_T = sem("hid_T")
        hidT_ready = sem("hidT_ready")
        down_done = sem("down_done")
        sum_done = sem("sum_done")
        last_stats = sem("last_stats")
        last_mv = sem("last_mv")
        last_ln = sem("last_ln")
        last_rstd = sem("last_rstd")
        out_ready = sem("out_ready")
        out_stored = [sem("out_stored0"), sem("out_stored1")]
        out_done = sem("out_done")
        recip = sb("recip", [P, H])
        on = sb("on", [P, 2, D])
        onT = sb("onT", [P, 2, KD, P])
        y = sb("y", [P, 2, D])
        xo = sb("xo", [P, 2, D])
        stats = sb("stats", [P, 6])
        wait_cell = sb("wait_cell", [P, 1])
        mv = sb("mv", [P, 2, 2, 2])
        rstd = sb("rstd", [P, 2, 2])
        negm = sb("negm", [P, TT, HEADS_AT_ONCE])
        neg_rest = sb("neg_rest", [P, TT, HEADS_AT_ONCE])
        neg_parts = sb("neg_parts", [P, TT, NEG, HEADS_AT_ONCE], BF16)
        neg_T = sb("neg_T", [NEG * HEADS_AT_ONCE, T], BF16)

        consts_in = sem("consts_in")
        consts_set = sem("consts_set")
        pool_set = sem("pool_set")
        pool_cell = sb("pool_cell", [P, 1])
        layer_a = Layer(0, sem, psum)
        layer_b = Layer(1, sem, psum, layer_a)
        N_CONST_DMAS, N_CONST_OPS = 19, 4
        PARTS_OF = (("qA", "qB"), ("kA", "kB"))

        def tiles(ap, b):
            return ap[bass.ds(b, 1), :, :].rearrange("a (t p) d -> p (a t) d", p=P)

        def tile_of(ap, b, t):
            return ap[bass.ds(b, 1), t * P:(t + 1) * P, :].rearrange("a p d -> (a p) d")

        def pipeline(eng, body):
            def of(L):
                return lambda b: (L, b)

            a, b = of(layer_a), of(layer_b)
            body(0, a(0), None, None)
            body(1, a(1), a(0), None)
            with eng.Fori(1, BATCH // 2) as pair:
                body(0, a(2 * pair), a(2 * pair - 1), a(2 * pair - 2))
                body(1, a(2 * pair + 1), a(2 * pair), a(2 * pair - 1))
            n = BATCH
            body(0, b(n), a(n - 1), a(n - 2))
            body(1, b(n + 1), b(n), a(n - 1))
            with eng.Fori(1, BATCH // 2) as pair:
                body(0, b(2 * pair + n), b(2 * pair + (n - 1)), b(2 * pair + (n - 2)))
                body(1, b(2 * pair + (n + 1)), b(2 * pair + n), b(2 * pair + (n - 1)))
            body(0, None, b(2 * n - 1), b(2 * n - 2))
            body(1, None, None, b(2 * n - 1))

        def outer_tasks(slot, par, projected, finished, task):
            if finished:
                L, b = finished
                for name in L.o_tasks.get(slot, []):
                    task(L, name, b, par)
            if projected:
                L, b = projected
                for name in L.p_tasks.get(slot, []):
                    task(L, name, b, par)

        def max_tiles(q, par, projected, attended):
            at = q - (QUADS - MAX_LEAD)
            of, at, s = (projected, at, par) if at >= 0 else (attended, at + QUADS, 1 - par)
            return [] if not of or not of[0].second else [
                (*of, at // TT, HEADS_AT_ONCE * (at % TT) + j, s) for j in range(HEADS_AT_ONCE)]

        def neg_group(q, par, projected, attended):
            at = q - (QUADS - MAX_LEAD)
            of, at, s = (projected, at, par) if at > 0 else (attended, at + QUADS, 1 - par)
            return [] if not of or not of[0].second or at % TT else [(*of, at // TT - 1, s)]

        def norms(L, b):
            return (2 - L.number) * TT * (b - L.first) + 2 * TT * L.first

        def o_steps(L, b):
            return O_STEPS[L.number] * TT * (b - L.first) + O_STEPS[0] * TT * L.first

        def half_of(name):
            return "qk".index(name[0]), "AB".index(name[1])

        def v_out(eng, ops, L, name, b, s):
            j, p = int(name[1]), L.p_ring
            eng.wait_ge(*p.full(b, name))
            if not isinstance(b, int) or b >= 2:
                eng.wait_ge(L.pv_done, QUADS * (b - 2) + QUADS)
            dst = v_aug[:, s, 2 * j:2 * j + 2, :, 0:HD]
            src = p.bank(name)[:, :].rearrange("p (t h e) -> p t h e", t=2, h=H)
            if ops is nc.scalar:
                last = nc.scalar.activation(dst, src, ACT.Copy)
            else:
                last = nc.vector.tensor_copy(dst, src)
            last.then_inc(p.drain_sem(name), 1)

        block = ctx.enter_context(nc.Block())

        @block.tensor
        def _(pe):
            pe.wait_ge(consts_in, 16 * N_CONST_DMAS)
            pe.wait_ge(consts_set, N_CONST_OPS)
            pe.wait_ge(pool_set, 3)

            def score(L, b, s, c):
                q, j = c // HEADS_AT_ONCE, c % HEADS_AT_ONCE
                g, kt = q // TT, q % TT
                h, n = HEADS_AT_ONCE * g + j, len(L.st_banks)
                if c == 0:
                    for arrived in L.stack_in:
                        pe.wait_ge(arrived, 16 * STACK_DMAS * b + 16 * STACK_DMAS)
                if L.second and j == 0 and kt == 0:
                    pe.wait_ge(L.neg_in, 16 * GROUPS * (b - L.first) + 16 * (g + 1))
                wait(pe, L.exps, CHUNKS * b + (c + 1 - n if CHUNKS % n == 0 or c else 0))
                nc.tensor.matmul(L.st_banks[c % n][:, :],
                                 k_stack[0:L.rows, s, h, kt * P:(kt + 1) * P],
                                 q_stack[0:L.rows, s, h, :], start=True, stop=True
                                 ).then_inc(L.scores, 1)

            def pv(L, b, s, q):
                g, kt, n = q // TT, q % TT, len(L.pv_banks)
                pe.wait_ge(L.exps, CHUNKS * b + HEADS_AT_ONCE * (q + 1))
                if q == 0:
                    all_empty(pe, L.p_ring, b, ("V0", "V1"))
                if kt == 0:
                    wait(pe, L.oT_ready, GROUPS * b + (g + 1 - n))
                for j in range(HEADS_AT_ONCE):
                    last = nc.tensor.matmul(L.pv_banks[g % n][VW * j:VW * (j + 1), :],
                                            v_aug[:, s, kt, HEADS_AT_ONCE * g + j, :],
                                            probs[:, q % 2, j, :],
                                            start=(kt == 0), stop=(kt == TT - 1))
                last.then_inc(L.pv_done, 1)

            def max_score(L, b, g, c, s):
                use, h, qt = ("MX", g, c), HEADS_AT_ONCE * g + c // TT, c % TT
                if g == 0 and c == 0:
                    for arrived in L.stack_in:
                        pe.wait_ge(arrived, 16 * STACK_DMAS * b + 16 * STACK_DMAS)
                wait(pe, *L.mx_ring.free(b, use))
                nc.tensor.matmul(L.mx_ring.bank(use)[:, :],
                                 q_stack[0:STACK, s, h, qt * P:(qt + 1) * P],
                                 k_stack[0:STACK, s, h, :], start=True, stop=True
                                 ).then_inc(L.mx_ring.filled, 1)

            def neg_rows(L, b, g):
                pe.wait_ge(L.neg_ready, GROUPS * (b - L.first) + (g + 1))
                wait(pe, *L.mx_ring.free(b, ("NG", g)))
                rows = L.mx_ring.bank(("NG", g))[0:NEG * HEADS_AT_ONCE, 0:T // 2].bitcast(BF16)
                for qt in range(TT):
                    last = nc.tensor.transpose(rows[:, qt * P:(qt + 1) * P],
                                               neg_parts[:, qt, :, :].rearrange("p a h -> p (a h)"),
                                               ident_bf[:, :])
                last.then_inc(L.mx_ring.filled, 1)

            def task(L, name, b, s):
                kind, t = name[:2], name[-1]
                if kind[0] in "Nmsuhl":
                    return
                ring = L.p_ring if name in L.p_ring.order else L.o_ring
                bank = ring.bank(name)
                if not (name == "qA" and len(ring.banks) > 1):
                    wait(pe, *ring.free(b, name))
                if name in ("T0", "T1"):
                    pe.wait_ge(L.x_in, 16 * b + 16)
                    for j in range(TT):
                        last = nc.tensor.transpose(bank[:, j * P:(j + 1) * P],
                                                   x_sb[:, j, int(t) * P:(int(t) + 1) * P],
                                                   ident_sb[:, :])
                elif name in ("qA", "qB", "kA", "kB"):
                    if name == "qA" and len(ring.banks) > 1:
                        all_empty(pe, ring, b, ("T0", "T1"))
                    c = ("qA", "qB", "kA", "kB").index(name)
                    for k in range(KD):
                        last = nc.tensor.matmul(bank[:, :],
                                                wqkv_sb[:, L.number, k, c * P:(c + 1) * P],
                                                xT[:, k, :], start=(k == 0), stop=(k == KD - 1))
                elif name in ("nq", "nk"):
                    pe.wait_ge(L.sq_done, 2 * b + (1 if name == "nq" else 2))
                    for k in range(2):
                        last = nc.tensor.matmul(bank[:, :], head_sum_sb[:, :], sq[:, k, :],
                                                start=(k == 0), stop=(k == 1))
                elif kind[0] == "V":
                    for j in range(2):
                        tt = 2 * int(t) + j
                        for k in range(KD):
                            last = nc.tensor.matmul(bank[:, j * D:(j + 1) * D],
                                                    xT[:, k, tt * P:(tt + 1) * P],
                                                    wqkv_sb[:, L.number, k, 2 * D:3 * D],
                                                    start=(k == 0), stop=(k == KD - 1))
                elif kind == "TO":
                    t = int(t)
                    if t == 0:
                        pe.wait_ge(L.oT_ready, GROUPS * b + GROUPS)
                    for g in range(GROUPS):
                        last = nc.tensor.transpose(bank[:, g * P:(g + 1) * P],
                                                   oT[:, s, g, t * P:(t + 1) * P], ident_sb[:, :])
                elif kind == "TP":
                    t = int(t)
                    pe.wait_ge(*ring.empty(b, f"TO{t}"))
                    for k in range(KD):
                        last = nc.tensor.transpose(bank[:, k * P:(k + 1) * P],
                                                   on[:, t % 2, k * P:(k + 1) * P], ident_sb[:, :])
                elif kind == "WO":
                    t = int(t)
                    pe.wait_ge(*ring.empty(b, f"TP{t}"))
                    for k in range(KD):
                        last = nc.tensor.matmul(bank[:, 0:D], onT[:, t % 2, k, :],
                                                wo_sb[:, L.number, k, :],
                                                start=(k == 0), stop=(k == KD - 1))
                elif kind == "HT":
                    t = int(t)
                    pe.wait_ge(L.h_ready, TT * b + (t + 1))
                    for k in range(KD):
                        last = nc.tensor.transpose(bank[:, k * P:(k + 1) * P],
                                                   hn[:, t, k * P:(k + 1) * P], ident_sb[:, :])
                elif kind == "GT":
                    t = int(t)
                    pe.wait_ge(*ring.empty(b, f"HT{t}"))
                    for k in range(KD):
                        last = nc.tensor.matmul(bank[:, 0:E], onT[:, t % 2, k, :],
                                                gate_w_sb[:, k, :],
                                                start=(k == 0), stop=(k == KD - 1))
                elif name == "RT":
                    pe.wait_ge(one_hot_ready, b - L.first + 1)
                    for t in range(TT + 1):
                        for before in range(min(t + 1, TT)):
                            last = nc.tensor.matmul(
                                bank[:, t * E:(t + 1) * E],
                                ones_sb[:, :] if before < t else route_c[:, 0:P],
                                one_hot[:, before, :], start=(before == 0),
                                stop=(before == min(t, TT - 1)))
                last.then_inc(ring.filled, 1)

            def body(par, projected, attended, finished):
                for q in range(QUADS):
                    mx = max_tiles(q, par, projected, attended)
                    groups = neg_group(q, par, projected, attended)
                    late = []
                    for j in range(HEADS_AT_ONCE):
                        if attended:
                            score(*attended, 1 - par, HEADS_AT_ONCE * q + j)
                        late += mx[j:j + 1]
                        if j == PV_AFTER:
                            if q == 0 and finished:
                                pv(*finished, par, QUADS - 1)
                            if q and attended:
                                pv(*attended, 1 - par, q - 1)
                            for L, b, g, s in groups:
                                neg_rows(L, b, g)
                            groups = []
                        if not groups:
                            for tile in late:
                                max_score(*tile)
                            late = []
                        outer_tasks((q, j), par, projected, finished, task)

            pipeline(pe, body)

            pe.wait_ge(tiles_ready, 1)
            for arrived in weights_in:
                pe.wait_ge(arrived, 16 * E)

            def expert_of(j):
                return pe.value_load(tile_expert[0:1, bass.ds(j, 1)], min_val=0, max_val=E - 1)

            def transpose_in(j, s):
                pe.wait_ge(xs_in[s], 8 * (j - s) + 16)
                wait(pe, xsT_ready, j)
                for k in range(KD):
                    last = nc.tensor.transpose(psum[4][:, k * P:(k + 1) * P],
                                               xs_sb[:, s, k * P:(k + 1) * P], ident_sb[:, :])
                last.then_inc(xs_T, 1)

            def up(j, s):
                e = expert_of(j)
                pe.wait_ge(xsT_ready, j + 1)
                for n in range(2):
                    wait(pe, gelu_done, 2 * j + (n - 1))
                    for k in range(KD):
                        last = nc.tensor.matmul(
                            psum[n][:, :], xsT[:, s, k, :],
                            w1_sb[:, bass.ds(e, 1), k, n * T:(n + 1) * T].rearrange(
                                "p a f -> p (a f)"),
                            start=(k == 0), stop=(k == KD - 1))
                    last.then_inc(up_done, 1)

            def transpose_hidden(j, s):
                for n in range(2):
                    pe.wait_ge(gelu_done, 2 * j + (n + 1))
                    wait(pe, hidT_ready, 2 * j + (n - 1))
                    for k in range(KF // 2):
                        at = n * T + k * P
                        last = nc.tensor.transpose(psum[2 + n][:, k * P:(k + 1) * P],
                                                   hid[:, s, at:at + P], ident_sb[:, :])
                    last.then_inc(hid_T, 1)

            def down(j, s):
                e = expert_of(j)
                pe.wait_ge(hidT_ready, 2 * j + 2)
                wait(pe, sum_done, j)
                for k in range(KF):
                    last = nc.tensor.matmul(
                        psum[5][:, 0:D], hidT[:, s, k, :],
                        w2_sb[:, bass.ds(e, 1), k, :].rearrange("p a d -> p (a d)"),
                        start=(k == 0), stop=(k == KF - 1))
                last.then_inc(down_done, 1)

            def expert_body(j, s, ends=False):
                transpose_hidden(j - 1, 1 - s)
                up(j, s)
                if not ends:
                    transpose_in(j + 1, 1 - s)
                down(j - 1, 1 - s)

            transpose_in(0, 0)
            up(0, 0)
            transpose_in(1, 1)
            expert_body(1, 1)
            expert_body(2, 0)
            with pe.Fori(1, TILES // 2 - 1) as pair:
                expert_body(2 * pair + 1, 1)
                expert_body(2 * pair + 2, 0)
            expert_body(TILES - 2, 1)
            expert_body(TILES - 1, 0, ends=True)
            transpose_hidden(TILES - 1, 0)
            down(TILES - 1, 0)

        @block.scalar
        def _(act):
            nc.scalar.preload_act_table_set("natural_log_exp_and_others")
            act.wait_ge(consts_set, N_CONST_OPS)

            def exp(L, b, c):
                q, j = c // HEADS_AT_ONCE, c % HEADS_AT_ONCE
                act.wait_ge(L.scores, CHUNKS * b + (c + 1))
                if j == 0:
                    wait(act, L.pv_done, QUADS * b + (q - 1))
                nc.scalar.activation(probs[:, q % 2, j, :], L.st_banks[c % len(L.st_banks)][:, :],
                                     ACT.Exp, scale=SCALE).then_inc(L.exps, 1)

            def group_out(L, b, s, g):
                act.wait_ge(L.pv_done, QUADS * b + TT * (g + 1))
                nc.scalar.activation(oT[:, s, g, :], L.pv_banks[g % len(L.pv_banks)][:, :], ACT.Copy
                                     ).then_inc(L.oT_ready, 1)

            def neg_rows(L, b, g):
                act.wait_ge(*L.mx_ring.full(b, ("NG", g)))
                wait(act, L.neg_in, 16 * GROUPS * (b - L.first) + 16 * g)
                nc.scalar.activation(neg_T[:, :],
                                     L.mx_ring.bank(("NG", g))[0:NEG * HEADS_AT_ONCE, 0:T // 2]
                                     .bitcast(BF16), ACT.Copy
                                     ).then_inc(L.mx_ring.drain_sem(("NG", g)), 1)

            def task(L, name, b, s):
                kind, t = name[:2], name[-1]
                p, o = L.p_ring, L.o_ring
                if name in ("T0", "T1") and L.second:
                    act.wait_ge(*p.full(b, name))
                    nc.scalar.activation(xT[:, int(t), :], p.bank(name)[:, :], ACT.Copy
                                         ).then_inc(p.drain_sem(name), 1)
                elif name in ("qA", "qB", "kA", "kB") and L.second:
                    qk, half = half_of(name)
                    act.wait_ge(*p.full(b, name))
                    wait(act, L.stack_in[qk], 16 * STACK_DMAS * b)
                    nc.scalar.activation(parts[:, qk, 0, half, :], p.bank(name)[:, :], ACT.Copy
                                         ).then_inc(L.high_done, 1)
                elif name in ("sq", "sk"):
                    qk = "qk".index(name[1])
                    act.wait_ge(L.rot_done, 2 * b + (qk + 1))
                    if qk:
                        act.wait_ge(*p.full(b, "nq"))
                    elif not isinstance(b, int) or b >= 1:
                        act.wait_ge(*p.full(b - 1, "nk"))
                    nc.scalar.activation(sq[:, :, :], rest[:, qk, :, :], ACT.Square
                                         ).then_inc(L.sq_done, 1)
                elif name in ("nq", "nk"):
                    n = "qk".index(name[1])
                    act.wait_ge(*p.full(b, name))
                    wait(act, L.p_step, 2 * SPLIT_STEPS * b + (SPLIT_STEPS * (n - 1) + 2))
                    nc.scalar.activation(rs[:, :], p.bank(name)[:, :], ACT.Ln,
                                         bias=eps_sb[:, 1:2]).then_inc(p.drain_sem(name), 1)
                    act.wait_ge(*p.empty(b, name))
                    nc.scalar.activation(rs[:, :], rs[:, :], ACT.Exp, scale=-0.5
                                         ).then_inc(L.rs_ready, 1)
                elif name in ("mq", "mk"):
                    qk = "qk".index(name[1])
                    all_empty(act, p, b, PARTS_OF[qk])
                    nc.scalar.activation(parts[:, qk, 1, :, :], rest[:, qk, :, :], ACT.Copy
                                         ).then_inc(L.mid_done, 1)
                elif kind[0] == "V" and L.second:
                    v_out(act, nc.scalar, L, name, b, s)
                elif kind in ("TP", "HT"):
                    act.wait_ge(*o.full(b, name))
                    nc.scalar.activation(onT[:, int(t) % 2, :, :].rearrange("p k c -> p (k c)"),
                                         o.bank(name)[:, 0:D], ACT.Copy
                                         ).then_inc(o.drain_sem(name), 1)
                elif kind[0] == "N":
                    t = int(t)
                    n = norms(L, b) + (t + 1 if L.second else 2 * t + int(kind[1]))
                    which = int(kind[1]) - 1
                    r = rstd[:, t % 2, which:which + 1]
                    act.wait_ge(L.mv_ready, n)
                    nc.scalar.activation(r, mv[:, t % 2, which, 1:2], ACT.Ln, bias=eps_sb[:, 0:1]
                                         ).then_inc(L.rstd_step, 1)
                    act.wait_ge(L.rstd_step, n)
                    nc.scalar.activation(r, r, ACT.Exp, scale=-0.5).then_inc(L.rstd_ready, 1)

            def load_weights(which, experts, free):
                for f in free:
                    act.wait_ge(*f)
                for e in experts:
                    dst, src = ((w1_sb, w1), (w2_sb, w2))[which]
                    act.dma_start(dst[:, e, :, :], src[e].rearrange("(k p) f -> p k f", p=P)
                                  ).then_inc(weights_in[which], 16)

            def body(par, projected, attended, finished):
                n = layer_b.first
                if not projected and attended:
                    load_weights(0, (0, 1, 4, 5), [(layer_b.scores, CHUNKS * (2 * BATCH - 1))])
                    load_weights(1, (6, 7), [(layer_b.parts_ready, 2 * 2 * BATCH)])
                if not projected and not attended:
                    load_weights(0, (2, 3, 6, 7), [(layer_b.scores, CHUNKS * 2 * BATCH)])
                    load_weights(1, (0, 4), [(layer_b.pv_done, QUADS * (2 * BATCH - 1)),
                                             layer_b.o_ring.full(2 * BATCH - 2, f"TO{TT - 1}")])
                if projected:
                    L, b = projected
                    if not isinstance(b, int) or b >= 1:
                        act.wait_ge(*L.p_ring.full(b - 1, "T1"))
                    if L.second:
                        stored = b - 2 if isinstance(b, int) else BATCH
                        for h_out in L.h_out:
                            act.wait_ge(h_out, 8 * TT * stored)
                    act.dma_start(x_sb[:, :, :], tiles(h1_dram if L.second else x, b - L.first)
                                  ).then_inc(L.x_in, 16)
                if finished:
                    L, b = finished
                    if L.second:
                        act.wait_ge(L.o_ring.drained[0], L.o_ring.base)
                        for x_out in L.x_out:
                            act.wait_ge(x_out, 8 * TT * BATCH)
                        act.wait_ge(L.sum_ready, TT * (b - n) + 2)
                    elif not isinstance(b, int) or b >= 1:
                        act.wait_ge(*L.o_ring.empty(b - 1, f"WO{TT - 1}"))
                    act.dma_start(res_sb[:, :, :], tiles(x1_dram if L.second else x, b - L.first)
                                  ).then_inc(L.res_in, 16)
                lag_of = attended[0].number if attended else projected[0].number if projected else 1
                for q in range(QUADS):
                    for j in range(HEADS_AT_ONCE):
                        if attended:
                            exp(*attended, HEADS_AT_ONCE * q + j)
                        if j == 1:
                            for L, b, g, s in neg_group(q, par, projected, attended):
                                neg_rows(L, b, g)
                        if j == 2 and q == 0 and finished:
                            group_out(*finished, par, GROUPS - 1)
                        if j == 2 and q and q % TT == 0 and attended:
                            group_out(*attended, 1 - par, q // TT - 1)
                        outer_tasks((q, j - ACT_LAG[lag_of]), par, projected, finished, task)

            pipeline(act, body)
            load_weights(1, (1, 2, 3, 5), [(layer_b.pv_done, QUADS * 2 * BATCH),
                                           layer_b.o_ring.full(2 * BATCH - 1, f"TO{TT - 1}")])

            def gelu(j, s):
                for n in range(2):
                    act.wait_ge(up_done, 2 * j + (n + 1))
                    if n == 0:
                        wait(act, hid_T, 2 * j - 2)
                    nc.scalar.activation(hid[:, s, n * T:(n + 1) * T], psum[n][:, :],
                                         ACT.Gelu_apprx_tanh).then_inc(gelu_done, 1)

            def last_norm(j, s):
                r = rstd[:, s, 0:1]
                act.wait_ge(last_mv, j + 1)
                nc.scalar.activation(r, mv[:, s, 0, 1:2], ACT.Ln, bias=eps_sb[:, 0:1]
                                     ).then_inc(last_ln, 1)
                act.wait_ge(last_ln, j + 1)
                nc.scalar.activation(r, r, ACT.Exp, scale=-0.5).then_inc(last_rstd, 1)

            gelu(0, 0)
            gelu(1, 1)
            last_norm(0, 0)
            gelu(2, 0)
            last_norm(1, 1)
            with act.Fori(1, TILES // 2) as pair:
                gelu(2 * pair + 1, 1)
                last_norm(2 * pair, 0)
                gelu(2 * pair + 2, 0)
                last_norm(2 * pair + 1, 1)
            last_norm(TILES - 1, 0)

        @block.vector
        def _(dve):
            ve = nc.vector
            dve.wait_ge(consts_in, 16 * N_CONST_DMAS)
            ve.tensor_copy(ident_bf[:, :], ident_sb[:, :]).then_inc(consts_set, 1)
            ve.memset(eps_sb[:, 0:1], EPS).then_inc(consts_set, 1)
            ve.memset(eps_sb[:, 1:2], 1e-6).then_inc(consts_set, 1)
            ve.memset(ones_sb[:, :], 1.0).then_inc(consts_set, 1)
            ve.tensor_copy(next_row[:, :], room_c)
            ve.tensor_copy(token[:, :], tok_c)

            def max_tile(L, b, g, c, s):
                use = ("MX", g, c)
                dve.wait_ge(*L.mx_ring.full(b, use))
                ve.tensor_reduce(negm[:, c % TT, c // TT:c // TT + 1], L.mx_ring.bank(use)[:, :],
                                 axis=AX.X, op=ALU.max, negate=True
                                 ).then_inc(L.mx_ring.drain_sem(use), 1)

            def neg_split(L, b, g):
                last_tile = HEADS_AT_ONCE * TT - 1
                dve.wait_ge(*L.mx_ring.empty(b, ("MX", g, last_tile - 1)))
                dve.wait_ge(*L.mx_ring.empty(b, ("MX", g, last_tile)))
                if g:
                    dve.wait_ge(*L.mx_ring.full(b, ("NG", g - 1)))
                elif not isinstance(b, int) or b > L.first:
                    dve.wait_ge(*L.mx_ring.full(b - 1, ("NG", GROUPS - 1)))
                n = 3 * GROUPS * (b - L.first)
                ve.tensor_copy(neg_parts[:, :, 0, :], negm[:, :, :]).then_inc(L.neg_step, 1)
                dve.wait_ge(L.neg_step, n + (3 * g + 1))
                ve.tensor_tensor(neg_rest[:, :, :], negm[:, :, :], neg_parts[:, :, 0, :],
                                 ALU.subtract).then_inc(L.neg_step, 1)
                dve.wait_ge(L.neg_step, n + (3 * g + 2))
                ve.tensor_copy(neg_parts[:, :, 1, :], neg_rest[:, :, :]).then_inc(L.neg_step, 1)
                dve.wait_ge(L.neg_step, n + (3 * g + 3))
                ve.tensor_tensor(neg_parts[:, :, 2, :], neg_rest[:, :, :], neg_parts[:, :, 1, :],
                                 ALU.subtract).then_inc(L.neg_ready, 1)

            def norm_and_split(L, name, b):
                qk = "qk".index(name[1])
                n = 2 * SPLIT_STEPS * b + SPLIT_STEPS * qk
                if name[0] == "u":
                    dve.wait_ge(L.rs_ready, 2 * b + (qk + 1))
                    for half in range(2):
                        ve.tensor_tensor(rest[:, qk, half, :], rest[:, qk, half, :], rs[:, :],
                                         ALU.mult).then_inc(L.p_step, 1)
                elif name[0] == "h":
                    wait(dve, L.stack_in[qk], 16 * STACK_DMAS * b)
                    for half in range(2):
                        dve.wait_ge(L.p_step, n + (1 + half))
                        ve.tensor_copy(parts[:, qk, 0, half, :], rest[:, qk, half, :]
                                       ).then_inc(L.p_step, 1)
                    for half in range(2):
                        dve.wait_ge(L.p_step, n + (3 + half))
                        ve.tensor_tensor(rest[:, qk, half, :], rest[:, qk, half, :],
                                         parts[:, qk, 0, half, :], ALU.subtract
                                         ).then_inc(L.p_step, 1)
                else:
                    for half in range(2):
                        dve.wait_ge(L.p_step, n + (5 + half))
                        ve.tensor_copy(parts[:, qk, 1, half, :], rest[:, qk, half, :]
                                       ).then_inc(L.mid_done if half else L.p_step, 1)

            def routing_step(b, k, op):
                op.then_inc(route_step, 1)
                dve.wait_ge(route_step, ROUTE_STEPS * b + k)

            def over(ap, n):
                return ap.unsqueeze(1).to_broadcast([P, n, E])

            def one_hots(b):
                over_e = lambda ap: ap.unsqueeze(2).to_broadcast([P, TT, E])
                routing_step(b, 1, ve.tensor_reduce(top[:, :], logits[:, :, :], axis=AX.X,
                                                    op=ALU.max))
                routing_step(b, 2, ve.tensor_tensor(one_hot[:, :, :], logits[:, :, :],
                                                    over_e(top[:, :]), ALU.is_equal))
                routing_step(b, 3, ve.tensor_tensor(one_hot[:, :, :], one_hot[:, :, :],
                                                    over(rank_c, TT), ALU.mult))
                routing_step(b, 4, ve.tensor_reduce(top[:, :], one_hot[:, :, :], axis=AX.X,
                                                    op=ALU.max))
                ve.tensor_tensor(one_hot[:, :, :], one_hot[:, :, :], over_e(top[:, :]),
                                 ALU.is_equal).then_inc(one_hot_ready, 1)

            def rows_of_tokens(L, b, own):
                ring = L.o_ring
                sums = ring.bank("RT")
                dve.wait_ge(*ring.full(b, "RT"))
                wait(dve, dispatched, 16 * TT * own)
                ve.tensor_copy(row_sb[:, :, 2 * D].bitcast(U32), token[:, :]).then_inc(route_step, 1)
                routing_step(own, 6, ve.tensor_tensor(
                    slot3[:, :, :], sums[:, 0:TT * E].rearrange("p (t e) -> p t e", t=TT),
                    over(next_row[:, 0:E], TT), ALU.add))
                ve.tensor_tensor(next_row[:, 0:E], next_row[:, 0:E], sums[:, TT * E:(TT + 1) * E],
                                 ALU.add).then_inc(ring.drain_sem("RT"), 1)
                ve.tensor_scalar(token[:, :], token[:, :], float(T), None, ALU.add
                                 ).then_inc(route_step, 1)
                routing_step(own, 8, ve.tensor_tensor(slot3[:, :, :], slot3[:, :, :],
                                                    one_hot[:, :, :], ALU.mult))
                routing_step(own, 9, ve.tensor_reduce(slot_f[:, :], slot3[:, :, :], axis=AX.X,
                                                    op=ALU.add))
                routing_step(own, 10, ve.tensor_copy(slot_u[:, :], slot_f[:, :]))
                dve.wait_ge(*ring.empty(b, "RT"))
                ve.memset(wait_cell[:, :], 0.0).then_inc(slots_ready, 1)

            def moments(L, n, src, dst):
                ve.bn_stats(stats[:, :], src).then_inc(L.o_step, 1)
                dve.wait_ge(L.o_step, n + 1)
                ve.memset(wait_cell[:, :], 0.0)
                ve.bn_aggr(dst, stats[:, :]).then_inc(L.mv_ready, 1)

            def task(L, name, b, s):
                kind, t = name[:2], name[-1]
                p, o = L.p_ring, L.o_ring
                if name in ("T0", "T1") and not L.second:
                    dve.wait_ge(*p.full(b, name))
                    ve.tensor_copy(xT[:, int(t), :], p.bank(name)[:, :]
                                   ).then_inc(p.drain_sem(name), 1)
                elif name in ("qA", "qB", "kA", "kB"):
                    qk, half = half_of(name)
                    if not L.second:
                        dve.wait_ge(*p.full(b, name))
                        wait(dve, L.rot_done, 2 * b + qk)
                        first, then = (sin_sb, cos_sb) if half else (cos_sb, sin_sb)
                        ve.tensor_tensor(trig[:, 2 * half, :], p.bank(name)[:, :], first[:, :],
                                         ALU.mult)
                        ve.tensor_tensor(trig[:, 2 * half + 1, :], p.bank(name)[:, :], then[:, :],
                                         ALU.mult).then_inc(p.drain_sem(name), 1)
                    else:
                        dve.wait_ge(L.high_done, 4 * (b - L.first) + (2 * qk + half + 1))
                        wait(dve, L.parts_ready, 2 * b + (qk - 1))
                        ve.tensor_tensor(rest[:, qk, half, :], p.bank(name)[:, :],
                                         parts[:, qk, 0, half, :], ALU.subtract
                                         ).then_inc(p.drain_sem(name), 1)
                elif kind[0] in "uhl":
                    norm_and_split(L, name, b)
                elif kind[0] == "V" and not L.second:
                    v_out(dve, nc.vector, L, name, b, s)
                elif kind == "TO":
                    t = int(t)
                    heads = o.bank(name)[:, :].rearrange("p (h e) -> p h e", h=H)
                    dve.wait_ge(*o.full(b, name))
                    ve.reciprocal(recip[:, :], heads[:, :, HD]).then_inc(L.o_step, 1)
                    dve.wait_ge(L.o_step, o_steps(L, b) + (O_STEPS[L.number] * t + 1))
                    ve.tensor_tensor(on[:, t % 2, :].rearrange("p (h e) -> p h e", h=H),
                                     heads[:, :, 0:HD],
                                     recip[:, :].unsqueeze(2).to_broadcast([P, H, HD]), ALU.mult
                                     ).then_inc(o.drain_sem(name), 1)
                elif kind == "WO":
                    t = int(t)
                    n = o_steps(L, b) + (O_STEPS[L.number] * t + 1)
                    dst = xo if L.second else y
                    dve.wait_ge(*o.full(b, name))
                    if t == 0:
                        if L.second:
                            dve.wait_ge(L.res_in, 16 * b + 16)
                        else:
                            dve.wait_ge(L.res_ready, b + 1)
                    if L.second:
                        dve.wait_ge(L.sum_ready, TT * (b - L.first) + (t + 1))
                        dve.wait_ge(L.x_out[t % 2], 8 * TT * BATCH)
                    ve.tensor_tensor(dst[:, t % 2, :], o.bank(name)[:, 0:D], res_sb[:, t, :],
                                     ALU.add).then_inc(o.drain_sem(name), 1)
                    dve.wait_ge(*o.empty(b, name))
                    moments(L, n, dst[:, t % 2, :], mv[:, t % 2, 1 if L.second else 0, :])
                elif kind == "N1":
                    t = int(t)
                    n = o_steps(L, b) + (O_STEPS[L.number] * t + 2)
                    dve.wait_ge(L.rstd_ready, norms(L, b) + (2 * t + 1))
                    wait(dve, L.x_out[t % 2], 8 * TT * b + 16 * (t // 2))
                    ve.tensor_scalar(xo[:, t % 2, :], y[:, t % 2, :], mv[:, t % 2, 0, 0:1],
                                     rstd[:, t % 2, 0:1], ALU.subtract, ALU.mult
                                     ).then_inc(L.o_step, 1)
                    dve.wait_ge(L.o_step, n + 1)
                    moments(L, n + 1, xo[:, t % 2, :], mv[:, t % 2, 1, :])
                elif kind == "N2":
                    t = int(t)
                    if L.second:
                        dve.wait_ge(L.rstd_ready, norms(L, b) + (t + 1))
                    else:
                        dve.wait_ge(L.rstd_ready, norms(L, b) + (2 * t + 2))
                    if L.second:
                        wait(dve, dispatched, 16 * TT * (b - L.first))
                        dve.wait_ge(L.h_out[t % 2], 8 * TT * BATCH)
                    else:
                        wait(dve, L.h_out[t % 2], 8 * TT * b + 16 * (t // 2))
                    ve.tensor_scalar(hn[:, t, :], xo[:, t % 2, :], mv[:, t % 2, 1, 0:1],
                                     rstd[:, t % 2, 1:2], ALU.subtract, ALU.mult
                                     ).then_inc(L.hn_ready, 1)
                elif kind == "GT":
                    t = int(t)
                    dve.wait_ge(*o.full(b, name))
                    ve.tensor_tensor(logits[:, t, :], o.bank(name)[:, 0:E], gate_b_sb[:, :],
                                     ALU.add).then_inc(o.drain_sem(name), 1)
                    if t == TT - 1:
                        dve.wait_ge(*o.empty(b, name))
                        one_hots(b - L.first)
                elif name == "RT":
                    rows_of_tokens(L, b, b - L.first)

            def body(par, projected, attended, finished):
                lag_of = attended[0].number if attended else projected[0].number if projected else 1
                for q in range(QUADS):
                    mx = max_tiles(q, par, projected, attended)
                    for L, b, g, s in neg_group(q, par, projected, attended):
                        neg_split(L, b, g)
                    for j in range(HEADS_AT_ONCE):
                        if mx:
                            max_tile(*mx[j])
                        outer_tasks((q, j - DVE_LAG[lag_of]), par, projected, finished, task)

            pipeline(dve, body)

            step = lambda k, op: routing_step(BATCH, k, op)
            dve.wait_ge(*layer_b.o_ring.empty(2 * BATCH - 1, "RT"))
            dve.wait_ge(pad_set, 1)
            ve.tensor_copy(pad_row[:, 2 * D:ROW].bitcast(U32), pad_c)
            ve.tensor_scalar(pad_u[:, :], next_row[:, :], tok_c[:, 0:1], None, ALU.add
                             ).then_inc(slots_ready, 1)
            one = slice(0, 1)
            step(1, ve.tensor_tensor(counts_i[:, :], next_row[one, 0:E], room_c[one, 0:E],
                                     ALU.subtract))
            step(2, ve.tensor_scalar(counts_i[:, :], counts_i[:, :], P - 1, None, ALU.add))
            step(3, ve.tensor_scalar(counts_i[:, :], counts_i[:, :], LOG_P, None,
                                     ALU.logical_shift_right))
            step(4, ve.tensor_copy(n_tiles[:, :], counts_i[:, :]))
            step(5, ve.tensor_tensor_scan(tile_end[:, :], ones_sb[one, 0:E], n_tiles[:, :], 0.0,
                                          ALU.mult, ALU.add))
            step(6, ve.tensor_tensor(past[:, :, :],
                                     tile_end[:, :].unsqueeze(1).to_broadcast([1, TILES, E]),
                                     tile_c[one, :].unsqueeze(2).to_broadcast([1, TILES, E]),
                                     ALU.is_le))
            step(7, ve.tensor_reduce(tile_e_f[:, :], past[:, :, :], axis=AX.X, op=ALU.add))
            step(8, ve.tensor_tensor(past[:, :, :], past[:, :, :],
                                     n_tiles[:, :].unsqueeze(1).to_broadcast([1, TILES, E]),
                                     ALU.mult))
            step(9, ve.tensor_reduce(tile_at[:, :], past[:, :, :], axis=AX.X, op=ALU.add))
            step(10, ve.tensor_tensor(tile_at[:, :], tile_c[one, :], tile_at[:, :], ALU.subtract))
            step(11, ve.tensor_scalar(tile_used[:, :], tile_e_f[:, :], float(E), float(P),
                                      ALU.is_lt, ALU.mult))
            step(12, ve.tensor_tensor(tile_at[:, :], tile_at[:, :], tile_used[:, :], ALU.mult))
            step(13, ve.tensor_scalar(tile_used[:, :], tile_e_f[:, :], float(ROOM), None,
                                      ALU.mult))
            step(14, ve.tensor_tensor(tile_row[:, :], tile_used[:, :], tile_at[:, :], ALU.add))
            ve.tensor_scalar(tile_expert[:, :], tile_e_f[:, :], float(E - 1), None, ALU.min
                             ).then_inc(tiles_ready, 1)

            def tile_in(j, s):
                dve.wait_ge(xs_T, j + 1)
                ve.tensor_copy(xsT[:, s, :, :].rearrange("p k t -> p (k t)"), psum[4][:, 0:D]
                               ).then_inc(xsT_ready, 1)

            def hidden(j, s):
                for n in range(2):
                    dve.wait_ge(hid_T, 2 * j + (n + 1))
                    if n == 0:
                        wait(dve, down_done, j - 1)
                    half = hidT[:, s, n * KF // 2:(n + 1) * KF // 2, :]
                    ve.tensor_copy(half.rearrange("p k t -> p (k t)"), psum[2 + n][:, :]
                                   ).then_inc(hidT_ready, 1)

            def tile_sum(j, s):
                dve.wait_ge(down_done, j + 1)
                dve.wait_ge(rest_in[s], 8 * (j - s) + 16)
                ve.tensor_tensor(z_sb[:, s, :], psum[5][:, 0:D], rest_sb[:, s, 0:D], ALU.add
                                 ).then_inc(sum_done, 1)
                dve.wait_ge(sum_done, j + 1)
                ve.bn_stats(stats[:, :], z_sb[:, s, :]).then_inc(last_stats, 1)
                dve.wait_ge(last_stats, j + 1)
                ve.memset(wait_cell[:, :], 0.0)
                ve.bn_aggr(mv[:, s, 0, :], stats[:, :]).then_inc(last_mv, 1)

            def tile_out(j, s):
                dve.wait_ge(last_rstd, j + 1)
                wait(dve, out_stored[s], 8 * (j - s))
                ve.tensor_scalar(o_sb[:, s, :], z_sb[:, s, :], mv[:, s, 0, 0:1], rstd[:, s, 0:1],
                                 ALU.subtract, ALU.mult).then_inc(out_ready, 1)

            def expert_body(j, s, first=False, ends=False):
                hidden(j - 1, 1 - s)
                if not ends:
                    tile_in(j + 1, 1 - s)
                if not first:
                    tile_out(j - 2, s)
                tile_sum(j - 1, 1 - s)

            tile_in(0, 0)
            tile_in(1, 1)
            expert_body(1, 1, first=True)
            expert_body(2, 0)
            with dve.Fori(1, TILES // 2 - 1) as pair:
                expert_body(2 * pair + 1, 1)
                expert_body(2 * pair + 2, 0)
            expert_body(TILES - 2, 1)
            expert_body(TILES - 1, 0, ends=True)
            hidden(TILES - 1, 0)
            tile_out(TILES - 2, 1)
            tile_sum(TILES - 1, 0)
            tile_out(TILES - 1, 0)

        @block.gpsimd
        def _(pool):
            pool.memset(pool_cell[:, :], 0.0).then_inc(layer_b.sum_ready, 2)
            pool.memset(v_aug[:, :, :, :, HD:VW], 0.0).then_inc(pool_set, 1)
            pool.wait_ge(pool_set, 1)
            pool.memset(v_aug[:, :, :, :, HD:HD + 1], 1.0).then_inc(pool_set, 1)
            pool.wait_ge(pool_set, 2)
            pool.memset(k_stack[STACK:STACK + NEG, :, :, :], 1.0).then_inc(pool_set, 1)
            pool.wait_ge(pool_set, 3)
            pool.wait_ge(consts_in, 16 * N_CONST_DMAS)

            def task(L, name, b, s):
                kind, t = name[:2], name[-1]
                p = L.p_ring
                if name in ("qB", "kB") and not L.second:
                    qk = "qk".index(name[0])
                    all_empty(pool, p, b, PARTS_OF[qk])
                    wait(pool, L.parts_ready, 2 * b + (qk - 1))
                    pool.tensor_tensor(rest[:, qk, 0, :], trig[:, 0, :], trig[:, 2, :],
                                       ALU.subtract)
                    pool.tensor_tensor(rest[:, qk, 1, :], trig[:, 1, :], trig[:, 3, :], ALU.add
                                       ).then_inc(L.rot_done, 1)
                elif kind[0] in "ml":
                    qk = "qk".index(name[1])
                    pool.wait_ge(L.mid_done, 2 * b + (qk + 1))
                    pool.tensor_tensor(parts[:, qk, 2, :, :], rest[:, qk, :, :],
                                       parts[:, qk, 1, :, :], ALU.subtract
                                       ).then_inc(L.parts_ready, 1)
                elif name == "TO0" and not L.second:
                    pool.wait_ge(L.res_in, 16 * b + 16)
                    pool.tensor_tensor(res_sb[:, :, :], res_sb[:, :, :],
                                       rows_sb[:, 0:1, :].to_broadcast([P, TT, D]), ALU.add
                                       ).then_inc(L.res_ready, 1)
                elif kind == "WO" and L.second:
                    t = int(t)
                    pool.wait_ge(*L.o_ring.empty(b, name))
                    if t == 0:
                        wait(pool, dispatched, 16 * TT * (b - L.first))
                    pool.tensor_tensor(row_sb[:, t, D:2 * D], res_sb[:, t, :], xo[:, t % 2, :],
                                       ALU.add).then_inc(L.sum_ready, 1)
                elif name == "RT":
                    pool.wait_ge(L.h_ready, TT * b + TT)
                    pool.wait_ge(L.sum_ready, TT * (b - L.first) + (TT + 2))
                    pool.wait_ge(slots_ready, b - L.first + 1)
                    pool.tensor_tensor(pool_cell[:, :], pool_cell[:, :], pool_cell[:, :], ALU.add)
                    for t in range(TT):
                        pool.indirect_dma_start(
                            rows_dram, bass.IndirectOffsetOnAxis(slot_u[:, t:t + 1], 0),
                            row_sb[:, t, :], None).then_inc(dispatched, 16)
                elif kind == "N2":
                    t = int(t)
                    r = 3 if L.second else 1
                    pool.wait_ge(L.hn_ready, TT * b + (t + 1))
                    pool.tensor_tensor(hn[:, t, :], hn[:, t, :], rows_sb[:, r, :], ALU.mult
                                       ).then_inc(L.hw_step, 1)
                    pool.wait_ge(L.hw_step, TT * b + (t + 1))
                    pool.tensor_tensor(hn[:, t, :], hn[:, t, :], rows_sb[:, r + 1, :],
                                       ALU.add).then_inc(L.h_ready, 1)

            def body(par, projected, attended, finished):
                for slot in SLOTS:
                    outer_tasks(slot, par, projected, finished, task)

            pipeline(pool, body)

            pool.wait_ge(*layer_b.p_ring.full(2 * BATCH - 1, "T1"))
            pool.memset(pad_row, 0.0).then_inc(pad_set, 1)
            pool.wait_ge(slots_ready, BATCH + 1)
            for e in range(E + 1):
                pool.indirect_dma_start(rows_dram, bass.IndirectOffsetOnAxis(pad_u[:, e:e + 1], 0),
                                        pad_row, None).then_inc(padded, 16)
            for j in range(TILES):
                s = j % 2
                if j:
                    pool.wait_ge(out_stored[1 - s], 16 * ((j + 1) // 2))
                pool.wait_ge(out_ready, j + 1)
                pool.indirect_dma_start(
                    out_rows, bass.IndirectOffsetOnAxis(rest_sb[:, s, D:D + 1].bitcast(U32), 0),
                    o_sb[:, s, :], None).then_inc(out_stored[s], 16)

        @block.sync
        def _(sp):
            n = 0
            for dst, src in (
                    (ident_sb[:, :], ident), (head_sum_sb[:, :], head_sum),
                    (cos_sb[:, :], cos_t), (sin_sb[:, :], sin_t),
                    (wqkv_sb[:, 0, 0, :], w_qkv1[0:P, :]), (wqkv_sb[:, 0, 1, :], w_qkv1[P:D, :]),
                    (wqkv_sb[:, 1, 0, :], w_qkv2[0:P, :]), (wqkv_sb[:, 1, 1, :], w_qkv2[P:D, :]),
                    (wo_sb[:, 0, :, :], w_o1.rearrange("(k p) n -> p k n", p=P)),
                    (wo_sb[:, 1, :, :], w_o2.rearrange("(k p) n -> p k n", p=P)),
                    (rows_sb[:, 0, :], b_o.partition_broadcast(P)),
                    (rows_sb[:, 1, :], ln1_w.partition_broadcast(P)),
                    (rows_sb[:, 2, :], ln1_b.partition_broadcast(P)),
                    (rows_sb[:, 3, :], ln2_w.partition_broadcast(P)),
                    (rows_sb[:, 4, :], ln2_b.partition_broadcast(P)),
                    (gate_w_sb[:, 0, :], gate_w[0:P, :]), (gate_w_sb[:, 1, :], gate_w[P:D, :]),
                    (gate_b_sb[:, :], gate_b.partition_broadcast(P)),
                    (route_c[:, :], route_consts)):
                sp.dma_start(dst, src).then_inc(consts_in, 16)
                n += 1
            assert n == N_CONST_DMAS
            def task(L, name, b, s):
                kind, t = name[:2], name[-1]
                if kind[0] in "ml":
                    qk = "qk".index(name[1])
                    stack, slots = ((q_stack, Q_SLOTS), (k_stack, K_SLOTS))[qk]
                    sp.wait_ge(L.parts_ready, 2 * b + (qk + 1))
                    if not isinstance(b, int) or b >= 2:
                        sp.wait_ge(L.scores, CHUNKS * b - CHUNKS)
                    for slot, part in enumerate(slots):
                        for half in range(2):
                            at = HD * slot + HALF * half
                            sp.dma_start(stack[at:at + HALF, s, :, :], parts[:, qk, part, half, :]
                                         ).then_inc(L.stack_in[qk], 16)
                elif kind == "N1":
                    t = int(t)
                    sp.wait_ge(L.mv_ready, norms(L, b) + (2 * t + 2))
                    sp.dma_start(tile_of(x1_dram, b, t), xo[:, t % 2, :]
                                 ).then_inc(L.x_out[t % 2], 16)
                elif kind == "N2" and not L.second:
                    t = int(t)
                    sp.wait_ge(L.h_ready, TT * b + (t + 1))
                    sp.dma_start(tile_of(h1_dram, b, t), hn[:, t, :]
                                 ).then_inc(L.h_out[t % 2], 16)

            def neg_rows(L, b, g, s):
                sp.wait_ge(*L.mx_ring.empty(b, ("NG", g)))
                sp.dma_start(q_stack[STACK:STACK + NEG, s, HEADS_AT_ONCE * g:HEADS_AT_ONCE * (g + 1), :],
                             neg_T[:, :]).then_inc(L.neg_in, 16)

            def body(par, projected, attended, finished):
                for q in range(QUADS):
                    for L, b, g, s in neg_group(q, par, projected, attended):
                        neg_rows(L, b, g, s)
                    for j in (0, 2):
                        outer_tasks((q, j), par, projected, finished, task)

            pipeline(sp, body)
            sp.wait_ge(tiles_ready, 1)
            sp.wait_ge(dispatched, 16 * TT * BATCH)
            sp.wait_ge(padded, 16 * (E + 1))

            def rows_of(j):
                row = sp.value_load(tile_row[0:1, bass.ds(j, 1)], min_val=0, max_val=E * ROOM)
                return rows_dram[bass.ds(row, P), :]

            def load_rest(j, s):
                rows = rows_of(j)
                wait(sp, out_stored[s], 8 * (j - s))
                sp.dma_start(rest_sb[:, s, :], rows[:, D:ROW]).then_inc(rest_in[s], 16)

            def load_tile(j, s):
                rows = rows_of(j)
                wait(sp, xs_T, j - 1)
                sp.dma_start(xs_sb[:, s, :], rows[:, 0:D]).then_inc(xs_in[s], 16)

            load_tile(0, 0)
            load_rest(0, 0)
            load_tile(1, 1)
            load_rest(1, 1)
            load_tile(2, 0)
            with sp.Fori(1, TILES // 2) as pair:
                load_tile(2 * pair + 1, 1)
                load_rest(2 * pair, 0)
                load_tile(2 * pair + 2, 0)
                load_rest(2 * pair + 1, 1)
            load_rest(TILES - 1, 0)

            for s in range(2):
                sp.wait_ge(out_stored[s], 16 * ((TILES + 1 - s) // 2))
            for b in range(BATCH):
                sp.dma_start(out[b], out_rows[b * T:(b + 1) * T, :]).then_inc(out_done, 16)
            sp.wait_ge(out_done, 16 * BATCH)


def lay_out(**inputs):
    a = {k.removeprefix("L0_"): np.asarray(v) for k, v in inputs.items()}
    def columns(w):
        qk = w[:, :2 * D].reshape(D, 2, H, 2, HALF).transpose(0, 1, 3, 4, 2).reshape(D, 2 * D)
        return np.ascontiguousarray(np.concatenate([qk, w[:, 2 * D:]], axis=1))
    inv_freq = (1.0 / np.float32(10000.0) ** (np.arange(HALF, dtype=np.float32) / np.float32(HALF)))
    angles = (np.arange(T, dtype=np.float32)[None, :] * inv_freq.astype(np.float32)[:, None])
    table = lambda f: np.repeat(f(angles).astype(np.float32), H, axis=0)
    of_head = np.arange(P) % H
    return {
        "x": a["attn_x"], "w_qkv1": columns(a["attn_Wqkv"]), "w_o1": a["attn_Wo"],
        "b_o": a["attn_bo"], "ln1_w": a["ffn_ln1_w"], "ln1_b": a["ffn_ln1_b"],
        "w_qkv2": columns(a["ffn_w_qkv"]), "w_o2": a["ffn_w_proj"], "ln2_w": a["ffn_ln2_w"],
        "ln2_b": a["ffn_ln2_b"], "gate_w": a["ffn_gate_w"], "gate_b": a["ffn_gate_b"],
        "w1": a["ffn_w1"], "w2": a["ffn_w2"], "cos_t": table(np.cos), "sin_t": table(np.sin),
        "head_sum": (of_head[:, None] == of_head[None, :]).astype(np.float32),
        "ident": np.eye(P, dtype=np.float32),
        "route_consts": np.concatenate([
            np.triu(np.ones((P, P)), 1), np.tile(E - np.arange(E), (P, 1)),
            np.tile(ROOM * np.arange(E + 1), (P, 1)), np.tile(np.arange(TILES), (P, 1)),
            np.arange(P)[:, None] + P * np.arange(TT)[None, :],
            BATCH * T + np.arange(P)[:, None]], axis=1).astype(np.float32),
    }


def kernel(**inputs):
    import concourse.bacc as bacc
    from concourse.bass_utils import run_bass_kernel_spmd

    nc = bacc.Bacc("TRN2", target_bir_lowering=False, num_devices=1)
    arrays, args = {}, {}
    for name, a in lay_out(**inputs).items():
        a = np.ascontiguousarray(a)
        arrays[f"in_{name}_dram"] = a
        args[name] = nc.dram_tensor(f"in_{name}_dram", a.shape, mybir.dt.from_np(a.dtype),
                                    kind="ExternalInput").ap()
    args["out"] = nc.dram_tensor("out_0_dram", (BATCH, T, D), FP32, kind="ExternalOutput").ap()
    program(nc, **args)
    return run_bass_kernel_spmd(nc, [arrays], core_ids=[0]).results[0]["out_0_dram"]
```

```python
from contextlib import ExitStack

import numpy as np

import concourse.bass as bass
from concourse import mybir

FP32 = mybir.dt.float32
BF16 = mybir.dt.bfloat16
I32 = mybir.dt.int32
U32 = mybir.dt.uint32
ALU = mybir.AluOpType
ACT = mybir.ActivationFunctionType
AX = mybir.AxisListType

BATCH, T, D, H = 8, 512, 256, 16
HD = D // H
P = 128
TT = T // P
KD = D // P
HALF = HD // 2
E = 8
HEADS_AT_ONCE = 4
GROUPS = H // HEADS_AT_ONCE
QUADS = GROUPS * TT
CHUNKS = QUADS * HEADS_AT_ONCE
VW = 32
Q_SLOTS = (0, 1, 2, 0, 1, 0)
K_SLOTS = (0, 0, 0, 1, 1, 2)
STACK = HD * len(Q_SLOTS)
NEG = 3
STACK_DMAS = 2 * len(Q_SLOTS)
F = 4 * D
KF = F // P
TILES = BATCH * T // P + E - 1
LOG_P = P.bit_length() - 1
EPS = 1e-5
SCALE = 1.0 / HD ** 0.5


class Ring:

    def __init__(self, name, banks, order, sem, first, before):
        self.banks, self.order, self.first = banks, order, first
        assert len(order) % len(banks) == 0
        self.base = before.base + len(before.order) * (first - before.first) if before else 0
        self.filled = sem(f"{name}_filled")
        self.drained = [sem(f"{name}_drained{i}") for i in range(len(banks))]

    def _k(self, use):
        return self.order.index(use)

    def bank(self, use):
        return self.banks[self._k(use) % len(self.banks)]

    def drain_sem(self, use):
        return self.drained[self._k(use) % len(self.banks)]

    def free(self, b, use):
        k, n = self._k(use), len(self.banks)
        return self.drain_sem(use), (b - self.first) * (len(self.order) // n) + (
            self.base // n + k // n + 1)

    def full(self, b, use):
        return self.filled, (b - self.first) * len(self.order) + (self.base + self._k(use) + 1)

    def empty(self, b, use):
        s, v = self.free(b, use)
        return s, v + 1


def all_empty(eng, ring, b, uses):
    for use in uses[-len(ring.banks):]:
        eng.wait_ge(*ring.empty(b, use))


def wait(eng, sem, value):
    if not (isinstance(value, int) and value <= 0):
        eng.wait_ge(sem, value)


class Layer:

    def __init__(self, number, sem, psum, before=None):
        self.number, self.second = number, number == 1
        self.first = number * BATCH
        self.rows = STACK + (NEG if self.second else 0)
        self.p_tasks, self.o_tasks = {}, {}
        if not self.second:
            p_steps = ((1, 2, "T0"), (2, 0, "T1"), (2, 2, "qA"), (3, 2, "qB"), (4, 2, "kA"),
                       (5, 2, "sq"), (5, 2, "kB"), (6, 2, "nq"), (7, 0, "uq"), (7, 2, "hq"),
                       (7, 2, "sk"), (8, 2, "nk"), (8, 2, "lq"), (9, 0, "uk"), (9, 2, "hk"),
                       (10, 0, "lk"), (10, 2, "V0"), (12, 2, "V1"))
            o_at = lambda t: (("TO", 4 + 6 * t), ("TP", 6 + 6 * t), ("WO", 8 + 6 * t),
                              ("N1", 10 + 6 * t), ("N2", 12 + 6 * t))
            p_bank, o_bank, st_banks, pv_bank, mx_banks = 4, 5, [0, 1, 2], 6, []
        else:
            p_steps = ((1, 2, "T0"), (2, 0, "T1"), (2, 2, "qA"), (3, 2, "qB"), (4, 0, "mq"),
                       (4, 2, "kA"), (5, 2, "kB"), (6, 0, "mk"), (8, 2, "V0"), (12, 2, "V1"))
            o_at = lambda t: (("TO", 3 + 5 * t), ("TP", 5 + 5 * t), ("WO", 7 + 5 * t),
                              ("N2", 9 + 5 * t), ("HT", 11 + 5 * t), ("GT", 14 + 5 * t))
            p_bank, o_bank, st_banks, pv_bank, mx_banks = 4, 5, [0, 1, 2], 6, [3, 7]
        for q, j, step in p_steps:
            self.p_tasks.setdefault((q, j), []).append(step)
        for t in range(TT):
            for step, at in o_at(t):
                self.o_tasks.setdefault(SLOTS[at], []).append(f"{step}{t}")
        if self.second:
            self.o_tasks.setdefault(SLOTS[-1], []).append("RT")
        in_psum = lambda tasks: [x for slot in SLOTS for x in tasks.get(slot, [])
                                 if x[0] not in "Nmsuhl"]
        banks = lambda ids: [psum[i] for i in ids]
        ring = lambda n, ids, order, last: Ring(n, banks(ids), order, sem, self.first, last)
        self.p_ring = ring("proj", [p_bank], in_psum(self.p_tasks), before and before.p_ring)
        self.o_ring = ring("out", [o_bank], in_psum(self.o_tasks), before and before.o_ring)
        self.st_banks, self.pv_banks = banks(st_banks), banks([pv_bank])
        if self.second:
            order = []
            for g in range(GROUPS):
                order += [("MX", g, c) for c in range(HEADS_AT_ONCE * TT)] + [("NG", g)]
            self.mx_ring = ring("max", mx_banks, order, None)
            self.neg_step = sem("neg_step")
            self.neg_ready = sem("neg_ready")
            self.neg_in = sem("neg_in")
        self.x_in = sem("x_in")
        self.res_in = sem("res_in")
        self.res_ready = sem("res_ready")
        self.sq_done = sem("sq_done")
        self.rot_done = sem("rot_done")
        self.rs_ready = sem("rs_ready")
        self.high_done = sem("high_done")
        self.mid_done = sem("mid_done")
        self.p_step = sem("p_step")
        self.parts_ready = sem("parts_ready")
        self.stack_in = [sem("q_in"), sem("k_in")]
        self.scores = sem("scores")
        self.exps = sem("exps")
        self.pv_done = sem("pv_done")
        self.oT_ready = sem("oT_ready")
        self.sum_ready = sem("sum_ready")
        self.o_step = sem("o_step")
        self.mv_ready = sem("mv_ready")
        self.rstd_step = sem("rstd_step")
        self.rstd_ready = sem("rstd_ready")
        self.hn_ready = sem("hn_ready")
        self.hw_step = sem("hw_step")
        self.h_ready = sem("h_ready")
        self.x_out = [sem("x_out0"), sem("x_out1")]
        self.h_out = [sem("h_out0"), sem("h_out1")]


SLOTS = [(q, j) for q in range(QUADS) for j in (0, 2)]
ROOM = BATCH * T
ROW = 2 * D + 1
ROUTE_STEPS = 10
SPLIT_STEPS = 7
MAX_LEAD = 6
ACT_LAG, DVE_LAG = (1, 0), (0, 0)
PV_AFTER = 1
O_STEPS = (4, 2)


def program(nc, x, w_qkv1, w_o1, b_o, ln1_w, ln1_b, w_qkv2, w_o2, ln2_w, ln2_b, gate_w, gate_b,
            w1, w2, cos_t, sin_t, head_sum, ident, route_consts, out):
    ctx = ExitStack()
    with ctx:
        def sb(name, shape, dt=FP32):
            return ctx.enter_context(nc.sbuf_tensor(name, shape, dt))

        sems = {}

        def sem(name):
            if name not in sems:
                sems[name] = ctx.enter_context(nc.semaphore(name))
            return sems[name]

        def dram(name, shape, dt=FP32):
            return nc.dram_tensor(name, shape, dt).ap()

        x1_dram = dram("x1_dram", [BATCH, T, D])
        h1_dram = dram("h1_dram", [BATCH, T, D])
        rows_dram = dram("rows_dram", [E * ROOM + P, ROW])
        out_rows = dram("out_rows", [BATCH * T + P, D])

        psum = [ctx.enter_context(nc.psum_tensor(f"bank{i}", [P, T], FP32)) for i in range(8)]
        ident_sb = sb("ident_sb", [P, P])
        ident_bf = sb("ident_bf", [P, P], BF16)
        head_sum_sb = sb("head_sum_sb", [P, P])
        cos_sb = sb("cos_sb", [P, T])
        sin_sb = sb("sin_sb", [P, T])
        wqkv_sb = sb("wqkv_sb", [P, 2, KD, 3 * D])
        wo_sb = sb("wo_sb", [P, 2, KD, D])
        rows_sb = sb("rows_sb", [P, 5, D])
        gate_w_sb = sb("gate_w_sb", [P, KD, E])
        gate_b_sb = sb("gate_b_sb", [P, E])
        eps_sb = sb("eps_sb", [P, 2])
        logits = sb("logits", [P, TT, E])

        def carve(space, pieces):
            at, got = 0, []
            for dims, shape, dt in pieces:
                n = int(np.prod(list(shape.values()))) * (1 if dt == FP32 else 2) // (
                    1 if dt == FP32 else 4)
                piece = space[:, at:at + n]
                if dt != FP32:
                    piece = piece.bitcast(dt)
                got.append(piece.rearrange(f"p ({dims}) -> p {dims}", **shape))
                at += n
            assert at <= space.shape[1], (at, space.shape)
            return got

        w1_space = sb("w1_space", [P, E * KD * F])
        w2_space = sb("w2_space", [P, E * KF * D])
        work_space = sb("work_space", [P, 7680])
        q_stack, k_stack = carve(w1_space, [("s h t", dict(s=2, h=H, t=T), BF16)] * 2)
        v_aug, probs, oT, trig, rest = carve(w2_space, [
            ("s t h e", dict(s=2, t=TT, h=H, e=VW), FP32),
            ("s j t", dict(s=2, j=HEADS_AT_ONCE, t=T), FP32),
            ("s g t", dict(s=2, g=GROUPS, t=T), FP32),
            ("n t", dict(n=4, t=T), FP32),
            ("a c t", dict(a=2, c=2, t=T), FP32)])
        x_sb, res_sb, xT, sq, rs, parts = carve(work_space, [
            ("t d", dict(t=TT, d=D), FP32), ("t d", dict(t=TT, d=D), FP32),
            ("k t", dict(k=KD, t=T), FP32), ("c t", dict(c=2, t=T), FP32),
            ("a t", dict(a=1, t=T), FP32),
            ("a n c t", dict(a=2, n=3, c=2, t=T), BF16)])
        rs = rs[:, 0, :]
        (w1_sb,) = carve(w1_space, [("e k f", dict(e=E, k=KD, f=F), FP32)])
        (w2_sb,) = carve(w2_space, [("e k d", dict(e=E, k=KF, d=D), FP32)])
        xs_sb, xsT, hid, hidT, rest_sb, z_sb, o_sb, by_tile = carve(work_space, [
            ("s d", dict(s=2, d=D), FP32), ("s k t", dict(s=2, k=KD, t=P), FP32),
            ("s f", dict(s=2, f=F), FP32), ("s k t", dict(s=2, k=KF, t=P), FP32),
            ("s d", dict(s=2, d=ROW - D), FP32), ("s d", dict(s=2, d=D), FP32),
            ("s d", dict(s=2, d=D), FP32), ("n t e", dict(n=3, t=TILES, e=E), FP32)])
        past, began, row_at = (by_tile[0:1, n, :, :] for n in range(3))

        route_c = sb("route_c", [P, P + E + (E + 1) + TILES + TT + 1])
        at = np.cumsum([P, E, E + 1, TILES, TT, 1])
        rank_c, room_c, tile_c, tok_c, pad_c = (
            route_c[:, lo:hi] for lo, hi in zip(at[:-1].tolist(), at[1:].tolist()))
        ones_sb = sb("ones_sb", [P, max(TILES, E)])
        ones_bf = sb("ones_bf", [P, P], BF16)
        earlier_bf = sb("earlier_bf", [P, P], BF16)
        top = sb("top", [P, TT])
        first_best = sb("first_best", [P, TT, E])
        one_hot = sb("one_hot", [P, TT + 1, E], BF16)
        slot3 = sb("slot3", [P, TT, E])
        next_row = sb("next_row", [P, E + 1])
        token = sb("token", [P, TT])
        slot_f = sb("slot_f", [P, TT])
        slot_u = sb("slot_u", [P, TT], U32)
        counts = sb("counts", [1, E])
        counts_i = sb("counts_i", [1, E], I32)
        n_tiles = sb("n_tiles", [1, E])
        tile_end = sb("tile_end", [1, E])
        tile_start = sb("tile_start", [1, E])
        tile_e_f = sb("tile_e_f", [1, TILES])
        tile_at = sb("tile_at", [1, TILES])
        tile_expert = sb("tile_expert", [1, TILES], I32)
        tile_row = sb("tile_row", [1, TILES], I32)
        row_sb = sb("row_sb", [P, TT, ROW])
        hn = row_sb[:, :, 0:D]

        weights_in = [sem("w1_in"), sem("w2_in")]
        route_step = sem("route_step")
        one_hot_ready = sem("one_hot_ready")
        slots_ready = sem("slots_ready")
        dispatched = sem("dispatched")
        rows_free = sem("rows_free")
        pad_set = sem("pad_set")
        tiles_ready = sem("tiles_ready")
        padded = sem("padded")
        xs_in = [sem("xs_in0"), sem("xs_in1")]
        rest_in = [sem("rest_in0"), sem("rest_in1")]
        xs_T = sem("xs_T")
        xsT_ready = sem("xsT_ready")
        up_done = sem("up_done")
        gelu_done = sem("gelu_done")
        hid_T = sem("hid_T")
        hidT_ready = sem("hidT_ready")
        down_done = sem("down_done")
        sum_done = sem("sum_done")
        last_stats = sem("last_stats")
        last_mv = sem("last_mv")
        last_ln = sem("last_ln")
        last_rstd = sem("last_rstd")
        out_ready = sem("out_ready")
        out_stored = [sem("out_stored0"), sem("out_stored1")]
        out_done = sem("out_done")

        recip = sb("recip", [P, H])
        on = sb("on", [P, 2, D])
        onT = sb("onT", [P, 2, KD, P])
        y = sb("y", [P, 2, D])
        xo = sb("xo", [P, 2, D])
        stats = sb("stats", [P, 6])
        mv = sb("mv", [P, 2, 2, 2])
        rstd = sb("rstd", [P, 2, 2])
        wait_cell = sb("wait_cell", [P, 1])
        pool_cell = sb("pool_cell", [P, 2])
        negm = sb("negm", [P, TT, HEADS_AT_ONCE])
        neg_rest = sb("neg_rest", [P, TT, HEADS_AT_ONCE])
        neg_parts = sb("neg_parts", [P, TT, NEG, HEADS_AT_ONCE], BF16)
        neg_T = sb("neg_T", [NEG * HEADS_AT_ONCE, T], BF16)

        consts_in = sem("consts_in")
        later_in = sem("later_in")
        consts_set = sem("consts_set")
        pool_set = sem("pool_set")
        layer_a = Layer(0, sem, psum)
        layer_b = Layer(1, sem, psum, layer_a)
        N_FIRST, N_LATER, N_CONST_OPS = 7, 12, 4
        PARTS_OF = (("qA", "qB"), ("kA", "kB"))

        def tiles(ap, b):
            return ap[bass.ds(b, 1), :, :].rearrange("a (t p) d -> p (a t) d", p=P)

        def tile_of(ap, b, t):
            return ap[bass.ds(b, 1), t * P:(t + 1) * P, :].rearrange("a p d -> (a p) d")

        def pipeline(eng, body):
            def of(L):
                return lambda b: (L, b)

            a, b = of(layer_a), of(layer_b)
            body(0, a(0), None, None)
            body(1, a(1), a(0), None)
            with eng.Fori(1, BATCH // 2) as pair:
                body(0, a(2 * pair), a(2 * pair - 1), a(2 * pair - 2))
                body(1, a(2 * pair + 1), a(2 * pair), a(2 * pair - 1))
            n = BATCH
            body(0, b(n), a(n - 1), a(n - 2))
            body(1, b(n + 1), b(n), a(n - 1))
            with eng.Fori(1, BATCH // 2) as pair:
                body(0, b(2 * pair + n), b(2 * pair + (n - 1)), b(2 * pair + (n - 2)))
                body(1, b(2 * pair + (n + 1)), b(2 * pair + n), b(2 * pair + (n - 1)))
            body(0, None, b(2 * n - 1), b(2 * n - 2))
            body(1, None, None, b(2 * n - 1))

        def outer_tasks(slot, par, projected, finished, task):
            if finished:
                L, b = finished
                for name in L.o_tasks.get(slot, []):
                    task(L, name, b, par)
            if projected:
                L, b = projected
                for name in L.p_tasks.get(slot, []):
                    task(L, name, b, par)

        def max_tiles(q, par, projected, attended):
            at = q - (QUADS - MAX_LEAD)
            of, at, s = (projected, at, par) if at >= 0 else (attended, at + QUADS, 1 - par)
            return [] if not of or not of[0].second else [
                (*of, at // TT, HEADS_AT_ONCE * (at % TT) + j, s) for j in range(HEADS_AT_ONCE)]

        def neg_group(q, par, projected, attended):
            at = q - (QUADS - MAX_LEAD)
            of, at, s = (projected, at, par) if at > 0 else (attended, at + QUADS, 1 - par)
            return [] if not of or not of[0].second or at % TT else [(*of, at // TT - 1, s)]

        def norms(L, b):
            return (2 - L.number) * TT * (b - L.first) + 2 * TT * L.first

        def o_steps(L, b):
            return O_STEPS[L.number] * TT * (b - L.first) + O_STEPS[0] * TT * L.first

        def half_of(name):
            return "qk".index(name[0]), "AB".index(name[1])

        def v_out(eng, ops, L, name, b, s):
            j, p = int(name[1]), L.p_ring
            eng.wait_ge(*p.full(b, name))
            if not isinstance(b, int) or b >= 2:
                eng.wait_ge(L.pv_done, QUADS * (b - 2) + QUADS)
            dst = v_aug[:, s, 2 * j:2 * j + 2, :, 0:HD]
            src = p.bank(name)[:, :].rearrange("p (t h e) -> p t h e", t=2, h=H)
            if ops is nc.scalar:
                last = nc.scalar.activation(dst, src, ACT.Copy)
            else:
                last = nc.vector.tensor_copy(dst, src)
            last.then_inc(p.drain_sem(name), 1)

        block = ctx.enter_context(nc.Block())

        @block.tensor
        def _(pe):
            pe.wait_ge(consts_in, 16 * N_FIRST)
            pe.wait_ge(consts_set, N_CONST_OPS)

            def score(L, b, s, c):
                q, j = c // HEADS_AT_ONCE, c % HEADS_AT_ONCE
                g, kt = q // TT, q % TT
                h, n = HEADS_AT_ONCE * g + j, len(L.st_banks)
                if c == 0:
                    for arrived in L.stack_in:
                        pe.wait_ge(arrived, 16 * STACK_DMAS * b + 16 * STACK_DMAS)
                if L.second and j == 0 and kt == 0:
                    pe.wait_ge(L.neg_in, 16 * GROUPS * (b - L.first) + 16 * (g + 1))
                wait(pe, L.exps, CHUNKS * b + (c + 1 - n if CHUNKS % n == 0 or c else 0))
                nc.tensor.matmul(L.st_banks[c % n][:, :],
                                 k_stack[0:L.rows, s, h, kt * P:(kt + 1) * P],
                                 q_stack[0:L.rows, s, h, :], start=True, stop=True
                                 ).then_inc(L.scores, 1)

            def pv(L, b, s, q):
                g, kt, n = q // TT, q % TT, len(L.pv_banks)
                pe.wait_ge(L.exps, CHUNKS * b + HEADS_AT_ONCE * (q + 1))
                if q == 0:
                    all_empty(pe, L.p_ring, b, ("V0", "V1"))
                if kt == 0:
                    wait(pe, L.oT_ready, GROUPS * b + (g + 1 - n))
                for j in range(HEADS_AT_ONCE):
                    last = nc.tensor.matmul(L.pv_banks[g % n][VW * j:VW * (j + 1), :],
                                            v_aug[:, s, kt, HEADS_AT_ONCE * g + j, :],
                                            probs[:, q % 2, j, :],
                                            start=(kt == 0), stop=(kt == TT - 1))
                last.then_inc(L.pv_done, 1)

            def max_score(L, b, g, c, s):
                use, h, qt = ("MX", g, c), HEADS_AT_ONCE * g + c // TT, c % TT
                if g == 0 and c == 0:
                    for arrived in L.stack_in:
                        pe.wait_ge(arrived, 16 * STACK_DMAS * b + 16 * STACK_DMAS)
                wait(pe, *L.mx_ring.free(b, use))
                nc.tensor.matmul(L.mx_ring.bank(use)[:, :],
                                 q_stack[0:STACK, s, h, qt * P:(qt + 1) * P],
                                 k_stack[0:STACK, s, h, :], start=True, stop=True
                                 ).then_inc(L.mx_ring.filled, 1)

            def neg_rows(L, b, g):
                pe.wait_ge(L.neg_ready, GROUPS * (b - L.first) + (g + 1))
                wait(pe, *L.mx_ring.free(b, ("NG", g)))
                rows = L.mx_ring.bank(("NG", g))[0:NEG * HEADS_AT_ONCE, 0:T // 2].bitcast(BF16)
                for qt in range(TT):
                    last = nc.tensor.transpose(rows[:, qt * P:(qt + 1) * P],
                                               neg_parts[:, qt, :, :].rearrange("p a h -> p (a h)"),
                                               ident_bf[:, :])
                last.then_inc(L.mx_ring.filled, 1)

            def task(L, name, b, s):
                kind, t = name[:2], name[-1]
                if kind[0] in "Nmsuhl":
                    return
                ring = L.p_ring if name in L.p_ring.order else L.o_ring
                bank = ring.bank(name)
                if not (name == "qA" and len(ring.banks) > 1):
                    wait(pe, *ring.free(b, name))
                if name in ("T0", "T1"):
                    pe.wait_ge(L.x_in, 16 * b + 16)
                    for j in range(TT):
                        last = nc.tensor.transpose(bank[:, j * P:(j + 1) * P],
                                                   x_sb[:, j, int(t) * P:(int(t) + 1) * P],
                                                   ident_sb[:, :])
                elif name in ("qA", "qB", "kA", "kB"):
                    if name == "qA" and len(ring.banks) > 1:
                        all_empty(pe, ring, b, ("T0", "T1"))
                    c = ("qA", "qB", "kA", "kB").index(name)
                    for k in range(KD):
                        last = nc.tensor.matmul(bank[:, :],
                                                wqkv_sb[:, L.number, k, c * P:(c + 1) * P],
                                                xT[:, k, :], start=(k == 0), stop=(k == KD - 1))
                elif name in ("nq", "nk"):
                    pe.wait_ge(L.sq_done, 2 * b + (1 if name == "nq" else 2))
                    for k in range(2):
                        last = nc.tensor.matmul(bank[:, :], head_sum_sb[:, :], sq[:, k, :],
                                                start=(k == 0), stop=(k == 1))
                elif kind[0] == "V":
                    for j in range(2):
                        tt = 2 * int(t) + j
                        for k in range(KD):
                            last = nc.tensor.matmul(bank[:, j * D:(j + 1) * D],
                                                    xT[:, k, tt * P:(tt + 1) * P],
                                                    wqkv_sb[:, L.number, k, 2 * D:3 * D],
                                                    start=(k == 0), stop=(k == KD - 1))
                elif kind == "TO":
                    t = int(t)
                    if t == 0:
                        pe.wait_ge(L.oT_ready, GROUPS * b + GROUPS)
                    for g in range(GROUPS):
                        last = nc.tensor.transpose(bank[:, g * P:(g + 1) * P],
                                                   oT[:, s, g, t * P:(t + 1) * P], ident_sb[:, :])
                elif kind == "TP":
                    t = int(t)
                    pe.wait_ge(*ring.empty(b, f"TO{t}"))
                    for k in range(KD):
                        last = nc.tensor.transpose(bank[:, k * P:(k + 1) * P],
                                                   on[:, t % 2, k * P:(k + 1) * P], ident_sb[:, :])
                elif kind == "WO":
                    t = int(t)
                    pe.wait_ge(*ring.empty(b, f"TP{t}"))
                    for k in range(KD):
                        last = nc.tensor.matmul(bank[:, 0:D], onT[:, t % 2, k, :],
                                                wo_sb[:, L.number, k, :],
                                                start=(k == 0), stop=(k == KD - 1))
                elif kind == "HT":
                    t = int(t)
                    pe.wait_ge(L.h_ready, TT * b + (t + 1))
                    for k in range(KD):
                        last = nc.tensor.transpose(bank[:, k * P:(k + 1) * P],
                                                   hn[:, t, k * P:(k + 1) * P], ident_sb[:, :])
                elif kind == "GT":
                    t = int(t)
                    pe.wait_ge(*ring.empty(b, f"HT{t}"))
                    for k in range(KD):
                        last = nc.tensor.matmul(bank[:, 0:E], onT[:, t % 2, k, :],
                                                gate_w_sb[:, k, :],
                                                start=(k == 0), stop=(k == KD - 1))
                elif name == "RT":
                    pe.wait_ge(one_hot_ready, b - L.first + 1)
                    for back in range(TT + 1):
                        last = nc.tensor.matmul(
                            bank[:, back * E:(TT + 1) * E],
                            ones_bf[:, :] if back else earlier_bf[:, :],
                            one_hot[:, 0:TT + 1 - back, :].rearrange("p t e -> p (t e)"),
                            start=(back == 0), stop=(back == TT))
                last.then_inc(ring.filled, 1)

            def body(par, projected, attended, finished):
                if attended and not finished:
                    pe.wait_ge(later_in, 16 * N_LATER)
                    pe.wait_ge(pool_set, 3)
                for q in range(QUADS):
                    mx = max_tiles(q, par, projected, attended)
                    groups = neg_group(q, par, projected, attended)
                    late = []
                    for j in range(HEADS_AT_ONCE):
                        if attended:
                            score(*attended, 1 - par, HEADS_AT_ONCE * q + j)
                        late += mx[j:j + 1]
                        if j == PV_AFTER:
                            if q == 0 and finished:
                                pv(*finished, par, QUADS - 1)
                            if q and attended:
                                pv(*attended, 1 - par, q - 1)
                            for L, b, g, s in groups:
                                neg_rows(L, b, g)
                            groups = []
                        if not groups:
                            for tile in late:
                                max_score(*tile)
                            late = []
                        outer_tasks((q, j), par, projected, finished, task)

            pipeline(pe, body)

            pe.wait_ge(tiles_ready, 1)
            for arrived in weights_in:
                pe.wait_ge(arrived, 16 * E)

            def expert_of(j):
                return pe.value_load(tile_expert[0:1, bass.ds(j, 1)], min_val=0, max_val=E - 1)

            def transpose_in(j, s):
                pe.wait_ge(xs_in[s], 8 * (j - s) + 16)
                wait(pe, xsT_ready, j)
                for k in range(KD):
                    last = nc.tensor.transpose(psum[4][:, k * P:(k + 1) * P],
                                               xs_sb[:, s, k * P:(k + 1) * P], ident_sb[:, :])
                last.then_inc(xs_T, 1)

            def up(j, s, e):
                pe.wait_ge(xsT_ready, j + 1)
                for n in range(2):
                    wait(pe, gelu_done, 2 * j + (n - 1))
                    for k in range(KD):
                        last = nc.tensor.matmul(
                            psum[n][:, :], xsT[:, s, k, :],
                            w1_sb[:, bass.ds(e, 1), k, n * T:(n + 1) * T].rearrange(
                                "p a f -> p (a f)"),
                            start=(k == 0), stop=(k == KD - 1))
                    last.then_inc(up_done, 1)

            def transpose_hidden(j, s):
                for n in range(2):
                    pe.wait_ge(gelu_done, 2 * j + (n + 1))
                    wait(pe, hidT_ready, 2 * j + (n - 1))
                    for k in range(KF // 2):
                        at = n * T + k * P
                        last = nc.tensor.transpose(psum[2 + n][:, k * P:(k + 1) * P],
                                                   hid[:, s, at:at + P], ident_sb[:, :])
                    last.then_inc(hid_T, 1)

            def down(j, s, e):
                pe.wait_ge(hidT_ready, 2 * j + 2)
                wait(pe, sum_done, j)
                for k in range(KF):
                    last = nc.tensor.matmul(
                        psum[5][:, 0:D], hidT[:, s, k, :],
                        w2_sb[:, bass.ds(e, 1), k, :].rearrange("p a d -> p (a d)"),
                        start=(k == 0), stop=(k == KF - 1))
                last.then_inc(down_done, 1)

            def expert_body(j, s, ends=False):
                this, last = expert_of(j), expert_of(j - 1)
                transpose_hidden(j - 1, 1 - s)
                up(j, s, this)
                if not ends:
                    transpose_in(j + 1, 1 - s)
                down(j - 1, 1 - s, last)

            transpose_in(0, 0)
            up(0, 0, expert_of(0))
            transpose_in(1, 1)
            expert_body(1, 1)
            expert_body(2, 0)
            with pe.Fori(1, TILES // 2 - 1) as pair:
                expert_body(2 * pair + 1, 1)
                expert_body(2 * pair + 2, 0)
            expert_body(TILES - 2, 1)
            expert_body(TILES - 1, 0, ends=True)
            transpose_hidden(TILES - 1, 0)
            down(TILES - 1, 0, expert_of(TILES - 1))

        @block.scalar
        def _(act):
            nc.scalar.preload_act_table_set("natural_log_exp_and_others")

            def exp(L, b, c):
                q, j = c // HEADS_AT_ONCE, c % HEADS_AT_ONCE
                act.wait_ge(L.scores, CHUNKS * b + (c + 1))
                if j == 0:
                    wait(act, L.pv_done, QUADS * b + (q - 1))
                nc.scalar.activation(probs[:, q % 2, j, :], L.st_banks[c % len(L.st_banks)][:, :],
                                     ACT.Exp, scale=SCALE).then_inc(L.exps, 1)

            def group_out(L, b, s, g):
                act.wait_ge(L.pv_done, QUADS * b + TT * (g + 1))
                nc.scalar.activation(oT[:, s, g, :], L.pv_banks[g % len(L.pv_banks)][:, :], ACT.Copy
                                     ).then_inc(L.oT_ready, 1)

            def neg_rows(L, b, g):
                act.wait_ge(*L.mx_ring.full(b, ("NG", g)))
                wait(act, L.neg_in, 16 * GROUPS * (b - L.first) + 16 * g)
                nc.scalar.activation(neg_T[:, :],
                                     L.mx_ring.bank(("NG", g))[0:NEG * HEADS_AT_ONCE, 0:T // 2]
                                     .bitcast(BF16), ACT.Copy
                                     ).then_inc(L.mx_ring.drain_sem(("NG", g)), 1)

            def task(L, name, b, s):
                kind, t = name[:2], name[-1]
                p, o = L.p_ring, L.o_ring
                if name in ("T0", "T1") and L.second:
                    act.wait_ge(*p.full(b, name))
                    nc.scalar.activation(xT[:, int(t), :], p.bank(name)[:, :], ACT.Copy
                                         ).then_inc(p.drain_sem(name), 1)
                elif name in ("qA", "qB", "kA", "kB") and L.second:
                    qk, half = half_of(name)
                    act.wait_ge(*p.full(b, name))
                    wait(act, L.stack_in[qk], 16 * STACK_DMAS * b)
                    nc.scalar.activation(parts[:, qk, 0, half, :], p.bank(name)[:, :], ACT.Copy
                                         ).then_inc(L.high_done, 1)
                elif name in ("sq", "sk"):
                    qk = "qk".index(name[1])
                    act.wait_ge(L.rot_done, 2 * b + (qk + 1))
                    if qk:
                        act.wait_ge(*p.full(b, "nq"))
                    elif not isinstance(b, int) or b >= 1:
                        act.wait_ge(*p.full(b - 1, "nk"))
                    nc.scalar.activation(sq[:, :, :], rest[:, qk, :, :], ACT.Square
                                         ).then_inc(L.sq_done, 1)
                elif name in ("nq", "nk"):
                    n = "qk".index(name[1])
                    act.wait_ge(*p.full(b, name))
                    wait(act, L.p_step, 2 * SPLIT_STEPS * b + (SPLIT_STEPS * (n - 1) + 2))
                    nc.scalar.activation(rs[:, :], p.bank(name)[:, :], ACT.Ln,
                                         bias=eps_sb[:, 1:2]).then_inc(p.drain_sem(name), 1)
                    act.wait_ge(*p.empty(b, name))
                    nc.scalar.activation(rs[:, :], rs[:, :], ACT.Exp, scale=-0.5
                                         ).then_inc(L.rs_ready, 1)
                elif name in ("mq", "mk"):
                    qk = "qk".index(name[1])
                    all_empty(act, p, b, PARTS_OF[qk])
                    nc.scalar.activation(parts[:, qk, 1, :, :], rest[:, qk, :, :], ACT.Copy
                                         ).then_inc(L.mid_done, 1)
                elif kind[0] == "V" and L.second:
                    v_out(act, nc.scalar, L, name, b, s)
                elif kind in ("TP", "HT"):
                    act.wait_ge(*o.full(b, name))
                    nc.scalar.activation(onT[:, int(t) % 2, :, :].rearrange("p k c -> p (k c)"),
                                         o.bank(name)[:, 0:D], ACT.Copy
                                         ).then_inc(o.drain_sem(name), 1)
                elif kind[0] == "N":
                    t = int(t)
                    n = norms(L, b) + (t + 1 if L.second else 2 * t + int(kind[1]))
                    which = int(kind[1]) - 1
                    r = rstd[:, t % 2, which:which + 1]
                    act.wait_ge(L.mv_ready, n)
                    nc.scalar.activation(r, mv[:, t % 2, which, 1:2], ACT.Ln, bias=eps_sb[:, 0:1]
                                         ).then_inc(L.rstd_step, 1)
                    act.wait_ge(L.rstd_step, n)
                    nc.scalar.activation(r, r, ACT.Exp, scale=-0.5).then_inc(L.rstd_ready, 1)

            def load_weights(which, experts, free):
                for f in free:
                    act.wait_ge(*f)
                for e in experts:
                    dst, src = ((w1_sb, w1), (w2_sb, w2))[which]
                    act.dma_start(dst[:, e, :, :], src[e].rearrange("(k p) f -> p k f", p=P)
                                  ).then_inc(weights_in[which], 16)

            def body(par, projected, attended, finished):
                if projected:
                    L, b = projected
                    if not isinstance(b, int) or b >= 1:
                        act.wait_ge(*L.p_ring.full(b - 1, "T1"))
                    if L.second:
                        stored = b - 2 if isinstance(b, int) else BATCH
                        for h_out in L.h_out:
                            act.wait_ge(h_out, 8 * TT * stored + 16)
                    act.dma_start(x_sb[:, :, :], tiles(h1_dram if L.second else x, b - L.first)
                                  ).then_inc(L.x_in, 16)
                    if isinstance(b, int) and b == 0:
                        act.wait_ge(consts_set, N_CONST_OPS)
                if finished:
                    L, b = finished
                    if L.second:
                        act.wait_ge(L.o_ring.drained[0], L.o_ring.base + 1)
                        for x_out in L.x_out:
                            act.wait_ge(x_out, 8 * TT * BATCH + 16)
                        act.wait_ge(L.sum_ready, TT * (b - L.first) + 2)
                    elif not isinstance(b, int) or b >= 1:
                        act.wait_ge(*L.o_ring.empty(b - 1, f"WO{TT - 1}"))
                    act.dma_start(res_sb[:, :, :], tiles(x1_dram if L.second else x, b - L.first)
                                  ).then_inc(L.res_in, 16)
                lag_of = attended[0].number if attended else projected[0].number if projected else 1
                for q in range(QUADS):
                    if not projected and attended and q in (3, 7, 11):
                        which, experts = {3: (0, (0, 1)), 7: (0, (4, 5)), 11: (1, (6, 7))}[q]
                        load_weights(which, experts, [(layer_b.scores, CHUNKS * (2 * BATCH - 1)),
                                                      (layer_b.parts_ready, 2 * 2 * BATCH)])
                    if q == 6 and not projected and not attended:
                        load_weights(0, (2, 3, 6, 7), [(layer_b.scores, CHUNKS * 2 * BATCH),
                                                       (dispatched, 16 * TT * (BATCH - 1))])
                        load_weights(1, (0, 1, 2, 3, 4), [
                            (layer_b.pv_done, QUADS * 2 * BATCH),
                            layer_b.o_ring.full(2 * BATCH - 2, f"TO{TT - 1}")])
                    for j in range(HEADS_AT_ONCE):
                        if attended:
                            exp(*attended, HEADS_AT_ONCE * q + j)
                        if j == 1:
                            for L, b, g, s in neg_group(q, par, projected, attended):
                                neg_rows(L, b, g)
                        if j == 2 and q == 0 and finished:
                            group_out(*finished, par, GROUPS - 1)
                        if j == 2 and q and q % TT == 0 and attended:
                            group_out(*attended, 1 - par, q // TT - 1)
                        outer_tasks((q, j - ACT_LAG[lag_of]), par, projected, finished, task)

            pipeline(act, body)
            load_weights(1, (5,), [layer_b.o_ring.full(2 * BATCH - 1, f"TO{TT - 1}")])

            def gelu(j, s):
                for n in range(2):
                    act.wait_ge(up_done, 2 * j + (n + 1))
                    if n == 0:
                        wait(act, hid_T, 2 * j - 2)
                    nc.scalar.activation(hid[:, s, n * T:(n + 1) * T], psum[n][:, :],
                                         ACT.Gelu_apprx_tanh).then_inc(gelu_done, 1)

            def last_norm(j, s):
                r = rstd[:, s, 0:1]
                act.wait_ge(last_mv, j + 1)
                nc.scalar.activation(r, mv[:, s, 0, 1:2], ACT.Ln, bias=eps_sb[:, 0:1]
                                     ).then_inc(last_ln, 1)
                act.wait_ge(last_ln, j + 1)
                nc.scalar.activation(r, r, ACT.Exp, scale=-0.5).then_inc(last_rstd, 1)

            gelu(0, 0)
            gelu(1, 1)
            last_norm(0, 0)
            gelu(2, 0)
            last_norm(1, 1)
            with act.Fori(1, TILES // 2) as pair:
                gelu(2 * pair + 1, 1)
                last_norm(2 * pair, 0)
                gelu(2 * pair + 2, 0)
                last_norm(2 * pair + 1, 1)
            last_norm(TILES - 1, 0)

        @block.vector
        def _(dve):
            ve = nc.vector
            dve.wait_ge(consts_in, 16 * N_FIRST)
            ve.tensor_copy(ident_bf[:, :], ident_sb[:, :]).then_inc(consts_set, 1)
            ve.tensor_copy(row_sb[:, 0, 2 * D:ROW].bitcast(U32), pad_c
                           ).then_inc(pad_set, 1)
            ve.memset(eps_sb[:, 0:1], EPS).then_inc(consts_set, 1)
            ve.memset(eps_sb[:, 1:2], 1e-6).then_inc(consts_set, 1)
            ve.memset(ones_sb[:, :], 1.0)
            ve.memset(one_hot[:, TT, :], 0.0)
            ve.memset(ones_bf[:, :], 1.0).then_inc(consts_set, 1)

            def max_tile(L, b, g, c, s):
                use = ("MX", g, c)
                dve.wait_ge(*L.mx_ring.full(b, use))
                ve.tensor_reduce(negm[:, c % TT, c // TT:c // TT + 1], L.mx_ring.bank(use)[:, :],
                                 axis=AX.X, op=ALU.max, negate=True
                                 ).then_inc(L.mx_ring.drain_sem(use), 1)

            def neg_split(L, b, g):
                last_tile = HEADS_AT_ONCE * TT - 1
                dve.wait_ge(*L.mx_ring.empty(b, ("MX", g, last_tile - 1)))
                dve.wait_ge(*L.mx_ring.empty(b, ("MX", g, last_tile)))
                if g:
                    dve.wait_ge(*L.mx_ring.full(b, ("NG", g - 1)))
                elif not isinstance(b, int) or b > L.first:
                    dve.wait_ge(*L.mx_ring.full(b - 1, ("NG", GROUPS - 1)))
                n = 3 * GROUPS * (b - L.first)
                ve.tensor_copy(neg_parts[:, :, 0, :], negm[:, :, :]).then_inc(L.neg_step, 1)
                dve.wait_ge(L.neg_step, n + (3 * g + 1))
                ve.tensor_tensor(neg_rest[:, :, :], negm[:, :, :], neg_parts[:, :, 0, :],
                                 ALU.subtract).then_inc(L.neg_step, 1)
                dve.wait_ge(L.neg_step, n + (3 * g + 2))
                ve.tensor_copy(neg_parts[:, :, 1, :], neg_rest[:, :, :]).then_inc(L.neg_step, 1)
                dve.wait_ge(L.neg_step, n + (3 * g + 3))
                ve.tensor_tensor(neg_parts[:, :, 2, :], neg_rest[:, :, :], neg_parts[:, :, 1, :],
                                 ALU.subtract).then_inc(L.neg_ready, 1)

            def norm_and_split(L, name, b):
                qk = "qk".index(name[1])
                n = 2 * SPLIT_STEPS * b + SPLIT_STEPS * qk
                if name[0] == "u":
                    dve.wait_ge(L.rs_ready, 2 * b + (qk + 1))
                    for half in range(2):
                        ve.tensor_tensor(rest[:, qk, half, :], rest[:, qk, half, :], rs[:, :],
                                         ALU.mult).then_inc(L.p_step, 1)
                elif name[0] == "h":
                    wait(dve, L.stack_in[qk], 16 * STACK_DMAS * b)
                    for half in range(2):
                        dve.wait_ge(L.p_step, n + (1 + half))
                        ve.tensor_copy(parts[:, qk, 0, half, :], rest[:, qk, half, :]
                                       ).then_inc(L.p_step, 1)
                    for half in range(2):
                        dve.wait_ge(L.p_step, n + (3 + half))
                        ve.tensor_tensor(rest[:, qk, half, :], rest[:, qk, half, :],
                                         parts[:, qk, 0, half, :], ALU.subtract
                                         ).then_inc(L.p_step, 1)
                else:
                    for half in range(2):
                        dve.wait_ge(L.p_step, n + (5 + half))
                        ve.tensor_copy(parts[:, qk, 1, half, :], rest[:, qk, half, :]
                                       ).then_inc(L.mid_done if half else L.p_step, 1)

            def routing_step(b, k, op):
                op.then_inc(route_step, 1)
                dve.wait_ge(route_step, ROUTE_STEPS * b + k)

            def over(ap, n):
                return ap.unsqueeze(1).to_broadcast([P, n, E])

            def one_hots(b):
                over_e = lambda ap: ap.unsqueeze(2).to_broadcast([P, TT, E])
                routing_step(b, 1, ve.tensor_reduce(top[:, :], logits[:, :, :], axis=AX.X,
                                                    op=ALU.max))
                routing_step(b, 2, ve.tensor_tensor(first_best[:, :, :], logits[:, :, :],
                                                    over_e(top[:, :]), ALU.is_equal))
                routing_step(b, 3, ve.tensor_tensor(first_best[:, :, :], first_best[:, :, :],
                                                    over(rank_c, TT), ALU.mult))
                routing_step(b, 4, ve.tensor_reduce(top[:, :], first_best[:, :, :], axis=AX.X,
                                                    op=ALU.max))
                ve.tensor_tensor(one_hot[:, 0:TT, :], first_best[:, :, :], over_e(top[:, :]),
                                 ALU.is_equal).then_inc(one_hot_ready, 1)

            def rows_of_tokens(L, b, own):
                ring = L.o_ring
                sums = ring.bank("RT")
                dve.wait_ge(*ring.full(b, "RT"))
                dve.wait_ge(rows_free, own + 1)
                ve.tensor_copy(row_sb[:, :, 2 * D].bitcast(U32), token[:, :]
                               ).then_inc(route_step, 1)
                routing_step(own, 6, ve.tensor_tensor(
                    slot3[:, :, :], sums[:, 0:TT * E].rearrange("p (t e) -> p t e", t=TT),
                    over(next_row[:, 0:E], TT), ALU.add))
                ve.tensor_tensor(next_row[:, 0:E], next_row[:, 0:E], sums[:, TT * E:(TT + 1) * E],
                                 ALU.add).then_inc(ring.drain_sem("RT"), 1)
                ve.tensor_scalar(token[:, :], token[:, :], float(T), None, ALU.add
                                 ).then_inc(route_step, 1)
                routing_step(own, 8, ve.tensor_tensor(slot3[:, :, :], slot3[:, :, :],
                                                    one_hot[:, 0:TT, :], ALU.mult))
                routing_step(own, 9, ve.tensor_reduce(slot_f[:, :], slot3[:, :, :], axis=AX.X,
                                                    op=ALU.add))
                routing_step(own, 10, ve.tensor_copy(slot_u[:, :], slot_f[:, :]))
                dve.wait_ge(*ring.empty(b, "RT"))
                ve.memset(wait_cell[:, :], 0.0).then_inc(slots_ready, 1)

            def moments(L, n, src, dst):
                ve.bn_stats(stats[:, :], src).then_inc(L.o_step, 1)
                dve.wait_ge(L.o_step, n + 1)
                ve.memset(wait_cell[:, :], 0.0)
                ve.bn_aggr(dst, stats[:, :]).then_inc(L.mv_ready, 1)

            def task(L, name, b, s):
                kind, t = name[:2], name[-1]
                p, o = L.p_ring, L.o_ring
                if name in ("T0", "T1") and not L.second:
                    dve.wait_ge(*p.full(b, name))
                    ve.tensor_copy(xT[:, int(t), :], p.bank(name)[:, :]
                                   ).then_inc(p.drain_sem(name), 1)
                elif name in ("qA", "qB", "kA", "kB"):
                    qk, half = half_of(name)
                    if not L.second:
                        dve.wait_ge(*p.full(b, name))
                        wait(dve, L.rot_done, 2 * b + qk)
                        first, then = (sin_sb, cos_sb) if half else (cos_sb, sin_sb)
                        ve.tensor_tensor(trig[:, 2 * half, :], p.bank(name)[:, :], first[:, :],
                                         ALU.mult)
                        ve.tensor_tensor(trig[:, 2 * half + 1, :], p.bank(name)[:, :], then[:, :],
                                         ALU.mult).then_inc(p.drain_sem(name), 1)
                    else:
                        dve.wait_ge(L.high_done, 4 * (b - L.first) + (2 * qk + half + 1))
                        wait(dve, L.parts_ready, 2 * b + (qk - 1))
                        ve.tensor_tensor(rest[:, qk, half, :], p.bank(name)[:, :],
                                         parts[:, qk, 0, half, :], ALU.subtract
                                         ).then_inc(p.drain_sem(name), 1)
                elif kind[0] in "uhl":
                    norm_and_split(L, name, b)
                elif kind[0] == "V" and not L.second:
                    v_out(dve, nc.vector, L, name, b, s)
                elif kind == "TO":
                    t = int(t)
                    heads = o.bank(name)[:, :].rearrange("p (h e) -> p h e", h=H)
                    dve.wait_ge(*o.full(b, name))
                    ve.reciprocal(recip[:, :], heads[:, :, HD]).then_inc(L.o_step, 1)
                    dve.wait_ge(L.o_step, o_steps(L, b) + (O_STEPS[L.number] * t + 1))
                    ve.tensor_tensor(on[:, t % 2, :].rearrange("p (h e) -> p h e", h=H),
                                     heads[:, :, 0:HD],
                                     recip[:, :].unsqueeze(2).to_broadcast([P, H, HD]), ALU.mult
                                     ).then_inc(o.drain_sem(name), 1)
                elif kind == "WO":
                    t = int(t)
                    n = o_steps(L, b) + (O_STEPS[L.number] * t + 1)
                    dst = xo if L.second else y
                    dve.wait_ge(*o.full(b, name))
                    if t == 0:
                        if L.second:
                            dve.wait_ge(L.res_in, 16 * b + 16)
                        else:
                            dve.wait_ge(L.res_ready, b + 1)
                    if L.second:
                        dve.wait_ge(L.sum_ready, TT * (b - L.first) + (t + 1))
                        dve.wait_ge(L.x_out[t % 2], 8 * TT * BATCH + 16)
                    ve.tensor_tensor(dst[:, t % 2, :], o.bank(name)[:, 0:D], res_sb[:, t, :],
                                     ALU.add).then_inc(o.drain_sem(name), 1)
                    dve.wait_ge(*o.empty(b, name))
                    moments(L, n, dst[:, t % 2, :], mv[:, t % 2, 1 if L.second else 0, :])
                elif kind == "N1":
                    t = int(t)
                    n = o_steps(L, b) + (O_STEPS[L.number] * t + 2)
                    dve.wait_ge(L.rstd_ready, norms(L, b) + (2 * t + 1))
                    dve.wait_ge(L.x_out[t % 2], 8 * TT * b + (16 * (t // 2) + 16))
                    ve.tensor_scalar(xo[:, t % 2, :], y[:, t % 2, :], mv[:, t % 2, 0, 0:1],
                                     rstd[:, t % 2, 0:1], ALU.subtract, ALU.mult
                                     ).then_inc(L.o_step, 1)
                    dve.wait_ge(L.o_step, n + 1)
                    moments(L, n + 1, xo[:, t % 2, :], mv[:, t % 2, 1, :])
                elif kind == "N2":
                    t = int(t)
                    if L.second:
                        dve.wait_ge(L.rstd_ready, norms(L, b) + (t + 1))
                    else:
                        dve.wait_ge(L.rstd_ready, norms(L, b) + (2 * t + 2))
                    if L.second:
                        dve.wait_ge(rows_free, b - L.first + 1)
                        dve.wait_ge(L.h_out[t % 2], 8 * TT * BATCH + 16)
                    else:
                        dve.wait_ge(L.h_out[t % 2], 8 * TT * b + (16 * (t // 2) + 16))
                    ve.tensor_scalar(hn[:, t, :], xo[:, t % 2, :], mv[:, t % 2, 1, 0:1],
                                     rstd[:, t % 2, 1:2], ALU.subtract, ALU.mult
                                     ).then_inc(L.hn_ready, 1)
                elif kind == "GT":
                    t = int(t)
                    dve.wait_ge(*o.full(b, name))
                    ve.tensor_tensor(logits[:, t, :], o.bank(name)[:, 0:E], gate_b_sb[:, :],
                                     ALU.add).then_inc(o.drain_sem(name), 1)
                    if t == TT - 1:
                        dve.wait_ge(*o.empty(b, name))
                        one_hots(b - L.first)
                elif name == "RT":
                    rows_of_tokens(L, b, b - L.first)

            def body(par, projected, attended, finished):
                if attended and not finished:
                    dve.wait_ge(later_in, 16 * N_LATER)
                    ve.tensor_copy(earlier_bf[:, :], route_c[:, 0:P])
                    ve.tensor_copy(next_row[:, :], room_c)
                    ve.tensor_copy(token[:, :], tok_c)
                    dve.wait_ge(padded, 16 * (E + 1))
                lag_of = attended[0].number if attended else projected[0].number if projected else 1
                for q in range(QUADS):
                    mx = max_tiles(q, par, projected, attended)
                    for L, b, g, s in neg_group(q, par, projected, attended):
                        neg_split(L, b, g)
                    for j in range(HEADS_AT_ONCE):
                        if mx:
                            max_tile(*mx[j])
                        outer_tasks((q, j - DVE_LAG[lag_of]), par, projected, finished, task)

            pipeline(dve, body)

            step = lambda k, op: routing_step(BATCH, k, op)
            of_expert = lambda ap: ap.unsqueeze(1).to_broadcast([1, TILES, E])
            of_tile = lambda ap: ap.unsqueeze(2).to_broadcast([1, TILES, E])
            one = slice(0, 1)
            dve.wait_ge(*layer_b.o_ring.empty(2 * BATCH - 1, "RT"))
            step(1, ve.tensor_tensor(counts[:, :], next_row[one, 0:E], room_c[one, 0:E],
                                     ALU.subtract))
            step(2, ve.tensor_scalar(counts_i[:, :], counts[:, :], float(P - 1), None, ALU.add))
            step(3, ve.tensor_scalar(counts_i[:, :], counts_i[:, :], LOG_P, None,
                                     ALU.logical_shift_right))
            step(4, ve.tensor_copy(n_tiles[:, :], counts_i[:, :]))
            step(5, ve.tensor_tensor_scan(tile_end[:, :], ones_sb[one, 0:E], n_tiles[:, :], 0.0,
                                          ALU.mult, ALU.add))
            step(6, ve.tensor_tensor(tile_start[:, :], tile_end[:, :], n_tiles[:, :],
                                     ALU.subtract))
            step(7, ve.tensor_tensor(past[:, :, :], of_expert(tile_end[:, :]),
                                     of_tile(tile_c[one, :]), ALU.is_le))
            step(8, ve.tensor_reduce(tile_e_f[:, :], past[:, :, :], axis=AX.X, op=ALU.add))
            ve.tensor_scalar(tile_expert[:, :], tile_e_f[:, :], float(E - 1), None, ALU.min
                             ).then_inc(tiles_ready, 1)
            step(9, ve.tensor_tensor(row_at[:, :, :], of_tile(tile_c[one, :]),
                                     of_expert(tile_start[:, :]), ALU.subtract))
            step(10, ve.tensor_scalar(row_at[:, :, :], row_at[:, :, :], float(P), float(P),
                                      ALU.mult, ALU.add))
            step(11, ve.tensor_tensor(row_at[:, :, :], row_at[:, :, :], of_expert(counts[:, :]),
                                      ALU.min))
            step(12, ve.tensor_scalar(row_at[:, :, :], row_at[:, :, :], float(-P), 0.0, ALU.add,
                                      ALU.max))
            step(13, ve.tensor_tensor(row_at[:, :, :], row_at[:, :, :],
                                      of_expert(room_c[one, 0:E]), ALU.add))
            step(14, ve.tensor_tensor(began[:, :, :], of_expert(tile_start[:, :]),
                                      of_tile(tile_c[one, :]), ALU.is_le))
            step(15, ve.tensor_tensor(began[:, :, :], began[:, :, :], past[:, :, :],
                                      ALU.subtract))
            step(16, ve.tensor_tensor(row_at[:, :, :], row_at[:, :, :], began[:, :, :], ALU.mult))
            step(17, ve.tensor_reduce(tile_at[:, :], row_at[:, :, :], axis=AX.X, op=ALU.add))
            step(18, ve.tensor_scalar(tile_e_f[:, :], tile_e_f[:, :], float(E), float(E * ROOM),
                                      ALU.is_ge, ALU.mult))
            ve.tensor_tensor(tile_row[:, :], tile_e_f[:, :], tile_at[:, :], ALU.add
                             ).then_inc(tiles_ready, 1)

            def tile_in(j, s):
                dve.wait_ge(xs_T, j + 1)
                ve.tensor_copy(xsT[:, s, :, :].rearrange("p k t -> p (k t)"), psum[4][:, 0:D]
                               ).then_inc(xsT_ready, 1)

            def hidden(j, s):
                for n in range(2):
                    dve.wait_ge(hid_T, 2 * j + (n + 1))
                    if n == 0:
                        wait(dve, down_done, j - 1)
                    half = hidT[:, s, n * KF // 2:(n + 1) * KF // 2, :]
                    ve.tensor_copy(half.rearrange("p k t -> p (k t)"), psum[2 + n][:, :]
                                   ).then_inc(hidT_ready, 1)

            def tile_sum(j, s):
                dve.wait_ge(down_done, j + 1)
                dve.wait_ge(rest_in[s], 8 * (j - s) + 16)
                ve.tensor_tensor(z_sb[:, s, :], psum[5][:, 0:D], rest_sb[:, s, 0:D], ALU.add
                                 ).then_inc(sum_done, 1)
                dve.wait_ge(sum_done, j + 1)
                ve.bn_stats(stats[:, :], z_sb[:, s, :]).then_inc(last_stats, 1)
                dve.wait_ge(last_stats, j + 1)
                ve.memset(wait_cell[:, :], 0.0)
                ve.bn_aggr(mv[:, s, 0, :], stats[:, :]).then_inc(last_mv, 1)

            def tile_out(j, s):
                dve.wait_ge(last_rstd, j + 1)
                wait(dve, out_stored[s], 8 * (j - s))
                ve.tensor_scalar(o_sb[:, s, :], z_sb[:, s, :], mv[:, s, 0, 0:1], rstd[:, s, 0:1],
                                 ALU.subtract, ALU.mult).then_inc(out_ready, 1)

            def expert_body(j, s, first=False, ends=False):
                hidden(j - 1, 1 - s)
                if not ends:
                    tile_in(j + 1, 1 - s)
                if not first:
                    tile_out(j - 2, s)
                tile_sum(j - 1, 1 - s)

            tile_in(0, 0)
            tile_in(1, 1)
            expert_body(1, 1, first=True)
            for j in range(2, 5):
                expert_body(j, j % 2)
            with dve.Fori(2, TILES // 2 - 1) as pair:
                expert_body(2 * pair + 1, 1)
                expert_body(2 * pair + 2, 0)
            expert_body(TILES - 2, 1)
            expert_body(TILES - 1, 0, ends=True)
            hidden(TILES - 1, 0)
            tile_out(TILES - 2, 1)
            tile_sum(TILES - 1, 0)
            tile_out(TILES - 1, 0)

        @block.gpsimd
        def _(pool):
            for started, by in ((layer_b.sum_ready, 2), (rows_free, 1),
                                *((stored, 16) for stored in (*layer_a.x_out, *layer_a.h_out)),
                                *((d, 1) for ring in (layer_a.p_ring, layer_a.o_ring,
                                                      layer_b.mx_ring) for d in ring.drained)):
                pool.memset(pool_cell[:, :], 0.0).then_inc(started, by)
                pool.wait_ge(started, by)
            pool.memset(row_sb[:, 0, 0:2 * D], 0.0).then_inc(pad_set, 1)
            pool.memset(v_aug[:, :, :, :, HD:VW], 0.0).then_inc(pool_set, 1)
            pool.wait_ge(pool_set, 1)
            pool.memset(v_aug[:, :, :, :, HD:HD + 1], 1.0).then_inc(pool_set, 1)
            pool.wait_ge(pool_set, 2)
            pool.memset(k_stack[STACK:STACK + NEG, :, :, :], 1.0).then_inc(pool_set, 1)
            pool.wait_ge(pool_set, 3)
            pool.wait_ge(consts_in, 16 * N_FIRST)

            def task(L, name, b, s):
                kind, t = name[:2], name[-1]
                p = L.p_ring
                if name in ("qB", "kB") and not L.second:
                    qk = "qk".index(name[0])
                    all_empty(pool, p, b, PARTS_OF[qk])
                    wait(pool, L.parts_ready, 2 * b + (qk - 1))
                    pool.tensor_tensor(rest[:, qk, 0, :], trig[:, 0, :], trig[:, 2, :],
                                       ALU.subtract)
                    pool.tensor_tensor(rest[:, qk, 1, :], trig[:, 1, :], trig[:, 3, :], ALU.add
                                       ).then_inc(L.rot_done, 1)
                elif kind[0] in "ml":
                    qk = "qk".index(name[1])
                    pool.wait_ge(L.mid_done, 2 * b + (qk + 1))
                    pool.tensor_tensor(parts[:, qk, 2, :, :], rest[:, qk, :, :],
                                       parts[:, qk, 1, :, :], ALU.subtract
                                       ).then_inc(L.parts_ready, 1)
                elif name == "TO0" and not L.second:
                    pool.wait_ge(L.res_in, 16 * b + 16)
                    pool.tensor_tensor(res_sb[:, :, :], res_sb[:, :, :],
                                       rows_sb[:, 0:1, :].to_broadcast([P, TT, D]), ALU.add
                                       ).then_inc(L.res_ready, 1)
                elif kind == "WO" and L.second:
                    t = int(t)
                    pool.wait_ge(*L.o_ring.empty(b, name))
                    pool.tensor_tensor(row_sb[:, t, D:2 * D], res_sb[:, t, :], xo[:, t % 2, :],
                                       ALU.add).then_inc(L.sum_ready, 1)
                elif name == "RT":
                    pool.wait_ge(L.h_ready, TT * b + TT)
                    pool.wait_ge(L.sum_ready, TT * (b - L.first) + (TT + 2))
                    pool.wait_ge(slots_ready, b - L.first + 1)
                    pool.tensor_tensor(pool_cell[:, 0:1], pool_cell[:, 0:1], pool_cell[:, 0:1],
                                       ALU.add)
                    for t in range(TT):
                        pool.indirect_dma_start(
                            rows_dram, bass.IndirectOffsetOnAxis(slot_u[:, t:t + 1], 0),
                            row_sb[:, t, :], None).then_inc(dispatched, 16)
                    pool.wait_ge(dispatched, 16 * TT * (b - L.first) + 16 * TT)
                    pool.wait_ge(rows_free, b - L.first + 1)
                    pool.tensor_tensor(pool_cell[:, 1:2], pool_cell[:, 1:2], pool_cell[:, 1:2],
                                       ALU.add).then_inc(rows_free, 1)
                elif kind == "N2":
                    t = int(t)
                    r = 3 if L.second else 1
                    pool.wait_ge(L.hn_ready, TT * b + (t + 1))
                    pool.tensor_tensor(hn[:, t, :], hn[:, t, :], rows_sb[:, r, :], ALU.mult
                                       ).then_inc(L.hw_step, 1)
                    pool.wait_ge(L.hw_step, TT * b + (t + 1))
                    pool.tensor_tensor(hn[:, t, :], hn[:, t, :], rows_sb[:, r + 1, :],
                                       ALU.add).then_inc(L.h_ready, 1)

            def body(par, projected, attended, finished):
                if attended and not finished:
                    pool.wait_ge(later_in, 16 * N_LATER)
                    pool.wait_ge(padded, 16 * (E + 1))
                for slot in SLOTS:
                    outer_tasks(slot, par, projected, finished, task)

            pipeline(pool, body)

            for j in range(TILES):
                s = j % 2
                if j:
                    pool.wait_ge(out_stored[1 - s], 16 * ((j + 1) // 2))
                pool.wait_ge(out_ready, j + 1)
                pool.indirect_dma_start(
                    out_rows, bass.IndirectOffsetOnAxis(rest_sb[:, s, D:D + 1].bitcast(U32), 0),
                    o_sb[:, s, :], None).then_inc(out_stored[s], 16)

        @block.sync
        def _(sp):
            first = (
                (ident_sb[:, :], ident),
                (wqkv_sb[:, 0, 0, :], w_qkv1[0:P, :]), (wqkv_sb[:, 0, 1, :], w_qkv1[P:D, :]),
                (cos_sb[:, :], cos_t), (sin_sb[:, :], sin_t), (head_sum_sb[:, :], head_sum),
                (route_c[:, :], route_consts))
            later = (
                (wo_sb[:, 0, :, :], w_o1.rearrange("(k p) n -> p k n", p=P)),
                (rows_sb[:, 0, :], b_o.partition_broadcast(P)),
                (rows_sb[:, 1, :], ln1_w.partition_broadcast(P)),
                (rows_sb[:, 2, :], ln1_b.partition_broadcast(P)),
                (rows_sb[:, 3, :], ln2_w.partition_broadcast(P)),
                (rows_sb[:, 4, :], ln2_b.partition_broadcast(P)),
                (wqkv_sb[:, 1, 0, :], w_qkv2[0:P, :]), (wqkv_sb[:, 1, 1, :], w_qkv2[P:D, :]),
                (wo_sb[:, 1, :, :], w_o2.rearrange("(k p) n -> p k n", p=P)),
                (gate_w_sb[:, 0, :], gate_w[0:P, :]), (gate_w_sb[:, 1, :], gate_w[P:D, :]),
                (gate_b_sb[:, :], gate_b.partition_broadcast(P)))
            assert (len(first), len(later)) == (N_FIRST, N_LATER)
            for dst, src in first:
                sp.dma_start(dst, src).then_inc(consts_in, 16)
            for dst, src in later:
                sp.dma_start(dst, src).then_inc(later_in, 16)
            sp.wait_ge(pad_set, 2)
            for e in range(E + 1):
                sp.dma_start(rows_dram[e * ROOM:e * ROOM + P, :], row_sb[:, 0, :]
                             ).then_inc(padded, 16)

            def task(L, name, b, s):
                kind, t = name[:2], name[-1]
                if kind[0] in "ml":
                    qk = "qk".index(name[1])
                    stack, slots = ((q_stack, Q_SLOTS), (k_stack, K_SLOTS))[qk]
                    sp.wait_ge(L.parts_ready, 2 * b + (qk + 1))
                    if not isinstance(b, int) or b >= 2:
                        sp.wait_ge(L.scores, CHUNKS * b - CHUNKS)
                    for slot, part in enumerate(slots):
                        for half in range(2):
                            at = HD * slot + HALF * half
                            sp.dma_start(stack[at:at + HALF, s, :, :], parts[:, qk, part, half, :]
                                         ).then_inc(L.stack_in[qk], 16)
                elif kind == "N1":
                    t = int(t)
                    sp.wait_ge(L.mv_ready, norms(L, b) + (2 * t + 2))
                    sp.dma_start(tile_of(x1_dram, b, t), xo[:, t % 2, :]
                                 ).then_inc(L.x_out[t % 2], 16)
                elif kind == "N2" and not L.second:
                    t = int(t)
                    sp.wait_ge(L.h_ready, TT * b + (t + 1))
                    sp.dma_start(tile_of(h1_dram, b, t), hn[:, t, :]
                                 ).then_inc(L.h_out[t % 2], 16)

            def neg_rows(L, b, g, s):
                sp.wait_ge(*L.mx_ring.empty(b, ("NG", g)))
                sp.dma_start(q_stack[STACK:STACK + NEG, s, HEADS_AT_ONCE * g:HEADS_AT_ONCE * (g + 1), :],
                             neg_T[:, :]).then_inc(L.neg_in, 16)

            def body(par, projected, attended, finished):
                for q in range(QUADS):
                    for L, b, g, s in neg_group(q, par, projected, attended):
                        neg_rows(L, b, g, s)
                    for j in (0, 2):
                        outer_tasks((q, j), par, projected, finished, task)

            pipeline(sp, body)
            sp.wait_ge(tiles_ready, 2)
            sp.wait_ge(dispatched, 16 * TT * BATCH)

            def rows_of(j):
                row = sp.value_load(tile_row[0:1, bass.ds(j, 1)], min_val=0, max_val=E * ROOM)
                return rows_dram[bass.ds(row, P), :]

            def load_rest(j, s):
                rows = rows_of(j)
                wait(sp, out_stored[s], 8 * (j - s))
                sp.dma_start(rest_sb[:, s, :], rows[:, D:ROW]).then_inc(rest_in[s], 16)

            def load_tile(j, s):
                rows = rows_of(j)
                wait(sp, xs_T, j - 1)
                sp.dma_start(xs_sb[:, s, :], rows[:, 0:D]).then_inc(xs_in[s], 16)

            load_tile(0, 0)
            load_rest(0, 0)
            load_tile(1, 1)
            load_rest(1, 1)
            load_tile(2, 0)
            with sp.Fori(1, TILES // 2) as pair:
                load_tile(2 * pair + 1, 1)
                load_rest(2 * pair, 0)
                load_tile(2 * pair + 2, 0)
                load_rest(2 * pair + 1, 1)
            load_rest(TILES - 1, 0)

            for s in range(2):
                sp.wait_ge(out_stored[s], 16 * ((TILES + 1 - s) // 2))
            for b in range(BATCH):
                sp.dma_start(out[b], out_rows[b * T:(b + 1) * T, :]).then_inc(out_done, 16)
            sp.wait_ge(out_done, 16 * BATCH)


def lay_out(**inputs):
    a = {k.removeprefix("L0_"): np.asarray(v) for k, v in inputs.items()}
    def columns(w):
        qk = w[:, :2 * D].reshape(D, 2, H, 2, HALF).transpose(0, 1, 3, 4, 2).reshape(D, 2 * D)
        return np.ascontiguousarray(np.concatenate([qk, w[:, 2 * D:]], axis=1))
    inv_freq = (1.0 / np.float32(10000.0) ** (np.arange(HALF, dtype=np.float32) / np.float32(HALF)))
    angles = (np.arange(T, dtype=np.float32)[None, :] * inv_freq.astype(np.float32)[:, None])
    table = lambda f: np.repeat(f(angles).astype(np.float32), H, axis=0)
    of_head = np.arange(P) % H
    return {
        "x": a["attn_x"], "w_qkv1": columns(a["attn_Wqkv"]), "w_o1": a["attn_Wo"],
        "b_o": a["attn_bo"], "ln1_w": a["ffn_ln1_w"], "ln1_b": a["ffn_ln1_b"],
        "w_qkv2": columns(a["ffn_w_qkv"]), "w_o2": a["ffn_w_proj"], "ln2_w": a["ffn_ln2_w"],
        "ln2_b": a["ffn_ln2_b"], "gate_w": a["ffn_gate_w"], "gate_b": a["ffn_gate_b"],
        "w1": a["ffn_w1"], "w2": a["ffn_w2"], "cos_t": table(np.cos), "sin_t": table(np.sin),
        "head_sum": (of_head[:, None] == of_head[None, :]).astype(np.float32),
        "ident": np.eye(P, dtype=np.float32),
        "route_consts": np.concatenate([
            np.triu(np.ones((P, P)), 1), np.tile(E - np.arange(E), (P, 1)),
            np.tile(ROOM * np.arange(E + 1), (P, 1)), np.tile(np.arange(TILES), (P, 1)),
            np.arange(P)[:, None] + P * np.arange(TT)[None, :],
            BATCH * T + np.arange(P)[:, None]], axis=1).astype(np.float32),
    }


def kernel(**inputs):
    import concourse.bacc as bacc
    from concourse.bass_utils import run_bass_kernel_spmd

    nc = bacc.Bacc("TRN2", target_bir_lowering=False, num_devices=1)
    arrays, args = {}, {}
    for name, a in lay_out(**inputs).items():
        a = np.ascontiguousarray(a)
        arrays[f"in_{name}_dram"] = a
        args[name] = nc.dram_tensor(f"in_{name}_dram", a.shape, mybir.dt.from_np(a.dtype),
                                    kind="ExternalInput").ap()
    args["out"] = nc.dram_tensor("out_0_dram", (BATCH, T, D), FP32, kind="ExternalOutput").ap()
    program(nc, **args)
    return run_bass_kernel_spmd(nc, [arrays], core_ids=[0]).results[0]["out_0_dram"]
```
